# Optimizing a Trainium2 kernel written in Bass

```python
import numpy as np
import jax
import jax.numpy as jnp

def _softmax(x, axis=-1):
    return jax.nn.softmax(x, axis=axis)

def _gelu(x):
    return jax.nn.gelu(x, approximate=True)

def _silu(x):
    return jax.nn.silu(x)

def _sigmoid(x):
    return jax.nn.sigmoid(x)

def _layernorm(x, axis=-1, eps=1e-05):
    m = jnp.mean(x, axis=axis, keepdims=True)
    v = jnp.var(x, axis=axis, keepdims=True)
    return (x - m) / jnp.sqrt(v + eps)

def _scatter_add(tgt, idx, src, axis=0):
    return tgt.at[idx].add(src)

def _segment_sum(src, seg, n):
    return jax.ops.segment_sum(src, seg, n)
kernel_name = 'mk_audio_tower_d1_tok_aud1d512_r4_f5ffe8'

def setup_inputs(seed: int=0):
    np.random.seed(seed)
    _w = jnp.asarray

    def _rec_inputs():
        import jax
        import jax.numpy as jnp
        _rk = jax.random.key(seed)
        x = 0.000265968 + 1.00011 * jax.random.normal(jax.random.fold_in(_rk, 1), (64, 4000), jnp.float32)
        return x
    x = _rec_inputs()

    def _L0_tok_setup():
        import jax, jax.numpy as jnp
        import numpy as np
        FRAME_LENGTH = 256

        def _mdct_matrix(L2):
            L = L2 // 2
            n = np.arange(L2, dtype=np.float64) + 0.5
            k = np.pi / L * n[:L]
            n2 = n + L / 2
            z = np.sqrt(4.0 / L)
            W = z * np.cos(np.outer(n2, k))
            return jnp.asarray(W, dtype=jnp.float32)

        def _sine_window(L2):
            n = np.arange(L2, dtype=np.float64)
            return jnp.asarray(np.sin(np.pi * (n + 0.5) / L2), dtype=jnp.float32)
        key = jax.random.key(seed)
        x = jax.random.normal(key, (16, 262144), dtype=jnp.float32)
        return {'x': x}
    _L0_tok_all = _L0_tok_setup()
    _L0_tok_in = {k: v for k, v in _L0_tok_all.items() if k in ()}
    del _L0_tok_all

    def _L0_attn_setup():
        import jax, jax.numpy as jnp
        import numpy as np
        from jax import lax
        D_MODEL, D_STATE, D_CONV, EXPAND, HEADDIM = (128, 64, 4, 2, 64)
        D_INNER = EXPAND * D_MODEL
        NHEADS = D_INNER // HEADDIM
        CONV_DIM = D_INNER + 2 * D_STATE
        D_IN_PROJ = 2 * D_INNER + 2 * D_STATE + NHEADS
        EPS = 1e-05

        def _silu(x):
            return x * jax.nn.sigmoid(x)
        key = jax.random.key(seed)
        ks = jax.random.split(key, 8)
        u = jax.random.normal(ks[0], (2, 512, D_MODEL), dtype=jnp.float32)
        W_in = jax.random.normal(ks[1], (D_IN_PROJ, D_MODEL), dtype=jnp.float32) * D_MODEL ** (-0.5)
        conv_w = jax.random.normal(ks[2], (CONV_DIM, 1, D_CONV), dtype=jnp.float32) * D_CONV ** (-0.5)
        conv_b = jax.random.normal(ks[3], (CONV_DIM,), dtype=jnp.float32) * 0.02
        dt_bias = jax.random.uniform(ks[4], (NHEADS,), dtype=jnp.float32, minval=-1.0, maxval=1.0)
        A_log = jnp.log(jnp.linspace(1.0, NHEADS, NHEADS, dtype=jnp.float32))
        D = jnp.ones((NHEADS,), dtype=jnp.float32)
        norm_w = jnp.ones((D_INNER,), dtype=jnp.float32)
        W_out = jax.random.normal(ks[5], (D_MODEL, D_INNER), dtype=jnp.float32) * D_INNER ** (-0.5)
        return {'u': u, 'W_in': W_in, 'conv_w': conv_w, 'conv_b': conv_b, 'dt_bias': dt_bias, 'A_log': A_log, 'D': D, 'norm_w': norm_w, 'W_out': W_out}
    _L0_attn_all = _L0_attn_setup()
    _L0_attn_in = {k: v for k, v in _L0_attn_all.items() if k in ('W_in', 'conv_w', 'conv_b', 'dt_bias', 'A_log', 'D', 'norm_w', 'W_out')}
    del _L0_attn_all

    def _L0_ffn_setup():
        import jax, jax.numpy as jnp
        import numpy as np
        D, H, E, B, S = (128, 512, 16, 8, 2048)
        MAX_GROUP_SIZE = 1024
        MIN_CAPACITY = 8
        CAPACITY_FACTOR = 1.0

        def _group_dims(num_tokens, num_experts):
            num_groups = -(-num_tokens // MAX_GROUP_SIZE)
            while num_tokens % num_groups != 0 or num_groups % num_experts != 0:
                num_groups += 1
            return (num_tokens // num_groups, num_groups)
        key = jax.random.key(seed)
        ks = jax.random.split(key, 6)
        s = 0.02
        return {'x': jax.random.normal(ks[0], (B, S, D), jnp.float32), 'gate_w': jax.random.normal(ks[1], (D, E), jnp.float32) * s, 'w1': jax.random.normal(ks[2], (E, D, H), jnp.float32) * s, 'b1': jnp.zeros((E, H), jnp.float32), 'w2': jax.random.normal(ks[3], (E, H, D), jnp.float32) * s, 'b2': jnp.zeros((E, D), jnp.float32), 'sw1': jax.random.normal(ks[4], (D, H), jnp.float32) * s, 'sb1': jnp.zeros((H,), jnp.float32), 'sw2': jax.random.normal(ks[5], (H, D), jnp.float32) * s, 'sb2': jnp.zeros((D,), jnp.float32)}
    _L0_ffn_all = _L0_ffn_setup()
    _L0_ffn_in = {k: v for k, v in _L0_ffn_all.items() if k in ('gate_w', 'w1', 'b1', 'w2', 'b2', 'sw1', 'sb1', 'sw2', 'sb2')}
    del _L0_ffn_all
    return {'x': x, 'L0_attn_W_in': _L0_attn_in['W_in'], 'L0_attn_conv_w': _L0_attn_in['conv_w'], 'L0_attn_conv_b': _L0_attn_in['conv_b'], 'L0_attn_dt_bias': _L0_attn_in['dt_bias'], 'L0_attn_A_log': _L0_attn_in['A_log'], 'L0_attn_D': _L0_attn_in['D'], 'L0_attn_norm_w': _L0_attn_in['norm_w'], 'L0_attn_W_out': _L0_attn_in['W_out'], 'L0_ffn_gate_w': _L0_ffn_in['gate_w'], 'L0_ffn_w1': _L0_ffn_in['w1'], 'L0_ffn_b1': _L0_ffn_in['b1'], 'L0_ffn_w2': _L0_ffn_in['w2'], 'L0_ffn_b2': _L0_ffn_in['b2'], 'L0_ffn_sw1': _L0_ffn_in['sw1'], 'L0_ffn_sb1': _L0_ffn_in['sb1'], 'L0_ffn_sw2': _L0_ffn_in['sw2'], 'L0_ffn_sb2': _L0_ffn_in['sb2']}

def reference(x, L0_attn_W_in, L0_attn_conv_w, L0_attn_conv_b, L0_attn_dt_bias, L0_attn_A_log, L0_attn_D, L0_attn_norm_w, L0_attn_W_out, L0_ffn_gate_w, L0_ffn_w1, L0_ffn_b1, L0_ffn_w2, L0_ffn_b2, L0_ffn_sw1, L0_ffn_sb1, L0_ffn_sw2, L0_ffn_sb2):
    import jax
    import jax.numpy as jnp

    def _L0_tok_ref(x):
        import jax, jax.numpy as jnp
        import numpy as np
        FRAME_LENGTH = 256

        def _mdct_matrix(L2):
            L = L2 // 2
            n = np.arange(L2, dtype=np.float64) + 0.5
            k = np.pi / L * n[:L]
            n2 = n + L / 2
            z = np.sqrt(4.0 / L)
            W = z * np.cos(np.outer(n2, k))
            return jnp.asarray(W, dtype=jnp.float32)

        def _sine_window(L2):
            n = np.arange(L2, dtype=np.float64)
            return jnp.asarray(np.sin(np.pi * (n + 0.5) / L2), dtype=jnp.float32)
        L2 = FRAME_LENGTH
        hop = L2 // 2
        x = jnp.pad(x, ((0, 0), (0, hop)))
        x = jnp.pad(x, ((0, 0), (L2 // 2, (L2 - 1) // 2)))
        T = x.shape[-1]
        n_frames = (T - L2) // hop + 1
        idx = jnp.arange(n_frames)[:, None] * hop + jnp.arange(L2)[None, :]
        frames = x[:, idx]
        w = _sine_window(L2)
        W = _mdct_matrix(L2)
        return jnp.einsum('bfl,l,lk->bfk', frames, w, W)

    def _L0_attn_ref(u, W_in, conv_w, conv_b, dt_bias, A_log, D, norm_w, W_out):
        import jax, jax.numpy as jnp
        import numpy as np
        from jax import lax
        D_MODEL, D_STATE, D_CONV, EXPAND, HEADDIM = (128, 64, 4, 2, 64)
        D_INNER = EXPAND * D_MODEL
        NHEADS = D_INNER // HEADDIM
        CONV_DIM = D_INNER + 2 * D_STATE
        D_IN_PROJ = 2 * D_INNER + 2 * D_STATE + NHEADS
        EPS = 1e-05

        def _silu(x):
            return x * jax.nn.sigmoid(x)
        b, s, _ = u.shape
        zxbcdt = u @ W_in.T
        z = zxbcdt[..., :D_INNER]
        xBC = zxbcdt[..., D_INNER:D_INNER + CONV_DIM]
        dt = zxbcdt[..., D_INNER + CONV_DIM:]
        dt = jax.nn.softplus(dt + dt_bias)
        xp = jnp.pad(xBC, ((0, 0), (D_CONV - 1, 0), (0, 0)))
        w = conv_w[:, 0, :]
        conv = conv_b
        for k in range(D_CONV):
            conv = conv + xp[:, k:k + s, :] * w[:, k]
        xBC = _silu(conv)
        x = xBC[..., :D_INNER].reshape(b, s, NHEADS, HEADDIM)
        B = xBC[..., D_INNER:D_INNER + D_STATE]
        C = xBC[..., D_INNER + D_STATE:]
        A = -jnp.exp(A_log)

        def step(h, inp):
            dt_t, B_t, C_t, x_t = inp
            dA = jnp.exp(A * dt_t)
            h = h * dA[..., None, None] + jnp.einsum('bh,bn,bhp->bhpn', dt_t, B_t, x_t)
            y_t = jnp.einsum('bhpn,bn->bhp', h, C_t)
            return (h, y_t)
        h0 = jnp.zeros((b, NHEADS, HEADDIM, D_STATE), dtype=u.dtype)
        xs = (dt.transpose(1, 0, 2), B.transpose(1, 0, 2), C.transpose(1, 0, 2), x.transpose(1, 0, 2, 3))
        _, ys = lax.scan(step, h0, xs)
        y = ys.transpose(1, 0, 2, 3) + x * D[:, None]
        y = y.reshape(b, s, D_INNER)
        y = y * _silu(z)
        y = y * lax.rsqrt(jnp.mean(y * y, axis=-1, keepdims=True) + EPS) * norm_w
        return y @ W_out.T

    def _L0_ffn_ref(x, gate_w, w1, b1, w2, b2, sw1, sb1, sw2, sb2):
        import jax, jax.numpy as jnp
        import numpy as np
        D, H, E, B, S = (128, 512, 16, 8, 2048)
        MAX_GROUP_SIZE = 1024
        MIN_CAPACITY = 8
        CAPACITY_FACTOR = 1.0

        def _group_dims(num_tokens, num_experts):
            num_groups = -(-num_tokens // MAX_GROUP_SIZE)
            while num_tokens % num_groups != 0 or num_groups % num_experts != 0:
                num_groups += 1
            return (num_tokens // num_groups, num_groups)
        Bn, Sn, Dn = x.shape
        En = gate_w.shape[1]
        T = Bn * Sn
        group_size, num_groups = _group_dims(T, En)
        cap = max(int(round(CAPACITY_FACTOR * group_size * num_groups / En)), MIN_CAPACITY)
        xg = x.reshape(num_groups, group_size, Dn)
        logits = jnp.einsum('gsd,de->gse', xg, gate_w)
        probs = jax.nn.softmax(logits, axis=-1)
        flat_probs = probs.transpose(2, 0, 1).reshape(En, T)
        scores, tok_idx = jax.lax.top_k(flat_probs, cap)
        xf = x.reshape(T, Dn)
        toks = xf[tok_idx]
        h = jax.nn.gelu(jnp.einsum('ecd,edh->ech', toks, w1) + b1[:, None, :])
        y = jnp.einsum('ech,ehd->ecd', h, w2) + b2[:, None, :]
        y = y * scores[..., None]
        routed = jnp.zeros_like(xf).at[tok_idx.reshape(-1)].add(y.reshape(-1, Dn))
        shared = jax.nn.gelu(xf @ sw1 + sb1) @ sw2 + sb2
        out = (routed + shared).reshape(Bn, Sn, Dn)
        return out
    h = _L0_tok_ref(x)
    h = h + _L0_attn_ref(_layernorm(h, axis=-1), L0_attn_W_in, L0_attn_conv_w, L0_attn_conv_b, L0_attn_dt_bias, L0_attn_A_log, L0_attn_D, L0_attn_norm_w, L0_attn_W_out)
    h = h + _L0_ffn_ref(_layernorm(h, axis=-1), L0_ffn_gate_w, L0_ffn_w1, L0_ffn_b1, L0_ffn_w2, L0_ffn_b2, L0_ffn_sw1, L0_ffn_sb1, L0_ffn_sw2, L0_ffn_sb2)
    return h

_drawn_inputs = setup_inputs


def setup_inputs(seed=0):
    import zlib

    import numpy as np

    out = dict(_drawn_inputs(seed))
    spreads = {'L0_attn_D': (1.0, 0.2),
     'L0_attn_norm_w': (1.0, 0.2),
     'L0_ffn_b1': (0.0, 0.8),
     'L0_ffn_b2': (0.0, 0.8),
     'L0_ffn_sb1': (0.0, 0.585),
     'L0_ffn_sb2': (0.0, 0.1)}
    factors = {'L0_attn_conv_b': 2.983, 'L0_ffn_gate_w': 8.0, 'L0_ffn_w1': 8.0, 'L0_ffn_w2': 8.0}
    for name, (base, spread) in spreads.items():
        noise = np.random.default_rng([zlib.crc32(name.encode()), seed]).standard_normal(out[name].shape)
        drawn = base * np.exp(spread * noise) if base else spread * noise
        out[name] = jnp.asarray(drawn.astype(out[name].dtype))
    for name, factor in factors.items():
        out[name] = (out[name] * factor).astype(out[name].dtype)
    return out
```

```python
from contextlib import ExitStack

import numpy as np

import concourse.bass as bass
from concourse import mybir

F32 = mybir.dt.float32
F16 = mybir.dt.float16
BF16 = mybir.dt.bfloat16
I32 = mybir.dt.int32
U32 = mybir.dt.uint32
ALU = mybir.AluOpType
ACT = mybir.ActivationFunctionType
AX = mybir.AxisListType

B, S = 64, 33
HOP = 128
NBLK = S + 1
TOK = 3 * S
T = -(-B // 3)
PAIRS = T // 2
BANKS = -(-T // 4)
PAIR = 2 * TOK
NTOK = B * S
D, DIN, NST, NH, HD = 128, 256, 64, 4, 64
E, HID, HC = 16, 512, 4
CAP = NTOK // E
EPS = 1e-5
MAIN = 128
LEFT = CAP - MAIN
NL = E * LEFT
SLOTB = 16
SLOTA = -(-CAP // SLOTB)
ROW = D + E
GROUPS = 3
BIG = 4096.0
VALUE0 = T * TOK // 2
XCUT = ((0, 2), (2, 6), (6, 12), (12, 17), (17, 22))
BITS = 30


def program(nc, a):
    ctx = ExitStack()
    with ctx:
        def sb(name, shape, dt=F32):
            return ctx.enter_context(nc.sbuf_tensor(name, shape, dt))

        def sem(name):
            return ctx.enter_context(nc.semaphore(name))

        xT = sb("xT", [128, 2, T * TOK])
        wtok = sb("wtok", [128, 2 * D])
        w_in = sb("w_in", [128, 644])
        w_out_raw = sb("w_out_raw", [128, 2, D])
        w_out = sb("w_out", [128, 2, D])
        cols = sb("cols", [128, 21])
        norm_w, conv_w, conv_b, d_col = cols[:, 0:2], cols[:, 2:14], cols[:, 14:17], cols[:, 17:19]
        rows = sb("rows", [TOK, 8])
        dt_bias, a_log = rows[:, 0:NH], rows[:, NH:2 * NH]
        tri = sb("tri", [TOK, TOK])
        mask32 = sb("mask32", [TOK, TOK])
        mask = sb("mask", [TOK, TOK], BF16)
        ident = sb("ident", [128, 128])
        ident16 = sb("ident16", [128, 128], BF16)
        ones = sb("ones", [128, TOK])
        gate_w = sb("gate_w", [128, E])
        sw1 = sb("sw1", [128, HID])
        sw2 = sb("sw2", [128, HC, D])
        sb2 = sb("sb2", [TOK, D])
        biases = sb("biases", [128, HC + E * HC + E])
        sb1, b1, b2 = biases[:, 0:HC], biases[:, HC:HC + E * HC], biases[:, HC + E * HC:]
        w1 = sb("w1", [128, E, HID])
        w2 = sb("w2", [128, E, HC * D])
        consts = sb("consts", [128, 256 + 32 + 16 + T + 8 + NL + E + 4])
        at = 0

        def const(n):
            nonlocal at
            at += n
            return consts[:, at - n:at]
        same_e = const(128)
        below = const(128)
        bitf = const(32)
        iota16 = const(16)
        value = const(T)
        diag = const(8)
        earlier = const(NL)
        own_e = const(E)
        valid = const(1)
        invalid = const(1)
        dummy = const(1)
        big = const(1)

        h = sb("h", [TOK, T, D])
        u = sb("u", [TOK, T, D])
        uT = sb("uT", [128, T * TOK])
        o = sb("o", [TOK, T, D + 1])
        table = sb("table", [TOK, T, ROW])
        stats = sb("stats", [TOK, T, 6])
        small = sb("small", [TOK, 8, T])
        mean, rstd, s_sum, s_dif, s_sq, s_var = (small[:, n, :] for n in range(6))
        half_neg = sb("half_neg", [TOK, T])
        dtw = sb("dtw", [TOK, 8, T * NH])
        dt_x, dt_abs, dt_exp, dt_log, dt, decay, neg_cum, dt4 = (dtw[:, n, :] for n in range(8))
        exp_a = sb("exp_a", [TOK, NH])
        decay_p = sb("decay_p", [TOK, 2, NH])
        work = sb("work", [128, 7300])
        used = [0]

        def carve(p, *shape):
            n = int(np.prod(shape))
            used[0] += n
            assert used[0] <= 7300
            ap = work[0:p, used[0] - n:used[0]]
            names = "abcd"[:len(shape)]
            if len(shape) == 1:
                return ap
            return ap.rearrange(f"p ({' '.join(names)}) -> p {' '.join(names)}", **dict(zip(names[1:], shape[1:])))
        conv = carve(128, 3, PAIR)
        raw = carve(128, 3, PAIR)
        tanh3 = carve(128, 2, PAIR)
        tanhz = carve(128, 2, PAIR)
        xs = carve(128, 2, PAIR)
        bs = carve(NST, PAIR)
        cs = carve(NST, PAIR)
        tanhb = carve(128, PAIR)
        zs = carve(128, 2, PAIR)
        xrow = carve(TOK, 2, DIN)
        lmask = carve(TOK, 2, NH, TOK)
        gm = carve(TOK, 2, NH, TOK)
        yd = carve(128, 2, PAIR)
        yg = carve(128, 2, PAIR)
        ysq = carve(128, 2, PAIR)
        used[0] = 0
        got = carve(128, E + 1, ROW)
        ys = carve(128, 4, D)
        yl = carve(NL, 2, D)
        dg = carve(8 * SLOTA, 2, 8, SLOTB)
        hid = carve(128, 2, HC, PAIR)
        stage = carve(TOK, 2, 2, D)
        xe = xT[:, 0, 0:E * CAP].rearrange("p (e c) -> p e c", e=E)
        ye = uT[:, 0:E * CAP].rearrange("p (e c) -> p e c", e=E)
        mx = sb("mx", [TOK, T])
        den = sb("den", [TOK, T])
        rden = sb("rden", [TOK, T])
        ex = sb("ex", [TOK, T, E])
        prob = sb("prob", [TOK, 8 * GROUPS, E])
        pse = sb("pse", [128, GROUPS, TOK])
        hits = sb("hits", [128, GROUPS, TOK])
        cnt = sb("cnt", [128, 1])
        bit_i = sb("bit_i", [128, 32], I32)
        cur = sb("cur", [128, 1], I32)
        cand = sb("cand", [128, 1], I32)
        step_i = sb("step_i", [128, 1], I32)
        m6 = sb("m6", [128, 2, GROUPS, TOK])
        ge = sb("ge", [128, GROUPS, TOK])
        rank = sb("rank", [128, 2, GROUPS, TOK])
        tot = sb("tot", [128, 6])
        pre = sb("pre", [128, 6])
        off = sb("off", [128, 6])
        pos = sb("pos", [128, GROUPS, TOK])
        pos_i = sb("pos_i", [TOK, T * E], I32)
        pa_i = sb("pa_i", [TOK, T * E], I32)
        pb_i = sb("pb_i", [TOK, T * E], I32)
        pa_f = sb("pa_f", [TOK, T * E])
        pb_f = sb("pb_f", [TOK, T * E])
        hotV = o[:, :, :].rearrange("p t c -> p (t c)")[:, 0:T * E * SLOTA // 2].bitcast(F16)\
            .rearrange("p (t e n) -> p t e n", e=E, n=SLOTA)
        hotA = xT[0:TOK, 1, 0:T * E * SLOTA // 2].bitcast(F16).rearrange("p (t e n) -> p t e n", e=E, n=SLOTA)
        hotB = u[:, :, :].rearrange("p t c -> p (t c)").bitcast(F16).rearrange("p (t e n) -> p t e n", e=E, n=SLOTB)
        dsum = sb("dsum", [8 * SLOTA, 2, SLOTB])
        lst = sb("lst", [8 * SLOTA, 2, SLOTB], U32)
        idx = sb("idx", [128, E], U32)
        idx_l = sb("idx_l", [NL, 1], U32)
        idx_lf = sb("idx_lf", [NL, 1])
        idx_row = sb("idx_row", [NL, NL], U32)
        idx_rowf = sb("idx_rowf", [NL, NL])
        eqm = sb("eqm", [NL, NL])
        eqe = sb("eqe", [NL, NL])
        dup = sb("dup", [NL, 4])
        idx_s = sb("idx_s", [NL, 1], U32)
        sc_l = sb("sc_l", [NL, E + 1])

        yel = sb("yel", [128, NL])
        ps = ctx.enter_context(nc.psum_tensor("ps", [128, 8, 512], F32))
        psf = ps[:, :, :].rearrange("p b n -> p (b n)")

        x_ld = {c: sem(f"x_ld{c}") for c, _ in XCUT}
        ld = {n: sem("ld_" + n) for n in (
            "wtok", "w_in", "cols", "rows", "tri", "mask", "ident", "w_out", "gate", "sw1", "sw2",
            "sb2", "biases", "w1", "w2", "consts")}
        h_mm, h_sb, st_a = sem("h_mm"), sem("h_sb"), sem("st_a")
        var_ok, pow_ok, u_ok, uT_mm, uT_sb = sem("var_ok"), sem("pow_ok"), sem("u_ok"), sem("uT_mm"), sem("uT_sb")
        dt_mm, dtx_ok, log_ok, dec_ok, cum_mm, cum_ok = (sem(n) for n in (
            "dt_mm", "dtx_ok", "log_ok", "dec_ok", "cum_mm", "cum_ok"))
        v_step, a_step, p_step = sem("v_step"), sem("a_step"), sem("p_step")
        prep_v, prep_p, exp_a_ok = sem("prep_v"), sem("prep_p"), sem("exp_a_ok")
        x_mm, bc_mm, z_mm, y_mm, seg_mm, xtr_mm, g_mm, o_mm = (sem(n) for n in (
            "x_mm", "bc_mm", "z_mm", "y_mm", "seg_mm", "xtr_mm", "g_mm", "o_mm"))
        raw_ok, taps, tanh_b, tanh_z, tanh_x, exp_ok, xrow_ok, o_sb = (sem(n) for n in (
            "raw_ok", "taps", "tanh_b", "tanh_z", "tanh_x", "exp_ok", "xrow_ok", "o_sb"))
        bc_ok, yd_ok, yg_ok, xs_ok, zs_ok, gm_ok, dec_p, ysq_ok = (sem(n) for n in (
            "bc_ok", "yd_ok", "yg_ok", "xs_ok", "zs_ok", "gm_ok", "dec_p", "ysq_ok"))
        tap_v = sem("tap_v")
        h2_ok, st2_ok, u2_ok, u2T_mm, u2T_sb, hb_ok = (sem(n) for n in (
            "h2_ok", "st2_ok", "u2_ok", "u2T_mm", "u2T_sb", "hb_ok"))
        lg_mm, sm_v, sm_a, prob_ok, pT_mm, pT_sb, tab_st = (sem(n) for n in (
            "lg_mm", "sm_v", "sm_a", "prob_ok", "pT_mm", "pT_sb", "tab_st"))
        cmp_ok, cnt_mm, srch_v, l1_mm, hid_ok, l2_mm, stg_ok, out_st = (sem(n) for n in (
            "cmp_ok", "cnt_mm", "srch_v", "l1_mm", "hid_ok", "l2_mm", "stg_ok", "out_st"))
        out_st = [sem("out_st0"), sem("out_st1")]
        tot_ok, off_mm, pos_ok, posT_mm, hot_ok, lst_mm, lst_ok, lst_st = (sem(n) for n in (
            "tot_ok", "off_mm", "pos_ok", "posT_mm", "hot_ok", "lst_mm", "lst_ok", "lst_st"))
        idx_ld = [sem(f"idx_ld{n}") for n in range(3)]
        got_ld = [sem(f"got_ld{n}") for n in range(E + 1)]
        xe_mm, xe_sb, e1_mm, e1_ok, e2_mm, ye_ok, yt_mm, ys_ok, added = (sem(n) for n in (
            "xe_mm", "xe_sb", "e1_mm", "e1_ok", "e2_mm", "ye_ok", "yt_mm", "ys_ok", "added"))
        yel_ok, left_ok, left_mm, dup_ok = sem("yel_ok"), sem("left_ok"), sem("left_mm"), sem("dup_ok")

        table_dram = nc.dram_tensor("table_dram", (T * TOK, ROW), F32).ap()
        list_dram = nc.dram_tensor("list_dram", (E, SLOTA * SLOTB), U32).ap()
        out = a["out"]

        block = ctx.enter_context(nc.Block())

        def tile_of(ap, t, n=1):
            return ap[:, bass.ds(t * TOK, n * TOK)]

        def ps_h(t, n=1):
            return psf[0:TOK, bass.ds(t * 128, n * 128)]
        XA, XB, BC, G = ps[:, 0, 0:PAIR], ps[:, 0, PAIR:2 * PAIR], ps[:, 1, 0:PAIR], ps[0:TOK, 1, PAIR:2 * PAIR]
        Z = ps[:, 2, 0:2 * PAIR]
        SEG = [ps[0:TOK, 3 + j, 0:NH * TOK] for j in range(2)]
        Y = ps[:, 5, 0:2 * PAIR].rearrange("p (c n) -> p c n", c=2)
        XR = ps[0:TOK, 6, :].rearrange("p (j c) -> p j c", j=2)
        O = ps[0:TOK, 7, 0:2 * (D + 1)].rearrange("p (j c) -> p j c", j=2)

        @block.sync
        def _(sp):
            for dst, name, key in (
                    (wtok[:, :], "wtok", "wtok"), *((xT[:, :, c * TOK:n * TOK], c, n) for c, n in XCUT), (w_in[:, :], "w_in", "w_in"),
                    (ident[:, :], "ident", "ident"), (rows[:, :], "rows", "rows"), (tri[:, :], "tri", "tri"),
                    (mask32[:, :], "mask", "mask"), (cols[:, :], "cols", "cols"),
                    (w_out_raw[:, :, :], "w_out", "w_out"), (gate_w[:, :], "gate_w", "gate"),
                    (consts[:, :], "consts", "consts"), (sw1[:, :], "sw1", "sw1"), (sw2[:, :, :], "sw2", "sw2"),
                    (sb2[:, :], "sb2", "sb2"), (biases[:, :], "biases", "biases"),
                    (w1[:, :, :], "w1", "w1"), (w2[:, :, :], "w2", "w2")):
                if isinstance(name, int):
                    sp.dma_start(dst, a["xT"][:, :, name * TOK:key * TOK]).then_inc(x_ld[name], 16)
                    continue
                sp.dma_start(dst, a[name]).then_inc(ld[key], 16)
            sp.wait_ge(prob_ok, 2)
            sp.dma_start(table_dram.rearrange("(t p) c -> p t c", p=TOK), table[:, :, :]).then_inc(tab_st, 16)
            with sp.Fori(0, PAIRS // 2) as i:
                for q in range(2):
                    sp.wait_ge(stg_ok, 2 * i + q + 1)
                    sp.dma_start(out[bass.ds((2 * i + q) * PAIR, PAIR), :].rearrange("(j p) c -> p j c", p=TOK),
                                 stage[:, q, :, :]).then_inc(out_st[q], 16)
            sp.wait_ge(stg_ok, PAIRS)
            sp.dma_start(out[(PAIRS - 1) * PAIR:NTOK - S, :], stage[:, 0, 0, :]).then_inc(out_st[0], 16)
            sp.dma_start(out[NTOK - S:NTOK, :], stage[0:S, 0, 1, :]).then_inc(out_st[0], 16)
            sp.wait_ge(lst_ok, 1)
            for half in range(2):
                sp.dma_start(list_dram[8 * half:8 * half + 8, :].rearrange("e (a b) -> (e a) b", b=SLOTB),
                             lst[:, half, :]).then_inc(lst_st, 16)
            sp.wait_ge(lst_st, 32)
            sp.dma_start(idx[:, :], list_dram[:, 0:MAIN].rearrange("e p -> p e"),
                         allow_slow_non_contiguous=True).then_inc(idx_ld[0], 16)
            sp.dma_start(idx_l[:, :], list_dram[:, MAIN:CAP].rearrange("e (r o) -> e r o", o=1)).then_inc(idx_ld[1], 16)
            sp.dma_start(idx_row[:, :].rearrange("p (e r) -> p e r", e=E),
                         list_dram[:, MAIN:CAP].rearrange("(o e) r -> o e r", o=1).broadcast_to([NL, E, LEFT])
                         ).then_inc(idx_ld[2], 16)

        @block.tensor
        def _(pe):
            pe.wait_ge(ld["wtok"], 16)
            for t in range(T):
                if t in x_ld:
                    pe.wait_ge(x_ld[t], 16)
                for half in range(2):
                    mm = pe.matmul(ps_h(t), xT[:, half, t * TOK:(t + 1) * TOK], wtok[:, half * D:(half + 1) * D],
                                   start=(half == 0), stop=(half == 1))
                mm.then_inc(h_mm, 1)
            pe.wait_ge(ld["ident"], 16)
            pe.wait_ge(h_sb, BANKS)
            for t in range(T):
                pe.wait_ge(u_ok, t + 1)
                pe.transpose(psf[:, t * 128:t * 128 + TOK], u[:, t, :], ident[0:TOK, 0:TOK]).then_inc(uT_mm, 1)
            pe.wait_ge(ld["w_in"], 16)
            for t in range(T):
                pe.wait_ge(uT_sb, t // 4 + 1)
                mm = pe.matmul(ps[0:TOK, 6, t * NH:(t + 1) * NH], tile_of(uT, t), w_in[:, 640:644], start=True, stop=True)
            mm.then_inc(dt_mm, 1)
            pe.wait_ge(ld["tri"], 16)
            pe.wait_ge(dec_ok, 1)
            pe.matmul(ps[0:TOK, 7, 0:T * NH], tri[:, :], decay, start=True, stop=True).then_inc(cum_mm, 1)
            pe.wait_ge(cum_ok, 1)
            pe.wait_ge(prep_v, 3)

            def block_mm(i, old, new):
                if new:
                    if old:
                        pe.wait_ge(raw_ok, 2 * i - 1)
                    for dst, c in ((XA, 256), (XB, 384)):
                        mm = pe.matmul(dst, w_in[:, c:c + 128], tile_of(uT, 2 * i, 2), start=True, stop=True)
                    mm.then_inc(x_mm, 1)
                    if old:
                        pe.wait_ge(zs_ok, i)
                    for c in range(2):
                        mm = pe.matmul(Z[:, c * PAIR:(c + 1) * PAIR], w_in[:, c * 128:(c + 1) * 128],
                                       tile_of(uT, 2 * i, 2), start=True, stop=True)
                    mm.then_inc(z_mm, 1)
                if old:
                    pe.wait_ge(gm_ok, i)
                    pe.wait_ge(xrow_ok, i)
                    for j in range(2):
                        for hh in range(NH):
                            mm = pe.matmul(Y[64 * (hh % 2):64 * (hh % 2) + 64, hh // 2, j * TOK:(j + 1) * TOK],
                                           xrow[:, j, hh * HD:(hh + 1) * HD], gm[:, j, hh, :], start=True, stop=True)
                    mm.then_inc(y_mm, 1)
                if new:
                    if old:
                        pe.wait_ge(raw_ok, 2 * i)
                    pe.matmul(BC, w_in[:, 512:640], tile_of(uT, 2 * i, 2), start=True, stop=True).then_inc(bc_mm, 1)
                    if old:
                        pe.wait_ge(exp_ok, i)
                    pe.wait_ge(dec_p, i + 1)
                    for j in range(2):
                        for hh in range(NH):
                            pe.matmul(SEG[j][:, hh * TOK:(hh + 1) * TOK],
                                      decay_p[:, j, hh:hh + 1].broadcast_to([TOK, TOK]), tri[:, :],
                                      start=(hh == 0), stop=False, skip_group_check=True)
                        mm = pe.matmul(SEG[j], ident16[0:TOK, 0:TOK],
                                       mask[:, :].unsqueeze(1).broadcast_to([TOK, NH, TOK]),
                                       start=False, stop=True, skip_group_check=True)
                    mm.then_inc(seg_mm, 1)
                    pe.wait_ge(bc_ok, i + 1)
                    for j in range(2):
                        mm = pe.matmul(G[:, j * TOK:(j + 1) * TOK], bs[:, j * TOK:(j + 1) * TOK],
                                       cs[:, j * TOK:(j + 1) * TOK], start=True, stop=True)
                    mm.then_inc(g_mm, 1)
                    pe.wait_ge(xs_ok, i + 1)
                    for j in range(2):
                        for c in range(2):
                            mm = pe.transpose(XR[:, j, c * 128:(c + 1) * 128], xs[:, c, j * TOK:(j + 1) * TOK],
                                              ident[:, :])
                    mm.then_inc(xtr_mm, 1)
                if old:
                    pe.wait_ge(yg_ok, i)
                    pe.wait_ge(ysq_ok, i)
                    pe.wait_ge(o_sb, i)
                    for j in range(2):
                        for c in range(2):
                            pe.matmul(O[:, j, 0:D], yg[:, c, j * TOK:(j + 1) * TOK], w_out[:, c, :],
                                      start=(c == 0), stop=(c == 1))
                        for c in range(2):
                            mm = pe.matmul(O[:, j, D:D + 1], ysq[:, c, j * TOK:(j + 1) * TOK], ones[:, 0:1],
                                           start=(c == 0), stop=(c == 1))
                    mm.then_inc(o_mm, 1)

            block_mm(0, old=False, new=True)
            with pe.Fori(1, PAIRS) as i:
                block_mm(i, old=True, new=True)
            block_mm(PAIRS, old=True, new=False)

            pe.wait_ge(o_sb, PAIRS + 1)
            for t in range(T):
                pe.wait_ge(u2_ok, t + 1)
                pe.transpose(psf[:, t * 128:t * 128 + TOK], table[:, t, 0:D], ident[0:TOK, 0:TOK]).then_inc(u2T_mm, 1)
            pe.wait_ge(ld["gate"], 16)
            for t in range(T):
                pe.wait_ge(u2T_sb, t // 4 + 1)
                mm = pe.matmul(ps[0:TOK, 6, t * E:(t + 1) * E], tile_of(uT, t), gate_w[:, :], start=True, stop=True)
            mm.then_inc(lg_mm, 1)
            pe.wait_ge(prob_ok, 2)
            for g in range(GROUPS):
                mm = pe.transpose(ps[:, 7, g * TOK:(g + 1) * TOK],
                                  prob[:, 8 * g:8 * g + 8, :].rearrange("p t e -> p (t e)"), ident[0:TOK, 0:TOK])
            mm.then_inc(pT_mm, 1)

            def l1(p, q):
                for c in range(HC):
                    mm = pe.matmul(ps[:, 2 * q + c // 2, (c % 2) * PAIR:(c % 2 + 1) * PAIR],
                                   sw1[:, c * 128:(c + 1) * 128], tile_of(uT, 2 * p, 2), start=True, stop=True)
                mm.then_inc(l1_mm, 1)

            def l2(q, j):
                for c in range(HC):
                    mm = pe.matmul(ps[0:TOK, 4 + q, j * D:(j + 1) * D], hid[:, q, c, j * TOK:(j + 1) * TOK],
                                   sw2[:, c, :], start=(c == 0), stop=(c == HC - 1))
                return mm

            def count(n):
                pe.wait_ge(cmp_ok, n + 1)
                pe.matmul(ps[:, 7, 0:1], same_e, cnt[:, :], start=True, stop=True).then_inc(cnt_mm, 1)

            pe.wait_ge(ld["sw1"], 16)
            pe.wait_ge(ld["sw2"], 16)
            pe.wait_ge(ld["consts"], 16)
            pe.wait_ge(pT_sb, 1)
            with pe.Fori(0, PAIRS // 2) as i:
                for q in range(2):
                    count(6 * i + 3 * q)
                    l1(2 * i + q, q)
                    count(6 * i + 3 * q + 1)
                    pe.wait_ge(hid_ok, 2 * i + q + 1)
                    l2(q, 0)
                    count(6 * i + 3 * q + 2)
                    l2(q, 1).then_inc(l2_mm, 1)
            l1(PAIRS - 1, 0)
            pe.wait_ge(hid_ok, PAIRS)
            pe.wait_ge(stg_ok, PAIRS - 1)
            l2(0, 0)
            l2(0, 1).then_inc(l2_mm, 1)

            pe.wait_ge(tot_ok, 1)
            pe.matmul(ps[:, 7, 0:6], same_e, pre[:, :], start=True, stop=False)
            pe.matmul(ps[:, 7, 0:6], below, tot[:, :], start=False, stop=True).then_inc(off_mm, 1)
            pe.wait_ge(pos_ok, 1)
            for g in range(GROUPS):
                mm = pe.transpose(ps[0:TOK, 6, g * 128:(g + 1) * 128], pos[:, g, :], ident[:, :])
            mm.then_inc(posT_mm, 1)
            pe.wait_ge(hot_ok, 1)
            for t in range(T):
                for half in range(2):
                    mm = pe.matmul(ps[0:8 * SLOTA, 2 + half, 0:8 * SLOTB], hotV[:, t, 8 * half:8 * half + 8, :],
                                   hotB[:, t, 8 * half:8 * half + 8, :], start=(t == 0), stop=(t == T - 1))
            mm.then_inc(lst_mm, 1)

            pe.wait_ge(ld["w1"], 16)
            pe.wait_ge(ld["w2"], 16)
            pe.wait_ge(got_ld[E], 16)
            pe.transpose(ps[:, 7, 0:NL], got[0:NL, E, 0:D], ident[0:NL, 0:NL]).then_inc(xe_mm, 1)

            def first(e):
                pe.wait_ge(got_ld[e], 16)
                if e:
                    pe.wait_ge(xe_sb, e)
                pe.transpose(ps[:, 6 + e % 2, 128 + 0:256], got[:, e, 0:D], ident[:, :]).then_inc(xe_mm, 1)

            def layer1(e):
                pe.wait_ge(xe_sb, e + 2)
                if e >= 2:
                    pe.wait_ge(e1_ok, e - 1)
                b = 2 * (e % 2)
                for c in range(HC):
                    mm = pe.matmul(ps[:, b + c // 2, (c % 2) * CAP:(c % 2 + 1) * CAP], w1[:, e, c * 128:(c + 1) * 128],
                                   xe[:, e, :], start=True, stop=True)
                mm.then_inc(e1_mm, 1)

            def layer2(e):
                pe.wait_ge(e1_ok, e + 1)
                if e >= 2:
                    pe.wait_ge(ys_ok, e - 1)
                for c in range(HC):
                    mm = pe.matmul(ps[:, 4 + e % 2, 0:CAP], w2[:, e, c * D:(c + 1) * D], hid[:, e % 2, c, 0:CAP],
                                   start=(c == 0), stop=(c == HC - 1))
                mm.then_inc(e2_mm, 1)

            def turn(e):
                pe.wait_ge(ye_ok, e + 1)
                if e >= 2:
                    pe.wait_ge(ys_ok, e - 1)
                pe.transpose(ps[:, 4 + e % 2, 256:384], ye[:, e, 0:MAIN], ident[:, :]).then_inc(yt_mm, 1)

            first(0)
            for e in range(E):
                if e + 1 < E:
                    first(e + 1)
                layer1(e)
                if e:
                    layer2(e - 1)
                if e >= 2:
                    turn(e - 2)
            layer2(E - 1)
            turn(E - 2)
            turn(E - 1)
            pe.wait_ge(yel_ok, 1)
            pe.transpose(ps[0:NL, 6, 0:D], yel[:, :], ident[:, :]).then_inc(yt_mm, 1)
            pe.wait_ge(dup_ok, 1)
            pe.wait_ge(left_ok, 1)
            pe.matmul(ps[0:NL, 6, 256:256 + D], eqm[:, :], yl[:, 0, :], start=True, stop=True).then_inc(left_mm, 1)

        @block.scalar
        def _(act):
            def keep_h(g, n):
                act.wait_ge(h_mm, 4 * g + n)
                act.activation(h[:, bass.ds(4 * g, n), :].rearrange("p t c -> p (t c)"), ps_h(4 * g, n), ACT.Copy)\
                   .then_inc(h_sb, 1)
            with act.Fori(0, T // 4) as g:
                keep_h(g, 4)
            keep_h(T // 4, T % 4)

            def keep_turned(g, n, turned, kept):
                act.wait_ge(turned, 4 * g + n)
                act.activation(tile_of(uT, 4 * g, n).rearrange("p (t c) -> p t c", t=n),
                               psf[:, bass.ds(g * 512, n * 128)].rearrange("p (t c) -> p t c", t=n)[:, :, 0:TOK],
                               ACT.Copy).then_inc(kept, 1)
            with act.Fori(0, T // 4) as g:
                keep_turned(g, 4, uT_mm, uT_sb)
            keep_turned(T // 4, T % 4, uT_mm, uT_sb)
            act.wait_ge(ld["rows"], 16)
            act.activation(exp_a[:, :], a_log, ACT.Exp).then_inc(exp_a_ok, 1)
            act.wait_ge(dtx_ok, 1)
            act.activation(dt_abs, dt_x, ACT.Abs).then_inc(a_step, 1)
            act.wait_ge(a_step, 1)
            act.activation(dt_exp, dt_abs, ACT.Exp, scale=-1.0).then_inc(a_step, 1)
            act.wait_ge(a_step, 2)
            act.activation(dt_log, dt_exp, ACT.Ln, bias=1.0).then_inc(log_ok, 1)
            act.activation(tanhz[:, 0, 0:1], ident[:, 0:1], ACT.Tanh).then_inc(o_sb, 1)
            act.wait_ge(o_sb, 1)
            act.wait_ge(ld["cols"], 16)
            act.wait_ge(cum_ok, 1)

            def block_act(i, old, new):
                if new:
                    act.wait_ge(x_mm, i + 1)
                    if old:
                        act.wait_ge(taps, 3 * i)
                    act.activation(raw[:, 0:2, :].rearrange("p c n -> p (c n)"), ps[:, 0, 0:2 * PAIR], ACT.Copy)\
                       .then_inc(raw_ok, 1)
                    act.wait_ge(bc_mm, i + 1)
                    act.activation(raw[:, 2, :], BC, ACT.Copy).then_inc(raw_ok, 1)
                    act.wait_ge(z_mm, i + 1)
                    if old:
                        act.wait_ge(zs_ok, i)
                    act.activation(tanhz[:, :, :].rearrange("p c n -> p (c n)"), Z, ACT.Tanh, scale=0.5).then_inc(tanh_z, 1)
                    act.wait_ge(taps, 3 * i + 3)
                    if old:
                        act.wait_ge(bc_ok, i)
                    act.activation(tanhb[:, :], conv[:, 2, :], ACT.Tanh, scale=0.5).then_inc(tanh_b, 1)
                    act.wait_ge(taps, 3 * i + 3)
                    act.activation(tanh3[:, 0:2, :], conv[:, 0:2, :], ACT.Tanh, scale=0.5).then_inc(tanh_x, 1)
                    act.wait_ge(seg_mm, i + 1)
                    if old:
                        act.wait_ge(gm_ok, i)
                    for j in range(2):
                        for hh in range(NH):
                            ex_ = act.activation(lmask[:, j, hh, :], SEG[j][:, hh * TOK:(hh + 1) * TOK], ACT.Exp,
                                                 bias=neg_cum[:, bass.ds((2 * i + j) * NH + hh, 1)])
                    ex_.then_inc(exp_ok, 1)
                    act.wait_ge(xtr_mm, i + 1)
                    if old:
                        act.wait_ge(y_mm, i)
                    act.activation(xrow[:, :, :], XR, ACT.Copy).then_inc(xrow_ok, 1)
                if old:
                    act.wait_ge(o_mm, i)
                    act.activation(o[:, bass.ds(2 * (i - 1), 2), :], O, ACT.Copy).then_inc(o_sb, 1)

            block_act(0, old=False, new=True)
            with act.Fori(1, PAIRS) as i:
                block_act(i, old=True, new=True)
            block_act(PAIRS, old=True, new=False)

            with act.Fori(0, T // 4) as g:
                keep_turned(g, 4, u2T_mm, u2T_sb)
            keep_turned(T // 4, T % 4, u2T_mm, u2T_sb)
            act.wait_ge(sm_v, 1)
            act.activation(ex[:, :, :], prob[:, 0:T, :], ACT.Exp).then_inc(sm_a, 1)

            act.wait_ge(ld["biases"], 16)

            def gelu(p, q):
                act.wait_ge(l1_mm, p + 1)
                for c in range(HC):
                    g_ = act.activation(hid[:, q, c, :], ps[:, 2 * q + c // 2, (c % 2) * PAIR:(c % 2 + 1) * PAIR],
                                        ACT.Gelu_apprx_tanh, bias=sb1[:, c:c + 1])
                g_.then_inc(hid_ok, 1)
            act.wait_ge(pT_mm, 1)
            act.activation(pse[:, :, :].rearrange("p g n -> p (g n)"), ps[:, 7, 0:GROUPS * TOK], ACT.Copy).then_inc(pT_sb, 1)
            act.activation(hid[:, 0, 0, 0:1], ident[:, 0:1], ACT.Gelu_apprx_tanh).then_inc(a_step, 1)
            act.wait_ge(a_step, 3)
            with act.Fori(0, PAIRS // 2) as i:
                for q in range(2):
                    gelu(2 * i + q, q)
            gelu(PAIRS - 1, 0)

            act.wait_ge(l2_mm, PAIRS)
            for e in range(E):
                act.wait_ge(e1_mm, e + 1)
                if e >= 2:
                    act.wait_ge(e2_mm, e - 1)
                b = 2 * (e % 2)
                for c in range(HC):
                    g_ = act.activation(hid[:, e % 2, c, 0:CAP], ps[:, b + c // 2, (c % 2) * CAP:(c % 2 + 1) * CAP],
                                        ACT.Gelu_apprx_tanh, bias=b1[:, e * HC + c:e * HC + c + 1])
                g_.then_inc(e1_ok, 1)

        @block.gpsimd
        def _(pool):
            pool.memset(half_neg[:, :], -0.5).then_inc(p_step, 1)
            pool.memset(ones[:, :], 1.0).then_inc(prep_p, 1)
            pool.memset(prob[:, :, :], -1.0).then_inc(prep_p, 1)
            pool.memset(cur[:, :], 0).then_inc(prep_p, 1)
            pool.wait_ge(p_step, 1)
            pool.wait_ge(var_ok, 1)
            pool.tensor_tensor(rstd, s_var, half_neg[:, :], ALU.pow).then_inc(pow_ok, 1)
            pool.wait_ge(dec_ok, 1)

            def pair_decay(i):
                pool.tensor_copy(decay_p[:, :, :].rearrange("p j h -> p (j h)"), decay[:, bass.ds(2 * NH * i, 2 * NH)])\
                    .then_inc(dec_p, 1)
            pair_decay(0)

            def square(i):
                pool.wait_ge(yg_ok, i)
                pool.tensor_tensor(ysq[:, :, :], yg[:, :, :], yg[:, :, :], ALU.mult).then_inc(ysq_ok, 1)
            with pool.Fori(1, PAIRS) as i:
                pool.wait_ge(seg_mm, i)
                pair_decay(i)
                square(i)
            square(PAIRS)
            pool.wait_ge(var_ok, 2)
            pool.tensor_tensor(rstd, s_var, half_neg[:, :], ALU.pow).then_inc(pow_ok, 1)
            pool.wait_ge(var_ok, 3)
            pool.tensor_tensor(rstd, s_var, half_neg[:, :], ALU.pow).then_inc(pow_ok, 1)
            pool.wait_ge(u2_ok, T)
            pool.wait_ge(ld["sb2"], 16)
            pool.tensor_tensor(h[:, :, :], h[:, :, :], sb2[:, :].unsqueeze(1).broadcast_to([TOK, T, D]), ALU.add)\
                .then_inc(hb_ok, 1)
            pool.wait_ge(tab_st, 16)
            pool.wait_ge(idx_ld[1], 16)
            pool.indirect_dma_start(got[0:NL, E, :], None, table_dram, bass.IndirectOffsetOnAxis(idx_l[:, 0:1], 0))\
                .then_inc(got_ld[E], 16)
            pool.wait_ge(idx_ld[0], 16)
            for e in range(E):
                pool.indirect_dma_start(got[:, e, :], None, table_dram, bass.IndirectOffsetOnAxis(idx[:, e:e + 1], 0))\
                    .then_inc(got_ld[e], 16)
            pool.wait_ge(out_st[0], 16 * (PAIRS // 2 + 2))
            pool.wait_ge(out_st[1], 16 * (PAIRS // 2))
            for e in range(E):
                pool.wait_ge(ys_ok, e + 1)
                if e:
                    pool.wait_ge(added, 16 * e)
                pool.indirect_dma_start(out, bass.IndirectOffsetOnAxis(idx[:, e:e + 1], 0), ys[:, e % 4, :], None,
                                        compute_op=ALU.add).then_inc(added, 16)
            pool.wait_ge(left_ok, 2)
            pool.wait_ge(added, 16 * E)
            pool.indirect_dma_start(out, bass.IndirectOffsetOnAxis(idx_s[:, 0:1], 0), yl[:, 1, :], None,
                                    compute_op=ALU.add).then_inc(added, 16)
            pool.wait_ge(added, 16 * (E + 1))

        @block.vector
        def _(dve):
            done = [0]

            def chain(ins):
                done[0] += 1
                ins.then_inc(v_step, 1)
                dve.wait_ge(v_step, done[0])

            dve.wait_ge(ld["mask"], 16)
            dve.tensor_copy(mask[:, :], mask32[:, :]).then_inc(prep_v, 1)
            dve.wait_ge(ld["ident"], 16)
            dve.tensor_copy(ident16[:, :], ident[:, :]).then_inc(prep_v, 1)
            dve.wait_ge(ld["cols"], 16)
            dve.wait_ge(ld["w_out"], 16)
            for c in range(2):
                wo = dve.tensor_scalar(w_out[:, c, :], w_out_raw[:, c, :], norm_w[:, c:c + 1], None, ALU.mult)
            wo.then_inc(prep_v, 1)
            dve.wait_ge(ld["consts"], 16)
            chain(dve.tensor_copy(bit_i[:, :], bitf))

            def variance(count_of_norms):
                me, qe, mo, qo = stats[:, :, 1], stats[:, :, 2], stats[:, :, 4], stats[:, :, 5]
                dve.tensor_tensor(s_sum, me, mo, ALU.add)
                dve.tensor_tensor(s_dif, me, mo, ALU.subtract)
                chain(dve.tensor_tensor(s_sq, qe, qo, ALU.add))
                dve.tensor_scalar(mean, s_sum, 0.5, None, ALU.mult)
                chain(dve.scalar_tensor_tensor(s_dif, s_dif, 0.25, s_dif, ALU.mult, ALU.mult))
                chain(dve.tensor_scalar(s_sq, s_sq, 1.0 / D, EPS, ALU.mult, ALU.add))
                dve.tensor_tensor(s_var, s_sq, s_dif, ALU.add).then_inc(var_ok, 1)

            with dve.Fori(0, T // 4) as g:
                dve.wait_ge(h_sb, g + 1)
                for j in range(4):
                    dve.bn_stats(stats[:, 4 * g + j, :], h[:, 4 * g + j, :]).then_inc(st_a, 1)
            dve.wait_ge(h_sb, BANKS)
            for t in range(T - T % 4, T):
                dve.bn_stats(stats[:, t, :], h[:, t, :]).then_inc(st_a, 1)
            dve.wait_ge(st_a, T)
            variance(1)
            dve.wait_ge(pow_ok, 1)
            with dve.Fori(0, T) as t:
                dve.tensor_scalar(u[:, t, :], h[:, t, :], mean[:, bass.ds(t, 1)], rstd[:, bass.ds(t, 1)],
                                  ALU.subtract, ALU.mult).then_inc(u_ok, 1)
            dve.wait_ge(dt_mm, 1)
            dve.wait_ge(ld["rows"], 16)
            per_tile = lambda ap: ap.unsqueeze(1).broadcast_to([TOK, T, NH])
            tiles = lambda ap: ap.rearrange("p (t h) -> p t h", h=NH)
            dve.tensor_tensor(tiles(dt_x), tiles(ps[0:TOK, 6, 0:T * NH]), per_tile(dt_bias), ALU.add).then_inc(dtx_ok, 1)
            dve.wait_ge(dtx_ok, 1)
            dve.wait_ge(log_ok, 1)
            chain(dve.scalar_tensor_tensor(dt, dt_x, 0.0, dt_log, ALU.max, ALU.add))
            dve.wait_ge(exp_a_ok, 1)
            dve.scalar_tensor_tensor(tiles(decay), tiles(dt), -1.0, per_tile(exp_a[:, :]), ALU.mult, ALU.mult)\
                .then_inc(dec_ok, 1)
            chain(dve.tensor_scalar(dt4, dt, 0.25, None, ALU.mult))
            dve.wait_ge(cum_mm, 1)
            dve.tensor_scalar(neg_cum, ps[0:TOK, 7, 0:T * NH], -1.0, None, ALU.mult).then_inc(cum_ok, 1)

            def block_dve(i, old, new):
                if new:
                    for n in range(4):
                        for k, c in enumerate((0, 1, 2)):
                            if n:
                                dve.wait_ge(tap_v, 9 * i + 3 * (n - 1) + k + 1)
                            else:
                                dve.wait_ge(raw_ok, 2 * i + 1 + (c == 2))
                                if old and c == 0:
                                    dve.wait_ge(xs_ok, i)
                            src, dst = (ap[:, c, :].rearrange("p (s k) -> p s k", k=S) for ap in (raw, conv))
                            w = conv_w[:, 4 * c + 3 - n:4 * c + 4 - n]
                            if n == 0:
                                ins = dve.tensor_scalar(conv[:, c, :], raw[:, c, :], w, conv_b[:, c:c + 1],
                                                        ALU.mult, ALU.add)
                            else:
                                ins = dve.scalar_tensor_tensor(dst[:, :, n:S], src[:, :, 0:S - n], w,
                                                               dst[:, :, n:S], ALU.mult, ALU.add)
                            ins.then_inc(tap_v if n < 3 else taps, 1)
                    dve.wait_ge(tanh_b, i + 1)
                    if old:
                        dve.wait_ge(g_mm, i)
                    dve.scalar_tensor_tensor(bs[:, :], tanhb[0:NST, :], 1.0, conv[0:NST, 2, :], ALU.add, ALU.mult)
                    dve.scalar_tensor_tensor(cs[:, :], tanhb[NST:2 * NST, :], 1.0, conv[NST:2 * NST, 2, :], ALU.add, ALU.mult)\
                        .then_inc(bc_ok, 1)
                if old:
                    dve.wait_ge(y_mm, i)
                    for c in range(2):
                        yy = dve.scalar_tensor_tensor(yd[:, c, :], xs[:, c, :], d_col[:, c:c + 1], Y[:, c, :],
                                                      ALU.mult, ALU.add)
                    yy.then_inc(yd_ok, 1)
                    dve.wait_ge(yd_ok, i)
                    dve.tensor_tensor(yg[:, :, :], yd[:, :, :], zs[:, :, :], ALU.mult).then_inc(yg_ok, 1)
                if new:
                    dve.wait_ge(tanh_x, i + 1)
                    dve.scalar_tensor_tensor(xs[:, :, :], tanh3[:, 0:2, :], 1.0, conv[:, 0:2, :], ALU.add, ALU.mult)\
                        .then_inc(xs_ok, 1)
                    dve.wait_ge(tanh_z, i + 1)
                    if old:
                        dve.wait_ge(yg_ok, i)
                    dve.scalar_tensor_tensor(zs[:, :, :].rearrange("p c n -> p (c n)"),
                                             tanhz[:, :, :].rearrange("p c n -> p (c n)"), 1.0, Z, ALU.add, ALU.mult)\
                        .then_inc(zs_ok, 1)
                    dve.wait_ge(exp_ok, i + 1)
                    dve.wait_ge(g_mm, i + 1)
                    for j in range(2):
                        for hh in range(NH):
                            g_ = dve.scalar_tensor_tensor(gm[:, j, hh, :], lmask[:, j, hh, :],
                                                          dt4[:, bass.ds((2 * i + j) * NH + hh, 1)],
                                                          G[:, j * TOK:(j + 1) * TOK], ALU.mult, ALU.mult)
                    g_.then_inc(gm_ok, 1)

            block_dve(0, old=False, new=True)
            with dve.Fori(1, PAIRS) as i:
                block_dve(i, old=True, new=True)
            block_dve(PAIRS, old=True, new=False)

            dve.wait_ge(o_sb, PAIRS + 1)
            dve.tensor_scalar(s_var, o[:, :, D], 1.0 / DIN, 16 * EPS, ALU.mult, ALU.add).then_inc(var_ok, 1)
            dve.wait_ge(pow_ok, 2)
            with dve.Fori(0, T) as t:
                dve.scalar_tensor_tensor(h[:, t, :], o[:, t, 0:D], rstd[:, bass.ds(t, 1)], h[:, t, :],
                                         ALU.mult, ALU.add).then_inc(h2_ok, 1)
            dve.wait_ge(h2_ok, T)
            with dve.Fori(0, T) as t:
                dve.bn_stats(stats[:, t, :], h[:, t, :]).then_inc(st2_ok, 1)
            dve.wait_ge(st2_ok, T)
            variance(2)
            dve.wait_ge(pow_ok, 3)
            with dve.Fori(0, T) as t:
                dve.tensor_scalar(table[:, t, 0:D], h[:, t, :], mean[:, bass.ds(t, 1)], rstd[:, bass.ds(t, 1)],
                                  ALU.subtract, ALU.mult).then_inc(u2_ok, 1)
            dve.wait_ge(lg_mm, 1)
            dve.wait_ge(prep_p, 3)
            lg = ps[0:TOK, 6, 0:T * E].rearrange("p (t e) -> p t e", e=E)
            over_e = lambda ap: ap.unsqueeze(2).broadcast_to([TOK, T, E])
            chain(dve.tensor_reduce(mx[:, :], lg, AX.X, ALU.max))
            dve.tensor_tensor(prob[:, 0:T, :], lg, over_e(mx[:, :]), ALU.subtract).then_inc(sm_v, 1)
            dve.wait_ge(sm_a, 1)
            chain(dve.tensor_reduce(den[:, :], ex[:, :, :], AX.X, ALU.add))
            chain(dve.reciprocal(rden[:, :], den[:, :]))
            dve.tensor_tensor(table[:, :, D:ROW], ex[:, :, :], over_e(rden[:, :]), ALU.mult).then_inc(prob_ok, 1)
            dve.wait_ge(sm_v, 1)
            chain(dve.tensor_tensor(prob[:, 0:T, :], ex[:, :, :], over_e(rden[:, :]), ALU.mult))
            dve.tensor_scalar(prob[:, T - 1, :], prob[:, T - 1, :], valid[0:TOK, :], invalid[0:TOK, :],
                              ALU.mult, ALU.add).then_inc(prob_ok, 1)

            dve.wait_ge(pT_sb, 1)
            chain(dve.tensor_copy(cand[:, :], bit_i[:, 0:1]))
            thr = cand[:, :].bitcast(F32)
            dve.wait_ge(hb_ok, 1)

            def step(n, i3):
                dve.tensor_scalar(hits[:, :, :], pse[:, :, :], thr[:, 0:1], 0.0, ALU.is_ge, ALU.add,
                                  accum_out=cnt[:, :]).then_inc(cmp_ok, 1)
                dve.wait_ge(cnt_mm, n + 1)
                dve.tensor_scalar(step_i[:, :], ps[:, 7, 0:1], CAP - 0.5, bitf[:, bass.ds(n, 1)], ALU.is_ge, ALU.mult)\
                    .then_inc(srch_v, 1)
                dve.wait_ge(srch_v, 3 * n + 1)
                dve.tensor_tensor(cur[:, :], cur[:, :], step_i[:, :], ALU.bitwise_or).then_inc(srch_v, 1)
                dve.wait_ge(srch_v, 3 * n + 2)
                dve.tensor_tensor(cand[:, :], cur[:, :], bit_i[:, bass.ds(n + 1, 1)], ALU.bitwise_or).then_inc(srch_v, 1)
                dve.wait_ge(srch_v, 3 * n + 3)

            def add_rows(p, q):
                dve.wait_ge(l2_mm, p + 1)
                dve.tensor_tensor(stage[:, q, :, :].rearrange("p j c -> p (j c)"), ps[0:TOK, 4 + q, 0:2 * D],
                                  h[:, bass.ds(2 * p, 2), :].rearrange("p j c -> p (j c)"), ALU.add).then_inc(stg_ok, 1)

            def part(i, q):
                step(6 * i + 3 * q, None)
                first = isinstance(i, int) and i < 1
                if not (first and q == 0):
                    if not first and (q or not isinstance(i, int)):
                        dve.wait_ge(out_st[1 - q], 16 * i if q else 16 * i - 16)
                    add_rows(2 * i + q - 1, 1 - q)
                step(6 * i + 3 * q + 1, None)
                step(6 * i + 3 * q + 2, None)

            part(0, 0)
            part(0, 1)
            part(1, 0)
            part(1, 1)
            with dve.Fori(2, PAIRS // 2) as i:
                part(i, 0)
                part(i, 1)
            dve.wait_ge(out_st[1], 16 * (PAIRS // 2 - 1))
            add_rows(PAIRS - 2, 1)

            tau = cur[:, :].bitcast(F32)
            dve.tensor_scalar(ge[:, :, :], pse[:, :, :], tau[:, 0:1], None, ALU.is_ge)
            chain(dve.tensor_scalar(m6[:, 1, :, :], pse[:, :, :], tau[:, 0:1], None, ALU.is_equal))
            chain(dve.tensor_tensor(m6[:, 0, :, :], ge[:, :, :], m6[:, 1, :, :], ALU.subtract))
            for k in range(2):
                for g in range(GROUPS):
                    sc_ = dve.tensor_tensor_scan(rank[:, k, g, :], ones[:, :], m6[:, k, g, :], 0.0, ALU.mult, ALU.add)
            chain(sc_)
            chain(dve.tensor_copy(tot[:, :], rank[:, :, :, TOK - 1].rearrange("p k g -> p (k g)")))
            chain(dve.tensor_tensor_scan(pre[:, :], ones[:, 0:6], tot[:, :], 0.0, ALU.mult, ALU.add))
            dve.tensor_tensor(pre[:, :], pre[:, :], tot[:, :], ALU.subtract).then_inc(tot_ok, 1)
            dve.wait_ge(out_st[0], 16 * (PAIRS // 2))
            add_rows(PAIRS - 1, 0)
            dve.wait_ge(off_mm, 1)
            chain(dve.tensor_copy(off[:, :], ps[:, 7, 0:6]))
            for k in range(2):
                for g in range(GROUPS):
                    st_ = dve.scalar_tensor_tensor(rank[:, k, g, :], rank[:, k, g, :], off[:, 3 * k + g:3 * k + g + 1],
                                                   m6[:, k, g, :], ALU.add, ALU.mult)
            dve.tensor_scalar(ge[:, :, :], ge[:, :, :], -BIG, BIG - 1, ALU.mult, ALU.add)
            chain(st_)
            chain(dve.tensor_tensor(pos[:, :, :], rank[:, 0, :, :], rank[:, 1, :, :], ALU.add))
            dve.tensor_tensor(pos[:, :, :], pos[:, :, :], ge[:, :, :], ALU.add).then_inc(pos_ok, 1)
            dve.wait_ge(posT_mm, 1)
            chain(dve.tensor_copy(pos_i[:, :], ps[0:TOK, 6, 0:T * E]))
            dve.tensor_scalar(pa_i[:, :], pos_i[:, :], 4, None, ALU.logical_shift_right)
            chain(dve.tensor_scalar(pb_i[:, :], pos_i[:, :], SLOTB - 1, None, ALU.bitwise_and))
            dve.tensor_copy(pa_f[:, :], pa_i[:, :])
            chain(dve.tensor_copy(pb_f[:, :], pb_i[:, :]))
            hot = lambda ap, n: ap.rearrange("p (t e) -> p t e", e=E).rearrange("p t e -> p (t e)").unsqueeze(2)\
                .broadcast_to([TOK, T * E, n])
            flat = lambda ap: ap.rearrange("p t e n -> p (t e) n")
            chain(dve.tensor_tensor(flat(hotA[:, :, :, :]), hot(pa_f[:, :], SLOTA),
                                    iota16[0:TOK, 0:SLOTA].unsqueeze(1).broadcast_to([TOK, T * E, SLOTA]), ALU.is_equal))
            dve.tensor_tensor(hotV[:, :, :, :].rearrange("p t e n -> p t (e n)"),
                              hotA[:, :, :, :].rearrange("p t e n -> p t (e n)"),
                              value[0:TOK, :].unsqueeze(2).broadcast_to([TOK, T, E * SLOTA]), ALU.mult)
            dve.tensor_tensor(flat(hotB[:, :, :, :]), hot(pb_f[:, :], SLOTB),
                              iota16[0:TOK, :].unsqueeze(1).broadcast_to([TOK, T * E, SLOTB]), ALU.is_equal)\
                .then_inc(hot_ok, 1)
            dve.wait_ge(lst_mm, 1)
            chain(dve.tensor_tensor(dg[:, :, :, :],
                                    ps[0:8 * SLOTA, 2:4, 0:8 * SLOTB].rearrange("p k (e b) -> p k e b", e=8),
                                    diag[0:8 * SLOTA, :].unsqueeze(1).unsqueeze(3).broadcast_to([8 * SLOTA, 2, 8, SLOTB]),
                                    ALU.mult))
            for k in range(2):
                dr = dve.tensor_reduce(dsum[:, k, :], dg[:, k, :, :].rearrange("p e b -> p b e"), AX.X, ALU.add)
            chain(dr)
            dve.tensor_scalar(lst[:, :, :], dsum[:, :, :], float(VALUE0), None, ALU.add).then_inc(lst_ok, 1)
            dve.wait_ge(idx_ld[1], 16)
            dve.wait_ge(idx_ld[2], 16)
            dve.tensor_copy(idx_lf[:, :], idx_l[:, :])
            chain(dve.tensor_copy(idx_rowf[:, :], idx_row[:, :]))
            chain(dve.tensor_scalar(eqm[:, :], idx_rowf[:, :], idx_lf[:, 0:1], None, ALU.is_equal))
            chain(dve.tensor_tensor(eqe[:, :], eqm[:, :], earlier[0:NL, :], ALU.mult))
            chain(dve.tensor_reduce(dup[:, 0:1], eqe[:, :], AX.X, ALU.max))
            chain(dve.tensor_scalar(dup[:, 1:2], dummy[0:NL, :], idx_lf[:, 0:1], None, ALU.subtract))
            dve.scalar_tensor_tensor(idx_s[:, :], dup[:, 1:2], dup[:, 0:1], idx_lf[:, :], ALU.mult, ALU.add)\
                .then_inc(dup_ok, 1)
            dve.wait_ge(xe_mm, 1)
            dve.tensor_copy(xe[:, :, MAIN:CAP], ps[:, 7, 0:NL].rearrange("p (e r) -> p e r", e=E)).then_inc(xe_sb, 1)

            def take(e):
                dve.wait_ge(xe_mm, e + 2)
                dve.tensor_copy(xe[:, e, 0:MAIN], ps[:, 6 + e % 2, 128:256]).then_inc(xe_sb, 1)

            def bias2(e):
                dve.wait_ge(e2_mm, e + 1)
                dve.tensor_scalar(ye[:, e, :], ps[:, 4 + e % 2, 0:CAP], b2[:, e:e + 1], None, ALU.add).then_inc(ye_ok, 1)

            def scale(e):
                dve.wait_ge(yt_mm, e + 1)
                if e >= 4:
                    dve.wait_ge(added, 16 * (e - 3))
                dve.tensor_scalar(ys[:, e % 4, :], ps[:, 4 + e % 2, 256:384], got[:, e, D + e:D + e + 1], None,
                                  ALU.mult).then_inc(ys_ok, 1)
            take(0)
            for e in range(E):
                if e + 1 < E:
                    take(e + 1)
                if e:
                    bias2(e - 1)
                if e >= 2:
                    scale(e - 2)
            bias2(E - 1)
            dve.wait_ge(ye_ok, E)
            dve.tensor_copy(yel[:, :].rearrange("p (e r) -> p e r", e=E), ye[:, :, MAIN:CAP]).then_inc(yel_ok, 1)
            scale(E - 2)
            scale(E - 1)
            chain(dve.tensor_tensor(sc_l[:, 0:E], got[0:NL, E, D:ROW], own_e[0:NL, :], ALU.mult))
            chain(dve.tensor_reduce(sc_l[:, E:E + 1], sc_l[:, 0:E], AX.X, ALU.add))
            dve.wait_ge(yt_mm, E + 1)
            dve.tensor_scalar(yl[:, 0, :], ps[0:NL, 6, 0:D], sc_l[:, E:E + 1], None, ALU.mult).then_inc(left_ok, 1)
            dve.wait_ge(left_mm, 1)
            dve.tensor_copy(yl[:, 1, :], ps[0:NL, 6, 256:256 + D]).then_inc(left_ok, 1)
    return nc


def constants():
    n = np.arange(2 * HOP, dtype=np.float64) + 0.5
    mdct = np.sqrt(4.0 / HOP) * np.cos(np.outer(n + HOP / 2, np.pi / HOP * n[:HOP]))
    wtok = np.sin(np.pi * n / (2 * HOP))[:, None].astype(np.float32) * mdct.astype(np.float32)
    r = np.arange(TOK)
    seq = r[:, None] // S == r[None, :] // S
    tri = (seq & (r[:, None] <= r[None, :])).astype(np.float32)
    q = np.arange(128)
    same = (q[:, None] % E == q[None, :] % E)
    below = same & (q[:, None] // E < q[None, :] // E)
    ea, el = q // SLOTA, q // LEFT
    parts = [
        same, below,
        np.tile([2.0 ** (BITS - 1 - k) if k < BITS else 0.0 for k in range(32)], (128, 1)),
        np.tile(np.arange(16.0), (128, 1)),
        q[:, None] + TOK * np.arange(T)[None, :] - float(VALUE0),
        ea[:, None] == np.arange(8)[None, :],
        np.arange(NL)[None, :] < q[:, None],
        el[:, None] == np.arange(E)[None, :],
        (q < S)[:, None], (q < S)[:, None] - 1.0, (NTOK + q)[:, None], np.full((128, 1), BIG)]
    return {
        "wtok": wtok.reshape(2, HOP, HOP).transpose(1, 0, 2).reshape(128, 2 * D),
        "tri": tri,
        "mask": np.where(tri > 0, 0.0, -1e30).astype(np.float32),
        "ident": np.eye(128, dtype=np.float32),
        "consts": np.concatenate([np.asarray(p, np.float32) for p in parts], axis=1),
    }


def layout(i):
    x = np.zeros((3 * T, NBLK * HOP), np.float32)
    x[:B, HOP:HOP + 4000] = i["x"]
    blocks = x.reshape(3 * T, NBLK, HOP)
    conv_w = i["L0_attn_conv_w"][:, 0, :].reshape(3, 128, 4).transpose(1, 0, 2).reshape(128, 12)
    cols = np.concatenate([
        i["L0_attn_norm_w"].reshape(2, 128).T, conv_w, i["L0_attn_conv_b"].reshape(3, 128).T,
        np.repeat(i["L0_attn_D"], HD).reshape(2, 128).T, np.zeros((128, 2), np.float32)], axis=1)
    return {
        "xT": np.stack([blocks[:, k:k + S].transpose(2, 0, 1).reshape(HOP, T * TOK) for k in range(2)], axis=1),
        "w_in": i["L0_attn_W_in"].T,
        "cols": cols,
        "rows": np.tile(np.concatenate([i["L0_attn_dt_bias"], i["L0_attn_A_log"]]), (TOK, 1)),
        "w_out": i["L0_attn_W_out"].T.reshape(2, 128, D).transpose(1, 0, 2),
        "gate_w": i["L0_ffn_gate_w"],
        "sw1": i["L0_ffn_sw1"],
        "sw2": i["L0_ffn_sw2"].reshape(HC, 128, D).transpose(1, 0, 2),
        "sb2": np.tile(i["L0_ffn_sb2"], (TOK, 1)),
        "biases": np.concatenate([
            i["L0_ffn_sb1"].reshape(HC, 128).T, i["L0_ffn_b1"].reshape(E * HC, 128).T, i["L0_ffn_b2"].T], axis=1),
        "w1": i["L0_ffn_w1"].transpose(1, 0, 2),
        "w2": i["L0_ffn_w2"].reshape(E, HC, 128, D).transpose(2, 0, 1, 3).reshape(128, E, HC * D),
    }


def kernel(**inputs):
    import concourse.bacc as bacc
    from concourse.bass_utils import run_bass_kernel_spmd

    nc = bacc.Bacc("TRN2", target_bir_lowering=False, num_devices=1)
    arrays = layout({k: np.asarray(v) for k, v in inputs.items()}) | constants()
    arrays = {k: np.ascontiguousarray(v) for k, v in arrays.items()}
    aps = {k: nc.dram_tensor("in_" + k, v.shape, F32, kind="ExternalInput").ap() for k, v in arrays.items()}
    aps["out"] = nc.dram_tensor("out_rows", (NTOK + NL, D), F32, kind="ExternalOutput").ap()
    program(nc, aps)
    r = run_bass_kernel_spmd(nc, [{"in_" + k: v for k, v in arrays.items()}], core_ids=[0])
    return r.results[0]["out_rows"][:NTOK].reshape(B, S, D)
```

```python
from contextlib import ExitStack

import numpy as np

import concourse.bass as bass
from concourse import mybir

F32 = mybir.dt.float32
F16 = mybir.dt.float16
BF16 = mybir.dt.bfloat16
I32 = mybir.dt.int32
U32 = mybir.dt.uint32
ALU = mybir.AluOpType
ACT = mybir.ActivationFunctionType
AX = mybir.AxisListType

B, S = 64, 33
HOP = 128
NBLK = S + 1
TOK = 3 * S
T = -(-B // 3)
PAIRS = T // 2
BANKS = -(-T // 4)
PAIR = 2 * TOK
NTOK = B * S
D, DIN, NST, NH, HD = 128, 256, 64, 4, 64
E, HID, HC = 16, 512, 4
CAP = NTOK // E
EPS = 1e-5
MAIN = 128
LEFT = CAP - MAIN
NL = E * LEFT
SLOTB = 16
SLOTA = -(-CAP // SLOTB)
ROW = D + E
GROUPS = 3
BIG = 4096.0
VALUE0 = T * TOK // 2
XCUT = ((0, 2), (2, 6), (6, 12), (12, 17), (17, 22))
AHEAD = 8
NORM1 = ((0, 8), (8, 16), (16, T))
NORM2 = ((0, 14), (14, 18), (18, T))
BITS = 30


def program(nc, a):
    ctx = ExitStack()
    with ctx:
        def sb(name, shape, dt=F32):
            return ctx.enter_context(nc.sbuf_tensor(name, shape, dt))

        def sem(name):
            return ctx.enter_context(nc.semaphore(name))

        xT = sb("xT", [128, 2, T * TOK])
        wtok = sb("wtok", [128, 2 * D])
        w_in = sb("w_in", [128, 644])
        w_out_raw = sb("w_out_raw", [128, 2, D])
        d_eye = sb("d_eye", [TOK, NH, TOK])
        w_out = sb("w_out", [128, 2, D])
        cols = sb("cols", [128, 17])
        norm_w, conv_w, conv_b = cols[:, 0:2], cols[:, 2:14], cols[:, 14:17]
        rows = sb("rows", [TOK, 12])
        dt_bias, a_log, d_row = rows[:, 0:NH], rows[:, NH:2 * NH], rows[:, 2 * NH:3 * NH]
        tri = sb("tri", [TOK, TOK])
        mask32 = sb("mask32", [TOK, TOK])
        mask = sb("mask", [TOK, TOK], BF16)
        ident = sb("ident", [128, 128])
        ident16 = sb("ident16", [128, 128], BF16)
        ones = sb("ones", [128, TOK])
        gate_w = sb("gate_w", [128, E])
        sw1 = sb("sw1", [128, HID])
        sw2 = sb("sw2", [128, HC, D])
        sb2 = sb("sb2", [TOK, D])
        biases = sb("biases", [128, HC + E * HC + E])
        sb1, b1, b2 = biases[:, 0:HC], biases[:, HC:HC + E * HC], biases[:, HC + E * HC:]
        w1 = sb("w1", [128, E, HID])
        w2 = sb("w2", [128, E, HC * D])
        consts = sb("consts", [128, 256 + 32 + 16 + T + 8 + NL + E + 4 + SLOTB + MAIN])
        at = 0

        def const(n):
            nonlocal at
            at += n
            return consts[:, at - n:at]
        same_e = const(128)
        below = const(128)
        bitf = const(32)
        iota16 = const(16)
        value = const(T)
        diag = const(8)
        earlier = const(NL)
        own_e = const(E)
        valid = const(1)
        invalid = const(1)
        dummy = const(1)
        last_a = const(1)
        slide = const(SLOTB + MAIN)

        h = sb("h", [TOK, T, D])
        u = sb("u", [TOK, T, D])
        uT = sb("uT", [128, T * TOK])
        o = sb("o", [TOK, T, D + 1])
        table = sb("table", [TOK, T, ROW])
        stats = sb("stats", [TOK, T, 6])
        small = sb("small", [TOK, 8, T])
        mean, rstd, s_sum, s_dif, s_sq, s_var, shift = (small[:, n, :] for n in range(7))
        zero = sb("zero", [128, D])
        half_neg = sb("half_neg", [TOK, T])
        share = sb("share", [128, 1])
        eps16 = sb("eps16", [TOK, 2])
        dtw = sb("dtw", [TOK, 9, T * NH])
        dt_x, dt_abs, dt_exp, dt_log, dt, decay, bias_s, dt_c, ln_dt = (dtw[:, n, :] for n in range(9))
        rms = sb("rms", [TOK, 2, T])
        exp_a = sb("exp_a", [TOK, NH])
        decay_p = sb("decay_p", [TOK, 2, NH])
        work = sb("work", [128, 7300])
        used = [0]

        def carve(p, *shape):
            n = int(np.prod(shape))
            used[0] += n
            assert used[0] <= 7300
            ap = work[0:p, used[0] - n:used[0]]
            names = "abcd"[:len(shape)]
            if len(shape) == 1:
                return ap
            return ap.rearrange(f"p ({' '.join(names)}) -> p {' '.join(names)}", **dict(zip(names[1:], shape[1:])))
        conv = carve(128, 3, PAIR)
        tanh3 = carve(128, 2, PAIR)
        tanhz = carve(128, 2, PAIR)
        xs = carve(128, 2, PAIR)
        bs = carve(NST, PAIR)
        cs = carve(NST, PAIR)
        tanhb = carve(128, PAIR)
        zs = carve(128, 2, PAIR)
        xrow = carve(TOK, 2, DIN)
        lmask = carve(TOK, 2, NH, TOK)
        gm = carve(TOK, 2, NH, TOK)
        yg = carve(128, 2, PAIR)
        ysq = carve(128, 2, PAIR)
        ysum = carve(128, PAIR)
        yg_last = carve(128, 2, PAIR)
        ysum_last = carve(128, PAIR)
        used[0] = 0
        got = carve(128, E + 1, ROW)
        ys = carve(128, 4, D)
        yl = carve(NL, 2, D)
        hid = carve(128, 2, HC, PAIR)
        stage = carve(TOK, 2, 2, D)
        xe = xT[:, 0, 0:E * CAP].rearrange("p (e c) -> p e c", e=E)
        ye = uT[:, 0:E * CAP].rearrange("p (e c) -> p e c", e=E)
        mx = sb("mx", [TOK, T])
        den = sb("den", [TOK, T])
        rden = sb("rden", [TOK, T])
        ex = sb("ex", [TOK, T, E])
        prob = sb("prob", [TOK, 8 * GROUPS, E])
        pse = sb("pse", [128, GROUPS, TOK])
        hits = sb("hits", [128, GROUPS, TOK])
        cnt = sb("cnt", [128, 1], F16)
        bit_i = sb("bit_i", [128, 32], I32)
        cand = sb("cand", [128, 1], I32)
        kept = sb("kept", [128, 1], I32)
        drop = sb("drop", [128, 1], I32)
        same16 = sb("same16", [128, 128], F16)
        m6 = sb("m6", [128, 2, GROUPS, TOK])
        ge = sb("ge", [128, GROUPS, TOK])
        rank = sb("rank", [128, 2, GROUPS, TOK])
        tot = sb("tot", [128, 6])
        pre = sb("pre", [128, 6])
        off = sb("off", [128, 6])
        pos = sb("pos", [128, GROUPS, TOK])
        pos_i = sb("pos_i", [TOK, E, T], I32)
        pa_i = sb("pa_i", [TOK, E, T], I32)
        pb_i = sb("pb_i", [TOK, E, T], I32)
        pa_h = sb("pa_h", [TOK, E, T], F16)
        pb_h = sb("pb_h", [TOK, E, T], F16)
        iota_t = sb("iota_t", [TOK, SLOTB, T], F16)
        value16 = sb("value16", [TOK, T], F16)
        slide16 = sb("slide16", [128, SLOTB + MAIN], F16)
        sel16 = sb("sel16", [128, NL], F16)
        hotV = o[:, :, :].rearrange("p t c -> p (t c)")[:, 0:T * E * SLOTA // 2].bitcast(F16)\
            .rearrange("p (e n t) -> p e n t", e=E, n=SLOTA)
        hotA = xT[0:TOK, 1, 0:T * E * SLOTA // 2].bitcast(F16).rearrange("p (e n t) -> p e n t", e=E, n=SLOTA)
        hotB = u[:, :, :].rearrange("p t c -> p (t c)").bitcast(F16).rearrange("p (e n t) -> p e n t", e=E, n=SLOTB)
        dg = sb("dg", [8 * SLOTA, 2, 8, SLOTB], F16)
        dgl = sb("dgl", [8 * SLOTA, NL], F16)
        idx = sb("idx", [128, E], U32)
        idx_l = sb("idx_l", [NL, 1], U32)
        idx_lf = sb("idx_lf", [NL, 1])
        idx_rowf = sb("idx_rowf", [NL, NL])
        eqm = sb("eqm", [NL, NL])
        eqe = sb("eqe", [NL, NL])
        dup = sb("dup", [NL, 4])
        idx_s = sb("idx_s", [NL, 1], U32)
        sc_l = sb("sc_l", [NL, E + 1])

        yel = sb("yel", [128, NL])
        ps = ctx.enter_context(nc.psum_tensor("ps", [128, 8, 512], F32))
        psf = ps[:, :, :].rearrange("p b n -> p (b n)")

        x_ld = {c: sem(f"x_ld{c}") for c, _ in XCUT}
        ld = {n: sem("ld_" + n) for n in (
            "wtok", "w_in", "cols", "rows", "tri", "mask", "ident", "w_out", "gate", "sw1", "sw2",
            "sb2", "biases", "w1", "w2", "consts")}
        h_mm, h_sb, st_a = sem("h_mm"), sem("h_sb"), sem("st_a")
        var_ok, pow_ok, u_ok, uT_mm, uT_sb = sem("var_ok"), sem("pow_ok"), sem("u_ok"), sem("uT_mm"), sem("uT_sb")
        dt_mm, dtx_ok, log_ok, dec_ok, cum_mm, cum_ok = (sem(n) for n in (
            "dt_mm", "dtx_ok", "log_ok", "dec_ok", "cum_mm", "cum_ok"))
        v_step, a_step, p_step = sem("v_step"), sem("a_step"), sem("p_step")
        ua_ok, u2a_ok, shift_ok = sem("ua_ok"), sem("u2a_ok"), sem("shift_ok")
        prep_v, prep_p, exp_a_ok = sem("prep_v"), sem("prep_p"), sem("exp_a_ok")
        x_mm, bc_mm, z_mm, y_mm, seg_mm, xtr_mm, g_mm, o_mm = (sem(n) for n in (
            "x_mm", "bc_mm", "z_mm", "y_mm", "seg_mm", "xtr_mm", "g_mm", "o_mm"))
        raw_ok, taps, tanh_b, tanh_z, tanh_x, exp_ok, xrow_ok, o_sb = (sem(n) for n in (
            "raw_ok", "taps", "tanh_b", "tanh_z", "tanh_x", "exp_ok", "xrow_ok", "o_sb"))
        bc_ok, yd_ok, yg_ok, xs_ok, zs_ok, gm_ok, dec_p, ysq_ok = (sem(n) for n in (
            "bc_ok", "yd_ok", "yg_ok", "xs_ok", "zs_ok", "gm_ok", "dec_p", "ysq_ok"))
        tap_v, tap0_ok, sq_p, ms_ok, rms_ok, skip_ok, dtc_ok, ln_ok = (sem(n) for n in (
            "tap_v", "tap0_ok", "sq_p", "ms_ok", "rms_ok", "skip_ok", "dtc_ok", "ln_ok"))
        h2_ok, st2_ok, u2_ok, u2T_mm, u2T_sb, hb_ok = (sem(n) for n in (
            "h2_ok", "st2_ok", "u2_ok", "u2T_mm", "u2T_sb", "hb_ok"))
        lg_mm, sm_v, sm_a, prob_ok, pT_mm, pT_sb, tab_st = (sem(n) for n in (
            "lg_mm", "sm_v", "sm_a", "prob_ok", "pT_mm", "pT_sb", "tab_st"))
        cmp_ok, cnt_mm, srch_v, l1_mm, hid_ok, l2_mm, stg_ok, out_st = (sem(n) for n in (
            "cmp_ok", "cnt_mm", "srch_v", "l1_mm", "hid_ok", "l2_mm", "stg_ok", "out_st"))
        out_st = [sem("out_st0"), sem("out_st1")]
        tot_ok, off_mm, pos_ok, posT_mm, hot_ok, lst_mm, lst_ok, lst_st = (sem(n) for n in (
            "tot_ok", "off_mm", "pos_ok", "posT_mm", "hot_ok", "lst_mm", "lst_ok", "lst_st"))
        zero_ok, odd_st = sem("zero_ok"), sem("odd_st")
        added, joined = [sem("added0"), sem("added1")], sem("joined")
        dg_ok, idx_mm, idx_ok = sem("dg_ok"), sem("idx_mm"), sem("idx_ok")
        got_ld = [sem(f"got_ld{n}") for n in range(E + 1)]
        xe_mm, xe_sb, e1_mm, e1_ok, e2_mm, ye_ok, yt_mm, ys_ok = (sem(n) for n in (
            "xe_mm", "xe_sb", "e1_mm", "e1_ok", "e2_mm", "ye_ok", "yt_mm", "ys_ok"))
        yel_ok, left_ok, left_mm, dup_ok = sem("yel_ok"), sem("left_ok"), sem("left_mm"), sem("dup_ok")

        table_dram = nc.dram_tensor("table_dram", (T * TOK, ROW), F32).ap()
        out = a["out"]
        odd_dram = nc.dram_tensor("odd_dram", (NTOK, D), F32).ap()

        block = ctx.enter_context(nc.Block())

        def tile_of(ap, t, n=1):
            return ap[:, bass.ds(t * TOK, n * TOK)]

        def pair(i):
            return not isinstance(i, int) or 0 <= i < PAIRS

        def last(i):
            return isinstance(i, int) and i == PAIRS - 1

        def ps_h(t, n=1):
            return psf[0:TOK, bass.ds(t * 128, n * 128)]
        XA, XB, BC = ps[:, 0, 0:PAIR], ps[:, 0, PAIR:2 * PAIR], ps[:, 1, 0:PAIR]
        Z = ps[:, 2, 0:2 * PAIR]
        SEG = [ps[0:TOK, 3 + j, 0:NH * TOK] for j in range(2)]
        G = [ps[0:TOK, 3 + j, NH * TOK:(NH + 1) * TOK] for j in range(2)]
        Y = ps[:, 5, 0:2 * PAIR].rearrange("p (c n) -> p c n", c=2)
        XR = ps[0:TOK, 6, :].rearrange("p (j c) -> p j c", j=2)
        O = ps[0:TOK, 7, 0:2 * (D + 1)].rearrange("p (j c) -> p j c", j=2)

        @block.sync
        def _(sp):
            for dst, name, key in (
                    (wtok[:, :], "wtok", "wtok"), *((xT[:, :, c * TOK:n * TOK], c, n) for c, n in XCUT), (w_in[:, :], "w_in", "w_in"),
                    (ident[:, :], "ident", "ident"), (rows[:, :], "rows", "rows"), (tri[:, :], "tri", "tri"),
                    (mask32[:, :], "mask", "mask"), (cols[:, :], "cols", "cols"),
                    (w_out_raw[:, :, :], "w_out", "w_out"), (gate_w[:, :], "gate_w", "gate"),
                    (consts[:, :], "consts", "consts"), (sw1[:, :], "sw1", "sw1"), (sw2[:, :, :], "sw2", "sw2"),
                    (sb2[:, :], "sb2", "sb2"), (biases[:, :], "biases", "biases"),
                    (w1[:, :, :], "w1", "w1"), (w2[:, :, :], "w2", "w2")):
                if isinstance(name, int):
                    sp.dma_start(dst, a["xT"][:, :, name * TOK:key * TOK]).then_inc(x_ld[name], 16)
                    continue
                sp.dma_start(dst, a[name]).then_inc(ld[key], 16)
            sp.wait_ge(zero_ok, 1)
            sp.dma_start(odd_dram.rearrange("(p r) c -> p r c", r=B // 2),
                         zero[0:NTOK // (B // 2), :].unsqueeze(1).broadcast_to([NTOK // (B // 2), B // 2, D])).then_inc(odd_st, 16)
            sp.wait_ge(prob_ok, 2)
            sp.dma_start(table_dram.rearrange("(t p) c -> p t c", p=TOK), table[:, :, :]).then_inc(tab_st, 16)
            with sp.Fori(0, PAIRS // 2) as i:
                for q in range(2):
                    sp.wait_ge(stg_ok, 2 * i + q + 1)
                    sp.dma_start(out[bass.ds((2 * i + q) * PAIR, PAIR), :].rearrange("(j p) c -> p j c", p=TOK),
                                 stage[:, q, :, :]).then_inc(out_st[q], 16)
            sp.wait_ge(stg_ok, PAIRS)
            sp.dma_start(out[(PAIRS - 1) * PAIR:NTOK - S, :], stage[:, 0, 0, :]).then_inc(out_st[0], 16)
            sp.dma_start(out[NTOK - S:NTOK, :], stage[0:S, 0, 1, :]).then_inc(out_st[0], 16)
        @block.tensor
        def _(pe):
            def project(p):
                if pair(p) and pair(p - 1):
                    pe.wait_ge(taps, 3 * p)
                if pair(p):
                    for dst, c in ((XA, 256), (XB, 384)):
                        mm = pe.matmul(dst, w_in[:, c:c + 128], tile_of(uT, 2 * p, 2), start=True, stop=True)
                    mm.then_inc(x_mm, 1)
                    pe.matmul(BC, w_in[:, 512:640], tile_of(uT, 2 * p, 2), start=True, stop=True).then_inc(bc_mm, 1)

            def block_mm(i):
                if pair(i):
                    if pair(i - 1):
                        pe.wait_ge(gm_ok, i)
                    pe.wait_ge(dec_p, i + 1)
                    for j in range(2):
                        for hh in range(NH):
                            pe.matmul(SEG[j][:, hh * TOK:(hh + 1) * TOK],
                                      decay_p[:, j, hh:hh + 1].broadcast_to([TOK, TOK]), tri[:, :],
                                      start=(hh == 0), stop=False, skip_group_check=True)
                        mm = pe.matmul(SEG[j], ident16[0:TOK, 0:TOK],
                                       mask[:, :].unsqueeze(1).broadcast_to([TOK, NH, TOK]),
                                       start=False, stop=True, skip_group_check=True)
                    mm.then_inc(seg_mm, 1)
                    pe.wait_ge(bc_ok, i + 1)
                    for j in range(2):
                        mm = pe.matmul(G[j], bs[:, j * TOK:(j + 1) * TOK], cs[:, j * TOK:(j + 1) * TOK],
                                       start=True, stop=True)
                    mm.then_inc(g_mm, 1)
                if pair(i - 1):
                    pe.wait_ge(skip_ok, i)
                    pe.wait_ge(xrow_ok, i)
                    if pair(i - 2):
                        pe.wait_ge(yg_ok, i - 1)
                    for j in range(2):
                        for hh in range(NH):
                            mm = pe.matmul(Y[64 * (hh % 2):64 * (hh % 2) + 64, hh // 2, j * TOK:(j + 1) * TOK],
                                           xrow[:, j, hh * HD:(hh + 1) * HD], gm[:, j, hh, :], start=True, stop=True)
                    mm.then_inc(y_mm, 1)
                if pair(i):
                    pe.wait_ge(xs_ok, i + 1)
                    for j in range(2):
                        for c in range(2):
                            mm = pe.transpose(XR[:, j, c * 128:(c + 1) * 128], xs[:, c, j * TOK:(j + 1) * TOK],
                                              ident[:, :])
                    mm.then_inc(xtr_mm, 1)
                    if pair(i - 1):
                        pe.wait_ge(zs_ok, i)
                    for c in range(2):
                        mm = pe.matmul(Z[:, c * PAIR:(c + 1) * PAIR], w_in[:, c * 128:(c + 1) * 128],
                                       tile_of(uT, 2 * i, 2), start=True, stop=True)
                    mm.then_inc(z_mm, 1)
                if pair(i - 2):
                    yg_, ysum_ = (yg_last, ysum_last) if last(i - 2) else (yg, ysum)
                    pe.wait_ge(yg_ok, i - 1)
                    pe.wait_ge(ysq_ok, i - 1)
                    if pair(i - 3):
                        pe.wait_ge(o_sb, i - 2)
                    for j in range(2):
                        for c in range(2):
                            pe.matmul(O[:, j, 0:D], yg_[:, c, j * TOK:(j + 1) * TOK], w_out[:, c, :],
                                      start=(c == 0), stop=(c == 1))
                        mm = pe.matmul(O[:, j, D:D + 1], ysum_[:, j * TOK:(j + 1) * TOK], share[:, :],
                                       start=True, stop=True)
                    mm.then_inc(o_mm, 1)

            pe.wait_ge(ld["wtok"], 16)
            for t in range(T):
                if t in x_ld:
                    pe.wait_ge(x_ld[t], 16)
                for half in range(2):
                    mm = pe.matmul(ps_h(t), xT[:, half, t * TOK:(t + 1) * TOK], wtok[:, half * D:(half + 1) * D],
                                   start=(half == 0), stop=(half == 1))
                mm.then_inc(h_mm, 1)
            pe.wait_ge(ld["ident"], 16)

            def turn_tiles(t0, t1, src, even, odd, turned, alone=0):
                for t in range(t0, t1):
                    if t < alone:
                        pe.wait_ge(even, t + 1)
                    elif t % 2:
                        pe.wait_ge(odd, (t - alone) // 2 + 1)
                    else:
                        pe.wait_ge(even, alone + (t - alone) // 2 + 1)
                    pe.transpose(psf[:, t * 128:t * 128 + TOK], src[:, t, 0:D], ident[0:TOK, 0:TOK]).then_inc(turned, 1)

            for k, (t0, t1) in enumerate(NORM1):
                pe.wait_ge(h_sb, -(-t1 // 4))
                turn_tiles(t0, t1, u, u_ok, ua_ok, uT_mm)
                if k == 0:
                    pe.wait_ge(ld["w_in"], 16)
                    pe.wait_ge(uT_sb, 2)
                    project(0)
                for t in range(t0, t1):
                    pe.wait_ge(uT_sb, t // 4 + 1)
                    mm = pe.matmul(ps[0:TOK, 6, t * NH:(t + 1) * NH], tile_of(uT, t), w_in[:, 640:644],
                                   start=True, stop=True)
            mm.then_inc(dt_mm, 1)
            project(1)
            pe.wait_ge(ld["tri"], 16)
            pe.wait_ge(dec_ok, 1)
            pe.matmul(ps[0:TOK, 7, 0:T * NH], tri[:, :], decay, start=True, stop=True).then_inc(cum_mm, 1)
            pe.wait_ge(prep_v, 3)

            block_mm(0)
            for i in range(1, 3):
                project(i + 1)
                block_mm(i)
            with pe.Fori(3, PAIRS - 1) as i:
                project(i + 1)
                block_mm(i)
            block_mm(PAIRS - 1)
            block_mm(PAIRS)
            block_mm(PAIRS + 1)

            pe.wait_ge(ld["gate"], 16)
            pe.wait_ge(zs_ok, PAIRS)
            pe.wait_ge(yg_ok, PAIRS)
            turn_tiles(*NORM2[0], table, u2_ok, u2a_ok, u2T_mm, NORM2[0][1])
            for t in range(T):
                if t == 8:
                    turn_tiles(*NORM2[1], table, u2_ok, u2a_ok, u2T_mm, NORM2[0][1])
                if t == 14:
                    turn_tiles(*NORM2[2], table, u2_ok, u2a_ok, u2T_mm, NORM2[0][1])
                pe.wait_ge(u2T_sb, t // 4 + 1)
                mm = pe.matmul(ps[0:TOK, 6, t * E:(t + 1) * E], tile_of(uT, t), gate_w[:, :], start=True, stop=True)
            mm.then_inc(lg_mm, 1)
            pe.wait_ge(prob_ok, 1)
            for g in range(GROUPS):
                mm = pe.transpose(ps[:, 7, g * TOK:(g + 1) * TOK],
                                  prob[:, 8 * g:8 * g + 8, :].rearrange("p t e -> p (t e)"), ident[0:TOK, 0:TOK])
            mm.then_inc(pT_mm, 1)

            def l1(p, q, c0, c1):
                for c in range(c0, c1):
                    mm = pe.matmul(ps[:, 2 * q + c // 2, (c % 2) * PAIR:(c % 2 + 1) * PAIR],
                                   sw1[:, c * 128:(c + 1) * 128], tile_of(uT, 2 * p, 2), start=True, stop=True)
                return mm

            def l2(q, j):
                for c in range(HC):
                    mm = pe.matmul(ps[0:TOK, 4 + q, j * D:(j + 1) * D], hid[:, q, c, j * TOK:(j + 1) * TOK],
                                   sw2[:, c, :], start=(c == 0), stop=(c == HC - 1))
                return mm

            def count(n):
                pe.wait_ge(cmp_ok, n + 1)
                pe.matmul(ps[:, 7, 0:1], same16[:, :], cnt[:, :], start=True, stop=True).then_inc(cnt_mm, 1)

            pe.wait_ge(ld["sw1"], 16)
            pe.wait_ge(ld["sw2"], 16)
            pe.wait_ge(prep_p, 9)
            pe.wait_ge(pT_sb, 1)

            def part(i, q):
                p = 2 * i + q
                count(3 * p)
                l1(p, q, 0, 3)
                count(3 * p + 1)
                l1(p, q, 3, HC).then_inc(l1_mm, 1)
                if not isinstance(p, int) or p > 0:
                    pe.wait_ge(hid_ok, p)
                    if not isinstance(p, int) or p > 2:
                        pe.wait_ge(stg_ok, p - 2)
                    l2(1 - q, 0)
                count(3 * p + 2)
                if not isinstance(p, int) or p > 0:
                    l2(1 - q, 1).then_inc(l2_mm, 1)

            for i in range(2):
                for q in range(2):
                    part(i, q)
            with pe.Fori(2, PAIRS // 2) as i:
                part(i, 0)
                part(i, 1)
            l1(PAIRS - 1, 0, 0, HC).then_inc(l1_mm, 1)
            pe.wait_ge(hid_ok, PAIRS - 1)
            pe.wait_ge(stg_ok, PAIRS - 3)
            l2(1, 0)
            l2(1, 1).then_inc(l2_mm, 1)

            pe.wait_ge(tot_ok, 1)
            pe.matmul(ps[:, 7, 0:6], same_e, pre[:, :], start=True, stop=False)
            pe.matmul(ps[:, 7, 0:6], below, tot[:, :], start=False, stop=True).then_inc(off_mm, 1)
            pe.wait_ge(hid_ok, PAIRS)
            pe.wait_ge(stg_ok, PAIRS - 2)
            l2(0, 0)
            l2(0, 1).then_inc(l2_mm, 1)
            pe.wait_ge(pos_ok, 1)
            for g in range(GROUPS):
                mm = pe.transpose(ps[0:TOK, 6, g * 128:(g + 1) * 128], pos[:, g, :], ident[:, :])
            mm.then_inc(posT_mm, 1)
            for half in range(2):
                pe.wait_ge(hot_ok, half + 1)
                for t in range(T):
                    mm = pe.matmul(ps[0:8 * SLOTA, 2 + half, 0:8 * SLOTB],
                                   hotV[:, 8 * half:8 * half + 8, :, t].rearrange("p e n -> p (e n)"),
                                   hotB[:, 8 * half:8 * half + 8, :, t].rearrange("p e n -> p (e n)"),
                                   start=(t == 0), stop=(t == T - 1))
                mm.then_inc(lst_mm, 1)
            pe.wait_ge(dg_ok, 1)
            pe.matmul(ps[0:NL, 5, 32:32 + NL], sel16[0:8 * SLOTA, :], dgl[:, :], start=True, stop=True)
            pe.matmul(ps[0:NL, 5, 16:17], dgl[:, :], sel16[0:8 * SLOTA, 0:1], start=True, stop=True).then_inc(idx_mm, 1)
            for b in range(SLOTB):
                mm = pe.matmul(ps[:, 4, 2 * D:2 * D + E], slide16[0:8 * SLOTA, SLOTB - b:SLOTB - b + MAIN],
                               dg[:, :, :, b].rearrange("p k e -> p (k e)"), start=(b == 0), stop=(b == SLOTB - 1))
            mm.then_inc(idx_mm, 1)

            pe.wait_ge(ld["w1"], 16)
            pe.wait_ge(ld["w2"], 16)
            pe.wait_ge(got_ld[E], 16)
            pe.transpose(ps[:, 7, 0:NL], got[0:NL, E, 0:D], ident[0:NL, 0:NL]).then_inc(xe_mm, 1)

            def first(e):
                pe.wait_ge(got_ld[e], 16)
                if e:
                    pe.wait_ge(xe_sb, e)
                pe.transpose(ps[:, 6 + e % 2, 128 + 0:256], got[:, e, 0:D], ident[:, :]).then_inc(xe_mm, 1)

            def layer1(e):
                pe.wait_ge(xe_sb, e + 2)
                if e >= 2:
                    pe.wait_ge(e1_ok, e - 1)
                b = 2 * (e % 2)
                for c in range(HC):
                    mm = pe.matmul(ps[:, b + c // 2, (c % 2) * CAP:(c % 2 + 1) * CAP], w1[:, e, c * 128:(c + 1) * 128],
                                   xe[:, e, :], start=True, stop=True)
                mm.then_inc(e1_mm, 1)

            def layer2(e):
                pe.wait_ge(e1_ok, e + 1)
                if e >= 2:
                    pe.wait_ge(ys_ok, e - 1)
                for c in range(HC):
                    mm = pe.matmul(ps[:, 4 + e % 2, 0:CAP], w2[:, e, c * D:(c + 1) * D], hid[:, e % 2, c, 0:CAP],
                                   start=(c == 0), stop=(c == HC - 1))
                mm.then_inc(e2_mm, 1)

            def turn(e):
                pe.wait_ge(ye_ok, e + 1)
                if e >= 2:
                    pe.wait_ge(ys_ok, e - 1)
                pe.transpose(ps[:, 4 + e % 2, 256:384], ye[:, e, 0:MAIN], ident[:, :]).then_inc(yt_mm, 1)

            first(0)
            for e in range(E):
                if e + 1 < E:
                    first(e + 1)
                layer1(e)
                if e:
                    layer2(e - 1)
                if e >= 2:
                    turn(e - 2)
            layer2(E - 1)
            turn(E - 2)
            turn(E - 1)
            pe.wait_ge(yel_ok, 1)
            pe.transpose(ps[0:NL, 6, 0:D], yel[:, :], ident[:, :]).then_inc(yt_mm, 1)
            pe.wait_ge(dup_ok, 1)
            pe.wait_ge(left_ok, 1)
            pe.matmul(ps[0:NL, 6, 256:256 + D], eqm[:, :], yl[:, 0, :], start=True, stop=True).then_inc(left_mm, 1)

        @block.scalar
        def _(act):
            def last_tap(p):
                if pair(p):
                    act.wait_ge(x_mm, p + 1)
                    if pair(p - 1):
                        act.wait_ge(xs_ok, p)
                    for c in range(2):
                        tp = act.activation(conv[:, c, :], ps[:, 0, c * PAIR:(c + 1) * PAIR], ACT.Identity,
                                            scale=conv_w[:, 4 * c + 3:4 * c + 4], bias=conv_b[:, c:c + 1])
                    tp.then_inc(tap0_ok, 1)
                    act.wait_ge(bc_mm, p + 1)
                    act.activation(conv[:, 2, :], BC, ACT.Identity, scale=conv_w[:, 11:12], bias=conv_b[:, 2:3])\
                       .then_inc(tap0_ok, 1)

            def half_tanh(p):
                if pair(p):
                    act.wait_ge(taps, 3 * p + 3)
                    act.activation(tanhb[:, :], conv[:, 2, :], ACT.Tanh, scale=0.5).then_inc(tanh_b, 1)
                    act.activation(tanh3[:, 0:2, :], conv[:, 0:2, :], ACT.Tanh, scale=0.5).then_inc(tanh_x, 1)

            def block_act(i):
                if pair(i):
                    act.wait_ge(g_mm, i + 1)
                    for j in range(2):
                        for hh in range(NH):
                            ex_ = act.activation(lmask[:, j, hh, :], SEG[j][:, hh * TOK:(hh + 1) * TOK], ACT.Exp,
                                                 bias=bias_s[:, bass.ds((2 * i + j) * NH + hh, 1)])
                    ex_.then_inc(exp_ok, 1)
                    act.wait_ge(xtr_mm, i + 1)
                    if pair(i - 1):
                        act.wait_ge(y_mm, i)
                    act.activation(xrow[:, :, :], XR, ACT.Copy).then_inc(xrow_ok, 1)
                    act.wait_ge(z_mm, i + 1)
                    act.activation(tanhz[:, :, :].rearrange("p c n -> p (c n)"), Z, ACT.Tanh, scale=0.5).then_inc(tanh_z, 1)
                half_tanh(i + 1)
                if pair(i - 2):
                    act.wait_ge(o_mm, i - 1)
                    act.activation(o[:, bass.ds(2 * (i - 2), 2), :], O, ACT.Copy).then_inc(o_sb, 1)

            act.wait_ge(p_step, 1)
            act.activation(tanhz[0:TOK, 0, 0:T], half_neg[:, :], ACT.Exp).then_inc(a_step, 1)

            def keep_h(g):
                n = min(4, T - 4 * g)
                act.wait_ge(h_mm, 4 * g + n)
                act.activation(h[:, 4 * g:4 * g + n, :].rearrange("p t c -> p (t c)"), ps_h(4 * g, n), ACT.Copy)\
                   .then_inc(h_sb, 1)

            def normalise(t0, t1, src, dst, ok):
                for t in range(t0 + 1, t1, 2):
                    act.activation(dst[:, t, 0:D], src[:, t, :], ACT.Identity, scale=rstd[:, t:t + 1],
                                   bias=shift[:, t:t + 1]).then_inc(ok, 1)

            def keep_turned(g, turned, kept):
                n = min(4, T - 4 * g)
                act.wait_ge(turned, 4 * g + n)
                act.activation(tile_of(uT, 4 * g, n).rearrange("p (t c) -> p t c", t=n),
                               psf[:, g * 512:g * 512 + n * 128].rearrange("p (t c) -> p t c", t=n)[:, :, 0:TOK],
                               ACT.Copy).then_inc(kept, 1)

            for g in range(4):
                keep_h(g)
            act.wait_ge(shift_ok, 1)
            normalise(*NORM1[0], h, u, ua_ok)
            for g in range(4, BANKS):
                keep_h(g)
            for g in range(2):
                keep_turned(g, uT_mm, uT_sb)
            act.wait_ge(shift_ok, 2)
            normalise(*NORM1[1], h, u, ua_ok)
            act.wait_ge(ld["cols"], 16)
            last_tap(0)
            for g in range(2, 4):
                keep_turned(g, uT_mm, uT_sb)
            act.wait_ge(shift_ok, 3)
            normalise(*NORM1[2], h, u, ua_ok)
            for g in range(4, BANKS):
                keep_turned(g, uT_mm, uT_sb)
            half_tanh(0)
            act.wait_ge(ld["rows"], 16)
            act.activation(exp_a[:, :], a_log, ACT.Exp).then_inc(exp_a_ok, 1)
            act.wait_ge(dtx_ok, 1)
            act.activation(dt_abs, dt_x, ACT.Abs).then_inc(a_step, 1)
            act.wait_ge(a_step, 2)
            act.activation(dt_exp, dt_abs, ACT.Exp, scale=-1.0).then_inc(a_step, 1)
            act.wait_ge(a_step, 3)
            act.activation(dt_log, dt_exp, ACT.Ln, bias=1.0).then_inc(log_ok, 1)
            last_tap(1)
            act.wait_ge(dtc_ok, 1)
            act.activation(ln_dt, dt_c, ACT.Ln).then_inc(ln_ok, 1)
            act.activation(tanhz[:, 0, 0:1], ident[:, 0:1], ACT.Tanh).then_inc(a_step, 1)
            act.wait_ge(a_step, 4)
            act.wait_ge(cum_ok, 1)
            block_act(0)
            for i in range(1, 3):
                last_tap(i + 1)
                block_act(i)
            with act.Fori(3, PAIRS - 1) as i:
                last_tap(i + 1)
                block_act(i)
            block_act(PAIRS - 1)
            block_act(PAIRS)
            block_act(PAIRS + 1)
            for k, (t0, t1) in enumerate(NORM2):
                if k:
                    act.wait_ge(shift_ok, 3 + k)
                    normalise(t0, t1, h, table, u2a_ok)
                for g in range(t0 // 4, BANKS if t1 == T else t1 // 4):
                    keep_turned(g, u2T_mm, u2T_sb)
            act.wait_ge(sm_v, 1)
            act.activation(ex[:, :, :], prob[:, 0:T, :], ACT.Exp).then_inc(sm_a, 1)

            act.wait_ge(ld["biases"], 16)

            def gelu(p, q):
                act.wait_ge(l1_mm, p + 1)
                for c in range(HC):
                    g_ = act.activation(hid[:, q, c, :], ps[:, 2 * q + c // 2, (c % 2) * PAIR:(c % 2 + 1) * PAIR],
                                        ACT.Gelu_apprx_tanh, bias=sb1[:, c:c + 1])
                g_.then_inc(hid_ok, 1)
            act.wait_ge(pT_mm, 1)
            act.activation(pse[:, :, :].rearrange("p g n -> p (g n)"), ps[:, 7, 0:GROUPS * TOK], ACT.Copy).then_inc(pT_sb, 1)
            act.activation(hid[:, 0, 0, 0:1], ident[:, 0:1], ACT.Gelu_apprx_tanh).then_inc(a_step, 1)
            act.wait_ge(a_step, 5)
            with act.Fori(0, PAIRS // 2) as i:
                for q in range(2):
                    gelu(2 * i + q, q)
            gelu(PAIRS - 1, 0)

            act.wait_ge(l2_mm, PAIRS)
            for e in range(E):
                act.wait_ge(e1_mm, e + 1)
                if e >= 2:
                    act.wait_ge(e2_mm, e - 1)
                b = 2 * (e % 2)
                for c in range(HC):
                    g_ = act.activation(hid[:, e % 2, c, 0:CAP], ps[:, b + c // 2, (c % 2) * CAP:(c % 2 + 1) * CAP],
                                        ACT.Gelu_apprx_tanh, bias=b1[:, e * HC + c:e * HC + c + 1])
                g_.then_inc(e1_ok, 1)

        @block.gpsimd
        def _(pool):
            pool.memset(half_neg[:, :], -0.5).then_inc(p_step, 1)
            pool.memset(zero[:, :], 0.0).then_inc(zero_ok, 1)
            pool.memset(ones[:, :], 1.0).then_inc(prep_p, 1)
            pool.memset(share[:, :], 1.0 / DIN).then_inc(prep_p, 1)
            pool.memset(eps16[:, :], 16 * EPS).then_inc(prep_p, 1)
            pool.memset(prob[:, :, :], -1.0).then_inc(prep_p, 1)
            pool.wait_ge(p_step, 1)

            def root(k, t0, t1):
                pool.wait_ge(var_ok, k)
                pool.tensor_tensor(rstd[:, t0:t1], s_var[:, t0:t1], half_neg[:, t0:t1], ALU.pow).then_inc(pow_ok, 1)

            pool.wait_ge(ld["ident"], 16)
            pool.tensor_copy(ident16[:, :], ident[:, :]).then_inc(prep_v, 1)
            root(1, *NORM1[0])
            pool.wait_ge(ld["mask"], 16)
            pool.tensor_copy(mask[:, :], mask32[:, :]).then_inc(prep_v, 1)
            root(2, *NORM1[1])
            root(3, *NORM1[2])
            pool.wait_ge(ld["cols"], 16)
            pool.wait_ge(ld["w_out"], 16)
            for c in range(2):
                wo = pool.tensor_scalar(w_out[:, c, :], w_out_raw[:, c, :], norm_w[:, c:c + 1], None, ALU.mult)
            wo.then_inc(prep_v, 1)
            pool.wait_ge(ld["rows"], 16)
            pool.tensor_tensor(d_eye[:, :, :], ident[0:TOK, 0:TOK].unsqueeze(1).broadcast_to([TOK, NH, TOK]),
                               d_row.unsqueeze(2).broadcast_to([TOK, NH, TOK]), ALU.mult).then_inc(p_step, 1)
            pool.wait_ge(p_step, 2)
            pool.wait_ge(dec_ok, 1)

            def pair_decay(i):
                pool.tensor_copy(decay_p[:, :, :].rearrange("p j h -> p (j h)"), decay[:, bass.ds(2 * NH * i, 2 * NH)])\
                    .then_inc(dec_p, 1)
            pair_decay(0)
            def block_pool(i):
                if pair(i + 1) and pair(i):
                    pool.wait_ge(seg_mm, i + 1)
                    pair_decay(i + 1)
                if pair(i):
                    pool.wait_ge(gm_ok, i + 1)
                    for j in range(2):
                        sk = pool.tensor_tensor(gm[:, j, :, :], gm[:, j, :, :], d_eye[:, :, :], ALU.add)
                    sk.then_inc(skip_ok, 1)
                if pair(i - 2):
                    if isinstance(i, int) and i == 2:
                        pool.wait_ge(prep_p, 3)
                    pool.wait_ge(o_sb, i - 1)
                    ms, rs = (rms[:, k, bass.ds(2 * (i - 2), 2)] for k in range(2))
                    pool.tensor_tensor(ms, o[:, bass.ds(2 * (i - 2), 2), D], eps16[:, :], ALU.add)\
                        .then_inc(ms_ok, 1)
                    pool.wait_ge(ms_ok, i - 1)
                    pool.tensor_tensor(rs, ms, half_neg[:, 0:2], ALU.pow).then_inc(rms_ok, 1)
                if pair(i - 1) and not last(i - 1):
                    pool.wait_ge(yg_ok, i)
                    pool.tensor_tensor(ysq[:, :, :], yg[:, :, :], yg[:, :, :], ALU.mult).then_inc(sq_p, 1)
                    pool.wait_ge(sq_p, i)
                    pool.tensor_tensor(ysum[:, :], ysq[:, 0, :], ysq[:, 1, :], ALU.add).then_inc(ysq_ok, 1)

            for i in range(3):
                block_pool(i)
            with pool.Fori(3, PAIRS - 1) as i:
                block_pool(i)
            block_pool(PAIRS - 1)
            root(4, *NORM2[0])
            block_pool(PAIRS)
            root(5, *NORM2[1])
            block_pool(PAIRS + 1)
            root(6, *NORM2[2])
            pool.wait_ge(ld["consts"], 16)
            pool.tensor_copy(same16[:, :], same_e).then_inc(prep_p, 1)
            pool.tensor_copy(value16[:, :], value[0:TOK, :]).then_inc(prep_p, 1)
            pool.tensor_copy(iota_t[:, :, :], iota16[0:TOK, :].unsqueeze(2).broadcast_to([TOK, SLOTB, T])).then_inc(prep_p, 1)
            pool.tensor_copy(slide16[:, :], slide).then_inc(prep_p, 1)
            pool.tensor_copy(sel16[:, :], last_a.broadcast_to([128, NL])).then_inc(prep_p, 1)
            pool.wait_ge(u2_ok, (NORM2[0][1] + T) // 2)
            pool.wait_ge(u2a_ok, (T - NORM2[0][1]) // 2)
            pool.wait_ge(ld["sb2"], 16)
            pool.tensor_tensor(h[:, :, :], h[:, :, :], sb2[:, :].unsqueeze(1).broadcast_to([TOK, T, D]), ALU.add)\
                .then_inc(hb_ok, 1)
            pool.wait_ge(tab_st, 16)
            pool.wait_ge(idx_ok, 1)
            pool.indirect_dma_start(got[0:NL, E, :], None, table_dram, bass.IndirectOffsetOnAxis(idx_l[:, 0:1], 0))\
                .then_inc(got_ld[E], 16)
            pool.wait_ge(idx_ok, 2)

            def fetch(e):
                pool.indirect_dma_start(got[:, e, :], None, table_dram, bass.IndirectOffsetOnAxis(idx[:, e:e + 1], 0))\
                    .then_inc(got_ld[e], 16)
            for e in range(AHEAD):
                fetch(e)
            pool.wait_ge(out_st[0], 16 * (PAIRS // 2 + 2))
            pool.wait_ge(out_st[1], 16 * (PAIRS // 2))
            pool.wait_ge(odd_st, 16)
            for e in range(E):
                pool.wait_ge(ys_ok, e + 1)
                if e >= 2:
                    pool.wait_ge(added[e % 2], 16 * (e // 2))
                pool.indirect_dma_start(odd_dram if e % 2 else out, bass.IndirectOffsetOnAxis(idx[:, e:e + 1], 0),
                                        ys[:, e % 4, :], None, compute_op=ALU.add).then_inc(added[e % 2], 16)
                if e + AHEAD < E:
                    fetch(e + AHEAD)
            pool.wait_ge(left_ok, 2)
            pool.wait_ge(added[0], 16 * (E // 2))
            pool.indirect_dma_start(out, bass.IndirectOffsetOnAxis(idx_s[:, 0:1], 0), yl[:, 1, :], None,
                                    compute_op=ALU.add).then_inc(added[0], 16)
            pool.wait_ge(added[0], 16 * (E // 2 + 1))
            pool.wait_ge(added[1], 16 * (E // 2))
            eight = lambda ap: ap.rearrange("(p r) c -> p (r c)", r=8)
            pool.dma_start(eight(out[0:NTOK, :]), eight(odd_dram), accum_op=ALU.add, max_dma_last_dim=8 * D * 4).then_inc(joined, 16)
            pool.wait_ge(joined, 16)

        @block.vector
        def _(dve):
            done = [0]

            def chain(ins):
                done[0] += 1
                ins.then_inc(v_step, 1)
                dve.wait_ge(v_step, done[0])

            def earlier_taps(p):
                if pair(p):
                    for n in range(1, 4):
                        for c in range(3):
                            if n == 1:
                                dve.wait_ge(tap0_ok, 2 * p + 1 + (c == 2))
                            else:
                                dve.wait_ge(tap_v, 6 * p + 3 * (n - 2) + c + 1)
                            dst = conv[:, c, :].rearrange("p (s k) -> p s k", k=S)
                            src = (XA, XB, BC)[c].rearrange("p (s k) -> p s k", k=S)
                            dve.scalar_tensor_tensor(dst[:, :, n:S], src[:, :, 0:S - n],
                                                     conv_w[:, 4 * c + 3 - n:4 * c + 4 - n], dst[:, :, n:S],
                                                     ALU.mult, ALU.add).then_inc(tap_v if n < 3 else taps, 1)

            def gate_x(p):
                if pair(p):
                    dve.wait_ge(tanh_b, p + 1)
                    dve.scalar_tensor_tensor(bs[:, :], tanhb[0:NST, :], 1.0, conv[0:NST, 2, :], ALU.add, ALU.mult)
                    dve.scalar_tensor_tensor(cs[:, :], tanhb[NST:2 * NST, :], 1.0, conv[NST:2 * NST, 2, :], ALU.add, ALU.mult)\
                        .then_inc(bc_ok, 1)
                    dve.wait_ge(tanh_x, p + 1)
                    if pair(p - 1):
                        dve.wait_ge(xtr_mm, p)
                    dve.scalar_tensor_tensor(xs[:, :, :], tanh3[:, 0:2, :], 1.0, conv[:, 0:2, :], ALU.add, ALU.mult)\
                        .then_inc(xs_ok, 1)

            def block_dve(i):
                if pair(i):
                    dve.wait_ge(exp_ok, i + 1)
                    if pair(i - 1):
                        dve.wait_ge(y_mm, i)
                    for j in range(2):
                        g_ = dve.tensor_tensor(gm[:, j, :, :], lmask[:, j, :, :],
                                               G[j].unsqueeze(1).broadcast_to([TOK, NH, TOK]), ALU.mult)
                    g_.then_inc(gm_ok, 1)
                gate_x(i + 1)
                if pair(i - 1):
                    dve.wait_ge(y_mm, i)
                    dve.wait_ge(zs_ok, i)
                    if last(i - 1):
                        dve.tensor_tensor(yg_last[:, :, :], Y, zs[:, :, :], ALU.mult).then_inc(yg_ok, 1)
                        dve.wait_ge(yg_ok, PAIRS)
                        dve.wait_ge(ysq_ok, PAIRS - 1)
                        chain(dve.tensor_tensor(ysq[:, :, :], yg_last[:, :, :], yg_last[:, :, :], ALU.mult))
                        dve.tensor_tensor(ysum_last[:, :], ysq[:, 0, :], ysq[:, 1, :], ALU.add).then_inc(ysq_ok, 1)
                    else:
                        if pair(i - 2):
                            dve.wait_ge(o_mm, i - 1)
                        dve.tensor_tensor(yg[:, :, :], Y, zs[:, :, :], ALU.mult).then_inc(yg_ok, 1)
                if pair(i - 3):
                    dve.wait_ge(rms_ok, i - 2)
                    for j in range(2):
                        dve.scalar_tensor_tensor(h[:, 2 * (i - 3) + j, :], o[:, 2 * (i - 3) + j, 0:D],
                                                 rms[:, 1, bass.ds(2 * (i - 3) + j, 1)], h[:, 2 * (i - 3) + j, :],
                                                 ALU.mult, ALU.add).then_inc(h2_ok, 1)
                    for j in range(2):
                        dve.wait_ge(h2_ok, 2 * (i - 3) + j + 1)
                        dve.bn_stats(stats[:, 2 * (i - 3) + j, :], h[:, 2 * (i - 3) + j, :]).then_inc(st2_ok, 1)
                if pair(i):
                    dve.wait_ge(tanh_z, i + 1)
                    if pair(i - 1):
                        dve.wait_ge(yg_ok, i)
                    dve.scalar_tensor_tensor(zs[:, :, :].rearrange("p c n -> p (c n)"),
                                             tanhz[:, :, :].rearrange("p c n -> p (c n)"), 1.0, Z, ALU.add, ALU.mult)\
                        .then_inc(zs_ok, 1)

            def variance(t0, t1):
                me, qe, mo, qo = (stats[:, t0:t1, k] for k in (1, 2, 4, 5))
                m_, s_, d_, q_, v_ = (ap[:, t0:t1] for ap in (mean, s_sum, s_dif, s_sq, s_var))
                dve.tensor_tensor(d_, me, mo, ALU.subtract)
                dve.tensor_tensor(s_, me, mo, ALU.add)
                chain(dve.tensor_tensor(q_, qe, qo, ALU.add))
                dve.tensor_scalar(m_, s_, 0.5, None, ALU.mult)
                dve.tensor_scalar(q_, q_, 1.0 / D, EPS, ALU.mult, ALU.add)
                chain(dve.scalar_tensor_tensor(d_, d_, 0.25, d_, ALU.mult, ALU.mult))
                dve.tensor_tensor(v_, q_, d_, ALU.add).then_inc(var_ok, 1)

            def normalise(k, t0, t1, src, dst, ok, shared=True):
                dve.wait_ge(pow_ok, k)
                if shared:
                    dve.scalar_tensor_tensor(shift[:, t0:t1], mean[:, t0:t1], -1.0, rstd[:, t0:t1], ALU.mult, ALU.mult)\
                        .then_inc(shift_ok, 1)
                for t in range(t0, t1, 2 if shared else 1):
                    dve.tensor_scalar(dst[:, t, 0:D], src[:, t, :], mean[:, t:t + 1], rstd[:, t:t + 1],
                                      ALU.subtract, ALU.mult).then_inc(ok, 1)

            for k, (t0, t1) in enumerate(NORM1):
                for t in range(t0, t1):
                    dve.wait_ge(h_sb, t // 4 + 1)
                    dve.bn_stats(stats[:, t, :], h[:, t, :]).then_inc(st_a, 1)
                if k:
                    normalise(k, *NORM1[k - 1], h, u, u_ok)
                dve.wait_ge(st_a, t1)
                variance(t0, t1)
            normalise(3, *NORM1[2], h, u, u_ok)
            dve.wait_ge(ld["cols"], 16)
            earlier_taps(0)
            dve.wait_ge(dt_mm, 1)
            dve.wait_ge(ld["rows"], 16)
            per_tile = lambda ap: ap.unsqueeze(1).broadcast_to([TOK, T, NH])
            tiles = lambda ap: ap.rearrange("p (t h) -> p t h", h=NH)
            dve.tensor_tensor(tiles(dt_x), tiles(ps[0:TOK, 6, 0:T * NH]), per_tile(dt_bias), ALU.add).then_inc(dtx_ok, 1)
            gate_x(0)
            dve.wait_ge(ld["consts"], 16)
            dve.tensor_copy(bit_i[:, :], bitf)
            dve.wait_ge(dtx_ok, 1)
            dve.wait_ge(log_ok, 1)
            chain(dve.scalar_tensor_tensor(dt, dt_x, 0.0, dt_log, ALU.max, ALU.add))
            dve.wait_ge(exp_a_ok, 1)
            dve.scalar_tensor_tensor(tiles(decay), tiles(dt), -1.0, per_tile(exp_a[:, :]), ALU.mult, ALU.mult)\
                .then_inc(dec_ok, 1)
            dve.tensor_scalar(dt_c, dt, 1e-19, 0.25, ALU.max, ALU.mult).then_inc(dtc_ok, 1)

            earlier_taps(1)
            dve.wait_ge(cum_mm, 1)
            dve.wait_ge(ln_ok, 1)
            dve.tensor_tensor(bias_s, ln_dt, ps[0:TOK, 7, 0:T * NH], ALU.subtract).then_inc(cum_ok, 1)
            block_dve(0)
            for i in range(1, 3):
                earlier_taps(i + 1)
                block_dve(i)
            with dve.Fori(3, PAIRS - 1) as i:
                earlier_taps(i + 1)
                block_dve(i)
            block_dve(PAIRS - 1)
            dve.wait_ge(st2_ok, NORM2[0][1])
            variance(*NORM2[0])
            block_dve(PAIRS)
            normalise(4, *NORM2[0], h, table, u2_ok, shared=False)
            for k in (1, 2):
                block_dve(PAIRS + k)
                dve.wait_ge(st2_ok, NORM2[k][1])
                variance(*NORM2[k])
                normalise(4 + k, *NORM2[k], h, table, u2_ok)
            dve.wait_ge(lg_mm, 1)
            dve.wait_ge(prep_p, 4)
            lg = ps[0:TOK, 6, 0:T * E].rearrange("p (t e) -> p t e", e=E)
            over_e = lambda ap: ap.unsqueeze(2).broadcast_to([TOK, T, E])
            chain(dve.tensor_reduce(mx[:, :], lg, AX.X, ALU.max))
            dve.tensor_tensor(prob[:, 0:T, :], lg, over_e(mx[:, :]), ALU.subtract).then_inc(sm_v, 1)
            dve.wait_ge(sm_a, 1)
            chain(dve.tensor_reduce(den[:, :], ex[:, :, :], AX.X, ALU.add))
            chain(dve.reciprocal(rden[:, :], den[:, :]))
            dve.wait_ge(sm_v, 1)
            chain(dve.tensor_tensor(prob[:, 0:T, :], ex[:, :, :], over_e(rden[:, :]), ALU.mult))
            dve.tensor_scalar(prob[:, T - 1, :], prob[:, T - 1, :], valid[0:TOK, :], invalid[0:TOK, :],
                              ALU.mult, ALU.add).then_inc(prob_ok, 1)
            chain(dve.tensor_copy(cand[:, :], bit_i[:, 0:1]))
            dve.tensor_tensor(table[:, :, D:ROW], ex[:, :, :], over_e(rden[:, :]), ALU.mult).then_inc(prob_ok, 1)

            dve.wait_ge(pT_sb, 1)
            thr = cand[:, :].bitcast(F32)

            def ask(n):
                dve.tensor_scalar(hits[:, :, :], pse[:, :, :], thr[:, 0:1], 0.0, ALU.is_ge, ALU.add,
                                  accum_out=cnt[:, :]).then_inc(cmp_ok, 1)
                dve.tensor_tensor(kept[:, :], cand[:, :], bit_i[:, bass.ds(n + 1, 1)], ALU.bitwise_xor).then_inc(srch_v, 1)

            def decide(n):
                dve.wait_ge(cnt_mm, n + 1)
                dve.tensor_scalar(drop[:, :], ps[:, 7, 0:1], CAP - 0.5, bitf[:, bass.ds(n, 1)], ALU.is_lt, ALU.mult)\
                    .then_inc(srch_v, 1)
                dve.wait_ge(srch_v, 3 * n + 2)
                dve.tensor_tensor(cand[:, :], kept[:, :], drop[:, :], ALU.bitwise_xor).then_inc(srch_v, 1)
                dve.wait_ge(srch_v, 3 * n + 3)

            def add_rows(i, q):
                p = 2 * i + q
                dve.wait_ge(l2_mm, p + 1)
                if not isinstance(i, int) or i > 0:
                    dve.wait_ge(out_st[q], 16 * i)
                dve.tensor_tensor(stage[:, q, :, :].rearrange("p j c -> p (j c)"), ps[0:TOK, 4 + q, 0:2 * D],
                                  h[:, bass.ds(2 * p, 2), :].rearrange("p j c -> p (j c)"), ALU.add).then_inc(stg_ok, 1)

            def part(i, q):
                for k in range(3):
                    ask(6 * i + 3 * q + k)
                    if k == 0 and (not isinstance(i, int) or i > 0):
                        add_rows(i - 1, q)
                    decide(6 * i + 3 * q + k)

            part(0, 0)
            part(0, 1)
            dve.wait_ge(hb_ok, 1)
            part(1, 0)
            part(1, 1)
            with dve.Fori(2, PAIRS // 2) as i:
                part(i, 0)
                part(i, 1)

            tau = thr
            dve.tensor_scalar(ge[:, :, :], pse[:, :, :], tau[:, 0:1], None, ALU.is_ge)
            chain(dve.tensor_scalar(m6[:, 1, :, :], pse[:, :, :], tau[:, 0:1], None, ALU.is_equal))
            chain(dve.tensor_tensor(m6[:, 0, :, :], ge[:, :, :], m6[:, 1, :, :], ALU.subtract))
            for k in range(2):
                for g in range(GROUPS):
                    sc_ = dve.tensor_tensor_scan(rank[:, k, g, :], ones[:, :], m6[:, k, g, :], 0.0, ALU.mult, ALU.add)
            chain(sc_)
            chain(dve.tensor_copy(tot[:, :], rank[:, :, :, TOK - 1].rearrange("p k g -> p (k g)")))
            chain(dve.tensor_tensor_scan(pre[:, :], ones[:, 0:6], tot[:, :], 0.0, ALU.mult, ALU.add))
            dve.tensor_tensor(pre[:, :], pre[:, :], tot[:, :], ALU.subtract).then_inc(tot_ok, 1)
            add_rows(PAIRS // 2 - 1, 0)
            dve.wait_ge(off_mm, 1)
            chain(dve.tensor_copy(off[:, :], ps[:, 7, 0:6]))
            for k in range(2):
                for g in range(GROUPS):
                    st_ = dve.scalar_tensor_tensor(rank[:, k, g, :], rank[:, k, g, :], off[:, 3 * k + g:3 * k + g + 1],
                                                   m6[:, k, g, :], ALU.add, ALU.mult)
            dve.tensor_scalar(ge[:, :, :], ge[:, :, :], -BIG, BIG - 1, ALU.mult, ALU.add)
            chain(st_)
            chain(dve.tensor_tensor(pos[:, :, :], rank[:, 0, :, :], rank[:, 1, :, :], ALU.add))
            dve.tensor_tensor(pos[:, :, :], pos[:, :, :], ge[:, :, :], ALU.add).then_inc(pos_ok, 1)
            dve.wait_ge(posT_mm, 1)
            by_e = lambda ap: ap.rearrange("p (t e) -> p e t", e=E)
            chain(dve.tensor_copy(pos_i[:, :, :], by_e(ps[0:TOK, 6, 0:T * E])))
            dve.tensor_scalar(pa_i[:, :, :], pos_i[:, :, :], 4, None, ALU.logical_shift_right)
            chain(dve.tensor_scalar(pb_i[:, :, :], pos_i[:, :, :], SLOTB - 1, None, ALU.bitwise_and))
            dve.tensor_copy(pa_h[:, :, :], pa_i[:, :, :])
            chain(dve.tensor_copy(pb_h[:, :, :], pb_i[:, :, :]))
            dve.wait_ge(prep_p, 9)
            for half in range(2):
                es = slice(8 * half, 8 * half + 8)
                hot = lambda ap, n: ap[:, es, :].unsqueeze(2).broadcast_to([TOK, 8, n, T])
                number = lambda n: iota_t[:, 0:n, :].unsqueeze(1).broadcast_to([TOK, 8, n, T])
                chain(dve.tensor_tensor(hotA[:, es, :, :], hot(pa_h, SLOTA), number(SLOTA), ALU.is_equal))
                dve.tensor_tensor(hotV[:, es, :, :].rearrange("p e n t -> p (e n) t"),
                                  hotA[:, es, :, :].rearrange("p e n t -> p (e n) t"),
                                  value16[:, :].unsqueeze(1).broadcast_to([TOK, 8 * SLOTA, T]), ALU.mult)
                dve.tensor_tensor(hotB[:, es, :, :], hot(pb_h, SLOTB), number(SLOTB), ALU.is_equal).then_inc(hot_ok, 1)
                if half == 0:
                    add_rows(PAIRS // 2 - 1, 1)
            for half in range(2):
                dve.wait_ge(lst_mm, half + 1)
                chain(dve.tensor_tensor(dg[:, half, :, :],
                                        ps[0:8 * SLOTA, 2 + half, 0:8 * SLOTB].rearrange("p (e b) -> p e b", e=8),
                                        diag[0:8 * SLOTA, :].unsqueeze(2).broadcast_to([8 * SLOTA, 8, SLOTB]),
                                        ALU.mult))
            dve.tensor_copy(dgl[:, :].rearrange("p (k e r) -> p k e r", k=2, e=8), dg[:, :, :, 0:LEFT]).then_inc(dg_ok, 1)
            dve.wait_ge(idx_mm, 1)
            dve.tensor_scalar(idx_l[:, :], ps[0:NL, 5, 16:17], float(VALUE0), None, ALU.add).then_inc(idx_ok, 1)
            dve.wait_ge(idx_mm, 2)
            dve.tensor_scalar(idx[:, :], ps[:, 4, 2 * D:2 * D + E], float(VALUE0), None, ALU.add).then_inc(idx_ok, 1)
            dve.tensor_scalar(idx_lf[:, :], ps[0:NL, 5, 16:17], float(VALUE0), None, ALU.add)
            chain(dve.tensor_scalar(idx_rowf[:, :], ps[0:NL, 5, 32:32 + NL], float(VALUE0), None, ALU.add))
            chain(dve.tensor_scalar(eqm[:, :], idx_rowf[:, :], idx_lf[:, 0:1], None, ALU.is_equal))
            chain(dve.tensor_tensor(eqe[:, :], eqm[:, :], earlier[0:NL, :], ALU.mult))
            chain(dve.tensor_reduce(dup[:, 0:1], eqe[:, :], AX.X, ALU.max))
            chain(dve.tensor_scalar(dup[:, 1:2], dummy[0:NL, :], idx_lf[:, 0:1], None, ALU.subtract))
            dve.scalar_tensor_tensor(idx_s[:, :], dup[:, 1:2], dup[:, 0:1], idx_lf[:, :], ALU.mult, ALU.add)\
                .then_inc(dup_ok, 1)
            add_rows(PAIRS // 2, 0)
            dve.wait_ge(xe_mm, 1)
            dve.tensor_copy(xe[:, :, MAIN:CAP], ps[:, 7, 0:NL].rearrange("p (e r) -> p e r", e=E)).then_inc(xe_sb, 1)

            def take(e):
                dve.wait_ge(xe_mm, e + 2)
                dve.tensor_copy(xe[:, e, 0:MAIN], ps[:, 6 + e % 2, 128:256]).then_inc(xe_sb, 1)

            def bias2(e):
                dve.wait_ge(e2_mm, e + 1)
                dve.tensor_scalar(ye[:, e, :], ps[:, 4 + e % 2, 0:CAP], b2[:, e:e + 1], None, ALU.add).then_inc(ye_ok, 1)

            def scale(e):
                dve.wait_ge(yt_mm, e + 1)
                if e >= 4:
                    dve.wait_ge(added[e % 2], 16 * (e // 2 - 1))
                dve.tensor_scalar(ys[:, e % 4, :], ps[:, 4 + e % 2, 256:384], got[:, e, D + e:D + e + 1], None,
                                  ALU.mult).then_inc(ys_ok, 1)
            take(0)
            for e in range(E):
                if e + 1 < E:
                    take(e + 1)
                if e:
                    bias2(e - 1)
                if e >= 2:
                    scale(e - 2)
            bias2(E - 1)
            dve.wait_ge(ye_ok, E)
            dve.tensor_copy(yel[:, :].rearrange("p (e r) -> p e r", e=E), ye[:, :, MAIN:CAP]).then_inc(yel_ok, 1)
            scale(E - 2)
            scale(E - 1)
            chain(dve.tensor_tensor(sc_l[:, 0:E], got[0:NL, E, D:ROW], own_e[0:NL, :], ALU.mult))
            chain(dve.tensor_reduce(sc_l[:, E:E + 1], sc_l[:, 0:E], AX.X, ALU.add))
            dve.wait_ge(yt_mm, E + 1)
            dve.tensor_scalar(yl[:, 0, :], ps[0:NL, 6, 0:D], sc_l[:, E:E + 1], None, ALU.mult).then_inc(left_ok, 1)
            dve.wait_ge(left_mm, 1)
            dve.tensor_copy(yl[:, 1, :], ps[0:NL, 6, 256:256 + D]).then_inc(left_ok, 1)
    return nc


def constants():
    n = np.arange(2 * HOP, dtype=np.float64) + 0.5
    mdct = np.sqrt(4.0 / HOP) * np.cos(np.outer(n + HOP / 2, np.pi / HOP * n[:HOP]))
    wtok = np.sin(np.pi * n / (2 * HOP))[:, None].astype(np.float32) * mdct.astype(np.float32)
    r = np.arange(TOK)
    seq = r[:, None] // S == r[None, :] // S
    tri = (seq & (r[:, None] <= r[None, :])).astype(np.float32)
    q = np.arange(128)
    same = (q[:, None] % E == q[None, :] % E)
    below = same & (q[:, None] // E < q[None, :] // E)
    ea, el = q // SLOTA, q // LEFT
    parts = [
        same, below,
        np.tile([2.0 ** (BITS - 1 - k) if k < BITS else 0.0 for k in range(32)], (128, 1)),
        np.tile(np.arange(16.0), (128, 1)),
        q[:, None] + TOK * np.arange(T)[None, :] - float(VALUE0),
        ea[:, None] == np.arange(8)[None, :],
        np.arange(NL)[None, :] < q[:, None],
        el[:, None] == np.arange(E)[None, :],
        (q < S)[:, None], (q < S)[:, None] - 1.0, (NTOK + q)[:, None],
        ((q % SLOTA == SLOTA - 1) & (q < 8 * SLOTA))[:, None],
        np.arange(SLOTB + MAIN)[None, :] == SLOTB + SLOTB * (q % SLOTA)[:, None]]
    return {
        "wtok": wtok.reshape(2, HOP, HOP).transpose(1, 0, 2).reshape(128, 2 * D),
        "tri": tri,
        "mask": np.where(tri > 0, 0.0, -1e30).astype(np.float32),
        "ident": np.eye(128, dtype=np.float32),
        "consts": np.concatenate([np.asarray(p, np.float32) for p in parts], axis=1),
    }


def layout(i):
    x = np.zeros((3 * T, NBLK * HOP), np.float32)
    x[:B, HOP:HOP + 4000] = i["x"]
    blocks = x.reshape(3 * T, NBLK, HOP)
    conv_w = i["L0_attn_conv_w"][:, 0, :].reshape(3, 128, 4).transpose(1, 0, 2).reshape(128, 12)
    cols = np.concatenate([
        i["L0_attn_norm_w"].reshape(2, 128).T, conv_w, i["L0_attn_conv_b"].reshape(3, 128).T], axis=1)
    return {
        "xT": np.stack([blocks[:, k:k + S].transpose(2, 0, 1).reshape(HOP, T * TOK) for k in range(2)], axis=1),
        "w_in": i["L0_attn_W_in"].T,
        "cols": cols,
        "rows": np.tile(np.concatenate([i["L0_attn_dt_bias"], i["L0_attn_A_log"], i["L0_attn_D"]]), (TOK, 1)),
        "w_out": i["L0_attn_W_out"].T.reshape(2, 128, D).transpose(1, 0, 2),
        "gate_w": i["L0_ffn_gate_w"],
        "sw1": i["L0_ffn_sw1"],
        "sw2": i["L0_ffn_sw2"].reshape(HC, 128, D).transpose(1, 0, 2),
        "sb2": np.tile(i["L0_ffn_sb2"], (TOK, 1)),
        "biases": np.concatenate([
            i["L0_ffn_sb1"].reshape(HC, 128).T, i["L0_ffn_b1"].reshape(E * HC, 128).T, i["L0_ffn_b2"].T], axis=1),
        "w1": i["L0_ffn_w1"].transpose(1, 0, 2),
        "w2": i["L0_ffn_w2"].reshape(E, HC, 128, D).transpose(2, 0, 1, 3).reshape(128, E, HC * D),
    }


def kernel(**inputs):
    import concourse.bacc as bacc
    from concourse.bass_utils import run_bass_kernel_spmd

    nc = bacc.Bacc("TRN2", target_bir_lowering=False, num_devices=1)
    arrays = layout({k: np.asarray(v) for k, v in inputs.items()}) | constants()
    arrays = {k: np.ascontiguousarray(v) for k, v in arrays.items()}
    aps = {k: nc.dram_tensor("in_" + k, v.shape, F32, kind="ExternalInput").ap() for k, v in arrays.items()}
    aps["out"] = nc.dram_tensor("out_rows", (NTOK + NL, D), F32, kind="ExternalOutput").ap()
    program(nc, aps)
    r = run_bass_kernel_spmd(nc, [{"in_" + k: v for k, v in arrays.items()}], core_ids=[0])
    return r.results[0]["out_rows"][:NTOK].reshape(B, S, D)
```

```python
from contextlib import ExitStack

import numpy as np

import concourse.bass as bass
from concourse import mybir

F32 = mybir.dt.float32
F16 = mybir.dt.float16
BF16 = mybir.dt.bfloat16
I32 = mybir.dt.int32
U32 = mybir.dt.uint32
ALU = mybir.AluOpType
ACT = mybir.ActivationFunctionType
AX = mybir.AxisListType

B, S = 64, 33
HOP = 128
NBLK = S + 1
TOK = 3 * S
T = -(-B // 3)
PAIRS = T // 2
BANKS = -(-T // 4)
PAIR = 2 * TOK
NTOK = B * S
D, DIN, NST, NH, HD = 128, 256, 64, 4, 64
E, HID, HC = 16, 512, 4
CAP = NTOK // E
EPS = 1e-5
MAIN = 128
LEFT = CAP - MAIN
NL = E * LEFT
SLOTB = 16
SLOTA = -(-CAP // SLOTB)
ROW = D + E
GROUPS = 3
BIG = 4096.0
VALUE0 = T * TOK // 2
XCUT = ((0, 2), (2, 6), (6, 12), (12, 17), (17, 22))
AHEAD = 8
NORM1 = ((0, 8), (8, 16), (16, T))
NORM2 = ((0, 14), (14, 20), (20, T))
DIGITS = 15
WORK = 7300
QUARTER = E // 4

def program(nc, a):
    ctx = ExitStack()
    with ctx:
        def sb(name, shape, dt=F32):
            return ctx.enter_context(nc.sbuf_tensor(name, shape, dt))

        def sem(name):
            return ctx.enter_context(nc.semaphore(name))

        xT = sb("xT", [128, 2, T * TOK])
        wtok = sb("wtok", [128, 2 * D])
        w_in = sb("w_in", [128, 644])
        w_out_raw = sb("w_out_raw", [128, 2, D])
        d_eye = sb("d_eye", [TOK, NH, TOK])
        w_out = sb("w_out", [128, 2, D])
        cols = sb("cols", [128, 17])
        norm_w, conv_w, conv_b = cols[:, 0:2], cols[:, 2:14], cols[:, 14:17]
        rows = sb("rows", [TOK, 12])
        dt_bias, a_log, d_row = rows[:, 0:NH], rows[:, NH:2 * NH], rows[:, 2 * NH:3 * NH]
        tri = sb("tri", [TOK, TOK])
        mask32 = sb("mask32", [TOK, TOK])
        mask = sb("mask", [TOK, TOK], BF16)
        ident = sb("ident", [128, 128])
        ident16 = sb("ident16", [128, 128], BF16)
        ones = sb("ones", [128, TOK])
        gate_w = sb("gate_w", [128, E])
        sw1 = sb("sw1", [128, HID])
        sw2 = sb("sw2", [128, HC, D])
        sb2 = sb("sb2", [TOK, D])
        biases = sb("biases", [128, HC + E * HC + E])
        sb1, b1, b2 = biases[:, 0:HC], biases[:, HC:HC + E * HC], biases[:, HC + E * HC:]
        w1 = sb("w1", [128, E, HID])
        w2 = sb("w2", [128, E, HC * D])
        consts = sb("consts", [128, 256 + 4 * (DIGITS + 1) + 16 + T + QUARTER + NL + E + 4 + SLOTB + MAIN])
        at = 0

        def const(n):
            nonlocal at
            at += n
            return consts[:, at - n:at]
        same_e = const(128)
        below = const(128)
        digits = const(4 * (DIGITS + 1))
        iota16 = const(16)
        value = const(T)
        diag = const(QUARTER)
        earlier = const(NL)
        own_e = const(E)
        valid = const(1)
        invalid = const(1)
        dummy = const(1)
        last_a = const(1)
        slide = const(SLOTB + MAIN)

        h = sb("h", [TOK, T, D])
        u = sb("u", [TOK, T, D])
        uT = sb("uT", [128, T * TOK])
        o = sb("o", [TOK, T, D + 1])
        table = sb("table", [TOK, T, ROW])
        stats = sb("stats", [TOK, T, 6])
        small = sb("small", [TOK, 8, T])
        mean, rstd, s_sum, s_dif, s_sq, s_var, shift = (small[:, n, :] for n in range(7))
        zero = sb("zero", [128, D])
        half_neg = sb("half_neg", [TOK, T])
        share = sb("share", [128, 1])
        eps16 = sb("eps16", [TOK, 2])
        dtw = sb("dtw", [TOK, 9, T * NH])
        dt_x, dt_abs, dt_exp, dt_log, dt, decay, bias_s, dt_c, ln_dt = (dtw[:, n, :] for n in range(9))
        rms = sb("rms", [TOK, 2, T])
        exp_a = sb("exp_a", [TOK, NH])
        ones3 = sb("ones3", [3, TOK], BF16)
        work = sb("work", [128, WORK])
        used = [0]

        def carve(p, *shape):
            n = int(np.prod(shape))
            used[0] += n
            assert used[0] <= WORK
            ap = work[0:p, used[0] - n:used[0]]
            names = "abcd"[:len(shape)]
            if len(shape) == 1:
                return ap
            return ap.rearrange(f"p ({' '.join(names)}) -> p {' '.join(names)}", **dict(zip(names[1:], shape[1:])))
        taps3 = carve(128, 3, PAIR)
        tap1 = carve(128, 3, PAIR)
        conv = carve(128, 3, PAIR)
        tanh3 = carve(128, 2, PAIR)
        tanhz = carve(128, 2, PAIR)
        xs = carve(128, 2, PAIR)
        bs = carve(NST, PAIR)
        cs = carve(NST, PAIR)
        tanhb = carve(128, PAIR)
        zs = carve(128, 2, PAIR)
        xrow = carve(TOK, 2, DIN)
        lmask = carve(TOK, 2, NH, TOK)
        gm = carve(TOK, 2, NH, TOK)
        yg = carve(128, 2, PAIR)
        ysq = carve(128, 2, PAIR)
        samples = xT[:, :, :].rearrange("p k n -> p (k n)")
        yg_last = samples[:, 0:2 * PAIR].rearrange("p (c n) -> p c n", c=2)
        cum_rows = samples[0:3, 2 * PAIR:2 * PAIR + (T - 2) * NH * TOK // 2].bitcast(BF16)
        ysq_last = carve(128, 2, PAIR)
        cum_r = ysq_last[0:T * NH, 0, :].rearrange("p (k n) -> p k n", k=2)
        cum_parts = ysq_last[0:T * NH, 1, :].bitcast(BF16)[:, 0:3 * TOK].rearrange("p (k n) -> p k n", k=3)
        used[0] = 0
        got = carve(128, E + 1, ROW)
        ys = carve(128, 4, D)
        yl = carve(NL, 2, D)
        hid = carve(128, 2, HC, PAIR)
        stage = carve(TOK, 2, 2, D)
        xe = xT[:, 0, 0:E * CAP].rearrange("p (e c) -> p e c", e=E)
        ye = uT[:, 0:E * CAP].rearrange("p (e c) -> p e c", e=E)
        mx = sb("mx", [TOK, T])
        den = sb("den", [TOK, T])
        rden = sb("rden", [TOK, T])
        ex = sb("ex", [TOK, T, E])
        prob = sb("prob", [TOK, 8 * GROUPS, E])
        pse = sb("pse", [128, GROUPS, TOK])
        hits = xT[:, 1, 0:2 * GROUPS * TOK].bitcast(F16)[:, 0:3 * GROUPS * TOK]\
            .rearrange("p (k g n) -> p k g n", k=3, g=GROUPS)
        cnt = sb("cnt", [128, 3], F16)
        met = sb("met", [128, 3])
        digit_i = sb("digit_i", [128, DIGITS + 1, 4], I32)
        cand = sb("cand", [128, 4], I32)
        settled = sb("settled", [128, 4], I32)
        digit = sb("digit", [128, 1])
        digit_bits = sb("digit_bits", [128, 1], I32)
        same16 = sb("same16", [128, 128], F16)
        m6 = sb("m6", [128, 2, GROUPS, TOK])
        ge = sb("ge", [128, GROUPS, TOK])
        rank = sb("rank", [128, 2, GROUPS, TOK])
        tot = sb("tot", [128, 6])
        pre = sb("pre", [128, 6])
        off = sb("off", [128, 6])
        pos = sb("pos", [128, GROUPS, TOK])
        pos_i = sb("pos_i", [TOK, E, T], I32)
        pa_i = sb("pa_i", [TOK, E, T], I32)
        pb_i = sb("pb_i", [TOK, E, T], I32)
        pa_h = sb("pa_h", [TOK, E, T], F16)
        pb_h = sb("pb_h", [TOK, E, T], F16)
        iota_t = sb("iota_t", [TOK, SLOTB, T], F16)
        value16 = sb("value16", [TOK, T], F16)
        slide16 = sb("slide16", [128, SLOTB + MAIN], F16)
        sel16 = sb("sel16", [128, NL], F16)
        hotV = o[:, :, :].rearrange("p t c -> p (t c)")[:, 0:T * E * SLOTA // 2].bitcast(F16)\
            .rearrange("p (e n t) -> p e n t", e=E, n=SLOTA)
        hotA = xT[0:TOK, 1, 0:T * E * SLOTA // 2].bitcast(F16).rearrange("p (e n t) -> p e n t", e=E, n=SLOTA)
        hotB = u[:, :, :].rearrange("p t c -> p (t c)").bitcast(F16).rearrange("p (e n t) -> p e n t", e=E, n=SLOTB)
        dg = sb("dg", [QUARTER * SLOTA, 4, QUARTER, SLOTB], F16)
        dgl = sb("dgl", [QUARTER * SLOTA, NL], F16)
        idx = sb("idx", [128, E], U32)
        idx_l = sb("idx_l", [NL, 1], U32)
        idx_lf = sb("idx_lf", [NL, 1])
        idx_rowf = sb("idx_rowf", [NL, NL])
        eqm = sb("eqm", [NL, NL])
        eqe = sb("eqe", [NL, NL])
        dup = sb("dup", [NL, 4])
        idx_s = sb("idx_s", [NL, 1], U32)
        sc_l = sb("sc_l", [NL, E + 1])

        yel = sb("yel", [128, NL])
        ps = ctx.enter_context(nc.psum_tensor("ps", [128, 8, 512], F32))
        psf = ps[:, :, :].rearrange("p b n -> p (b n)")

        x_ld = {c: sem(f"x_ld{c}") for c, _ in XCUT}
        ld = {n: sem("ld_" + n) for n in (
            "wtok", "w_in", "cols", "rows", "tri", "mask", "ident", "w_out", "gate", "sw1", "sw2",
            "sb2", "biases", "w1", "w2", "consts")}
        h_mm, h_sb, st_a = sem("h_mm"), sem("h_sb"), sem("st_a")
        var_ok, pow_ok, u_ok, uT_mm, uT_sb = sem("var_ok"), sem("pow_ok"), sem("u_ok"), sem("uT_mm"), sem("uT_sb")
        dt_mm, dtx_ok, log_ok, dec_ok, cum_mm, cum_ok = (sem(n) for n in (
            "dt_mm", "dtx_ok", "log_ok", "dec_ok", "cum_mm", "cum_ok"))
        v_step, a_step, p_step = sem("v_step"), sem("a_step"), sem("p_step")
        ua_ok, u2a_ok, shift_ok = sem("ua_ok"), sem("u2a_ok"), sem("shift_ok")
        prep_v, prep_p, exp_a_ok = sem("prep_v"), sem("prep_p"), sem("exp_a_ok")
        x_mm, bc_mm, z_mm, y_mm, xtr_mm, g_mm, o_mm = (sem(n) for n in (
            "x_mm", "bc_mm", "z_mm", "y_mm", "xtr_mm", "g_mm", "o_mm"))
        taps, tanh_b, tanh_z, tanh_x, exp_ok, xrow_ok, o_sb = (sem(n) for n in (
            "taps", "tanh_b", "tanh_z", "tanh_x", "exp_ok", "xrow_ok", "o_sb"))
        bc_ok, yg_ok, xs_ok, zs_ok, gm_ok, ysq_ok = (sem(n) for n in (
            "bc_ok", "yg_ok", "xs_ok", "zs_ok", "gm_ok", "ysq_ok"))
        parts_ok, cum_ld = sem("parts_ok"), sem("cum_ld")
        conv_ok, tap1_zero, ones3_ok = sem("conv_ok"), sem("tap1_zero"), sem("ones3_ok")
        tap_v, tap0_ok, ms_ok, rms_ok, skip_ok, dtc_ok, ln_ok = (sem(n) for n in (
            "tap_v", "tap0_ok", "ms_ok", "rms_ok", "skip_ok", "dtc_ok", "ln_ok"))
        h2_ok, st2_ok, u2_ok, u2T_mm, u2T_sb, hb_ok = (sem(n) for n in (
            "h2_ok", "st2_ok", "u2_ok", "u2T_mm", "u2T_sb", "hb_ok"))
        lg_mm, sm_v, sm_a, prob_ok, pT_mm, pT_sb, tab_st = (sem(n) for n in (
            "lg_mm", "sm_v", "sm_a", "prob_ok", "pT_mm", "pT_sb", "tab_st"))
        cmp_ok, cnt_mm, srch_v, l1_mm, hid_ok, l2_mm, stg_ok = (sem(n) for n in (
            "cmp_ok", "cnt_mm", "srch_v", "l1_mm", "hid_ok", "l2_mm", "stg_ok"))
        out_st = [sem("out_st0"), sem("out_st1")]
        tot_ok, off_mm, pos_ok, posT_mm, hot_ok, lst_mm = (sem(n) for n in (
            "tot_ok", "off_mm", "pos_ok", "posT_mm", "hot_ok", "lst_mm"))
        zero_ok, odd_st = sem("zero_ok"), sem("odd_st")
        added, joined = [sem("added0"), sem("added1")], sem("joined")
        hot_a = sem("hot_a")
        dg_ok, idx_mm, idx_ok = sem("dg_ok"), sem("idx_mm"), sem("idx_ok")
        got_ld = [sem(f"got_ld{n}") for n in range(E + 1)]
        xe_mm, xe_sb, e1_mm, e1_ok, e2_mm, ye_ok, yt_mm, ys_ok = (sem(n) for n in (
            "xe_mm", "xe_sb", "e1_mm", "e1_ok", "e2_mm", "ye_ok", "yt_mm", "ys_ok"))
        yel_ok, left_ok, left_mm, dup_ok = sem("yel_ok"), sem("left_ok"), sem("left_mm"), sem("dup_ok")

        table_dram = nc.dram_tensor("table_dram", (T * TOK, ROW), F32).ap()
        out = a["out"]
        odd_dram = nc.dram_tensor("odd_dram", (NTOK, D), F32).ap()

        block = ctx.enter_context(nc.Block())

        def tile_of(ap, t, n=1):
            return ap[:, bass.ds(t * TOK, n * TOK)]

        def by_seq(ap):
            return ap.rearrange("p (s k) -> p s k", k=S)

        def pair(i):
            return not isinstance(i, int) or 0 <= i < PAIRS

        def first_pair(i):
            return isinstance(i, int) and i == 0

        def last(i):
            return isinstance(i, int) and i == PAIRS - 1

        def ps_h(t, n=1):
            return psf[0:TOK, bass.ds(t * 128, n * 128)]
        XA, XB, BC = ps[:, 0, 0:PAIR], ps[:, 0, PAIR:2 * PAIR], ps[:, 1, 0:PAIR]
        Z = ps[:, 2, 0:2 * PAIR]
        SEG = [ps[0:TOK, 3 + j, 0:NH * TOK] for j in range(2)]
        G = [ps[0:TOK, 3 + j, NH * TOK:(NH + 1) * TOK] for j in range(2)]
        Y = ps[:, 5, 0:2 * PAIR].rearrange("p (c n) -> p c n", c=2)
        XR = ps[0:TOK, 6, :].rearrange("p (j c) -> p j c", j=2)
        O = ps[0:TOK, 7, 0:2 * (D + 1)].rearrange("p (j c) -> p j c", j=2)

        @block.sync
        def _(sp):
            for dst, name, key in (
                    (wtok[:, :], "wtok", "wtok"), *((xT[:, :, c * TOK:n * TOK], c, n) for c, n in XCUT), (w_in[:, :], "w_in", "w_in"),
                    (ident[:, :], "ident", "ident"), (rows[:, :], "rows", "rows"), (tri[:, :], "tri", "tri"),
                    (mask32[:, :], "mask", "mask"), (cols[:, :], "cols", "cols"),
                    (w_out_raw[:, :, :], "w_out", "w_out"), (gate_w[:, :], "gate_w", "gate"),
                    (consts[:, :], "consts", "consts"), (sw1[:, :], "sw1", "sw1"), (sw2[:, :, :], "sw2", "sw2"),
                    (sb2[:, :], "sb2", "sb2"), (biases[:, :], "biases", "biases"),
                    (w1[:, :, :], "w1", "w1"), (w2[:, :, :], "w2", "w2")):
                if isinstance(name, int):
                    sp.dma_start(dst, a["xT"][:, :, name * TOK:key * TOK]).then_inc(x_ld[name], 16)
                    continue
                sp.dma_start(dst, a[name]).then_inc(ld[key], 16)
            sp.wait_ge(parts_ok, 1)
            for k in range(3):
                sp.dma_start(cum_rows[k:k + 1, :], cum_parts[2 * NH:T * NH, k, :]).then_inc(cum_ld, 16)
            sp.wait_ge(zero_ok, 1)
            sp.dma_start(odd_dram.rearrange("(p r) c -> p r c", r=B // 2),
                         zero[0:NTOK // (B // 2), :].unsqueeze(1).broadcast_to([NTOK // (B // 2), B // 2, D])).then_inc(odd_st, 16)
            sp.wait_ge(prob_ok, 2)
            sp.dma_start(table_dram.rearrange("(t p) c -> p t c", p=TOK), table[:, :, :]).then_inc(tab_st, 16)
            with sp.Fori(0, PAIRS // 2) as i:
                for q in range(2):
                    sp.wait_ge(stg_ok, 2 * i + q + 1)
                    sp.dma_start(out[bass.ds((2 * i + q) * PAIR, PAIR), :].rearrange("(j p) c -> p j c", p=TOK),
                                 stage[:, q, :, :]).then_inc(out_st[q], 16)
            sp.wait_ge(stg_ok, PAIRS)
            sp.dma_start(out[(PAIRS - 1) * PAIR:NTOK - S, :], stage[:, 0, 0, :]).then_inc(out_st[0], 16)
            sp.dma_start(out[NTOK - S:NTOK, :], stage[0:S, 0, 1, :]).then_inc(out_st[0], 16)
        @block.tensor
        def _(pe):
            def project(p):
                if pair(p) and pair(p - 1):
                    pe.wait_ge(taps, 3 * p)
                if pair(p):
                    pe.matmul(BC, w_in[:, 512:640], tile_of(uT, 2 * p, 2), start=True, stop=True).then_inc(bc_mm, 1)
                    for dst, c in ((XA, 256), (XB, 384)):
                        mm = pe.matmul(dst, w_in[:, c:c + 128], tile_of(uT, 2 * p, 2), start=True, stop=True)
                    mm.then_inc(x_mm, 1)

            def block_mm(i):
                if not first_pair(i):
                    project(i + 1)
                if pair(i):
                    if pair(i - 1):
                        pe.wait_ge(gm_ok, i)
                    if isinstance(i, int) and i == 1:
                        pe.wait_ge(cum_ld, 16 * 3)
                        pe.wait_ge(ones3_ok, 1)
                    for j in range(2):
                        if first_pair(i):
                            for hh in range(NH):
                                pe.matmul(SEG[j][:, hh * TOK:(hh + 1) * TOK],
                                          decay[:, j * NH + hh:j * NH + hh + 1].broadcast_to([TOK, TOK]), tri[:, :],
                                          start=(hh == 0), stop=False, skip_group_check=True)
                        else:
                            pe.matmul(SEG[j], ones3[:, :], cum_rows[:, bass.ds((2 * (i - 1) + j) * NH * TOK, NH * TOK)],
                                      start=True, stop=False, skip_group_check=True)
                        pe.matmul(SEG[j], ident16[0:TOK, 0:TOK],
                                  mask[:, :].unsqueeze(1).broadcast_to([TOK, NH, TOK]),
                                  start=False, stop=True, skip_group_check=True)
                if pair(i):
                    pe.wait_ge(bc_ok, i + 1)
                    for j in range(2):
                        mm = pe.matmul(G[j], bs[:, j * TOK:(j + 1) * TOK], cs[:, j * TOK:(j + 1) * TOK],
                                       start=True, stop=True)
                    mm.then_inc(g_mm, 1)
                if pair(i - 2):
                    yg_, ysq_ = (yg_last, ysq_last) if last(i - 2) else (yg, ysq)
                    pe.wait_ge(yg_ok, i - 1)
                    pe.wait_ge(ysq_ok, i - 1)
                    if pair(i - 3):
                        pe.wait_ge(o_sb, i - 2)
                    for j in range(2):
                        for c in range(2):
                            pe.matmul(O[:, j, 0:D], yg_[:, c, j * TOK:(j + 1) * TOK], w_out[:, c, :],
                                      start=(c == 0), stop=(c == 1))
                        for c in range(2):
                            mm = pe.matmul(O[:, j, D:D + 1], ysq_[:, c, j * TOK:(j + 1) * TOK], share[:, :],
                                           start=(c == 0), stop=(c == 1))
                    mm.then_inc(o_mm, 1)
                if pair(i - 1):
                    pe.wait_ge(skip_ok, i)
                    pe.wait_ge(xrow_ok, i)
                    if pair(i - 2):
                        pe.wait_ge(yg_ok, i - 1)
                    for j in range(2):
                        for hh in range(NH):
                            mm = pe.matmul(Y[64 * (hh % 2):64 * (hh % 2) + 64, hh // 2, j * TOK:(j + 1) * TOK],
                                           xrow[:, j, hh * HD:(hh + 1) * HD], gm[:, j, hh, :], start=True, stop=True)
                    mm.then_inc(y_mm, 1)
                if pair(i):
                    pe.wait_ge(xs_ok, i + 1)
                    for j in range(2):
                        for c in range(2):
                            mm = pe.transpose(XR[:, j, c * 128:(c + 1) * 128], xs[:, c, j * TOK:(j + 1) * TOK],
                                              ident[:, :])
                    mm.then_inc(xtr_mm, 1)
                if pair(i):
                    if pair(i - 1):
                        pe.wait_ge(zs_ok, i)
                    for c in range(2):
                        mm = pe.matmul(Z[:, c * PAIR:(c + 1) * PAIR], w_in[:, c * 128:(c + 1) * 128],
                                       tile_of(uT, 2 * i, 2), start=True, stop=True)
                    mm.then_inc(z_mm, 1)

            pe.wait_ge(ld["wtok"], 16)
            for t in range(T):
                if t in x_ld:
                    pe.wait_ge(x_ld[t], 16)
                for half in range(2):
                    mm = pe.matmul(ps_h(t), xT[:, half, t * TOK:(t + 1) * TOK], wtok[:, half * D:(half + 1) * D],
                                   start=(half == 0), stop=(half == 1))
                mm.then_inc(h_mm, 1)
            pe.wait_ge(ld["ident"], 16)

            def turn_tiles(t0, t1, src, even, odd, turned, alone=0):
                for t in range(t0, t1):
                    if t < alone:
                        pe.wait_ge(even, t + 1)
                    elif t % 2:
                        pe.wait_ge(odd, (t - alone) // 2 + 1)
                    else:
                        pe.wait_ge(even, alone + (t - alone) // 2 + 1)
                    pe.transpose(psf[:, t * 128:t * 128 + TOK], src[:, t, 0:D], ident[0:TOK, 0:TOK]).then_inc(turned, 1)

            for k, (t0, t1) in enumerate(NORM1):
                pe.wait_ge(h_sb, -(-t1 // 4))
                turn_tiles(t0, t1, u, u_ok, ua_ok, uT_mm)
                if k == 0:
                    pe.wait_ge(ld["w_in"], 16)
                    pe.wait_ge(uT_sb, 2)
                    project(0)
                for t in range(t0, t1):
                    pe.wait_ge(uT_sb, t // 4 + 1)
                    mm = pe.matmul(ps[0:TOK, 6, t * NH:(t + 1) * NH], tile_of(uT, t), w_in[:, 640:644],
                                   start=True, stop=True)
            mm.then_inc(dt_mm, 1)
            project(1)
            pe.wait_ge(ld["tri"], 16)
            pe.wait_ge(dec_ok, 1)
            pe.matmul(ps[0:TOK, 7, 0:T * NH], tri[:, :], decay, start=True, stop=True)
            pe.matmul(ps[0:T * NH, 7, 128:128 + TOK], decay, tri[:, :], start=True, stop=True).then_inc(cum_mm, 1)
            pe.wait_ge(prep_v, 3)

            block_mm(0)
            for i in range(1, 3):
                block_mm(i)
            with pe.Fori(3, PAIRS - 1) as i:
                block_mm(i)
            block_mm(PAIRS - 1)
            block_mm(PAIRS)
            block_mm(PAIRS + 1)

            def l1(p):
                for c in range(HC):
                    mm = pe.matmul(ps[:, 2 * (p % 2) + c // 2, (c % 2) * PAIR:(c % 2 + 1) * PAIR],
                                   sw1[:, c * 128:(c + 1) * 128], tile_of(uT, 2 * p, 2), start=True, stop=True)
                mm.then_inc(l1_mm, 1)

            def l2(p):
                pe.wait_ge(hid_ok, p + 1)
                if p >= 2:
                    pe.wait_ge(stg_ok, p - 1)
                for j in range(2):
                    for c in range(HC):
                        mm = pe.matmul(ps[0:TOK, 4 + p % 2, j * D:(j + 1) * D], hid[:, p % 2, c, j * TOK:(j + 1) * TOK],
                                       sw2[:, c, :], start=(c == 0), stop=(c == HC - 1))
                mm.then_inc(l2_mm, 1)

            pe.wait_ge(ld["gate"], 16)
            pe.wait_ge(zs_ok, PAIRS)
            pe.wait_ge(yg_ok, PAIRS)
            turn_tiles(*NORM2[0], table, u2_ok, u2a_ok, u2T_mm, NORM2[0][1])
            for t in range(T):
                if t == 8:
                    turn_tiles(*NORM2[1], table, u2_ok, u2a_ok, u2T_mm, NORM2[0][1])
                if t == 14:
                    turn_tiles(*NORM2[2], table, u2_ok, u2a_ok, u2T_mm, NORM2[0][1])
                pe.wait_ge(u2T_sb, t // 4 + 1)
                mm = pe.matmul(ps[0:TOK, 6, t * E:(t + 1) * E], tile_of(uT, t), gate_w[:, :], start=True, stop=True)
            mm.then_inc(lg_mm, 1)
            pe.wait_ge(ld["sw1"], 16)
            l1(0)
            pe.wait_ge(prob_ok, 1)
            for g in range(GROUPS):
                mm = pe.transpose(ps[:, 7, g * TOK:(g + 1) * TOK],
                                  prob[:, 8 * g:8 * g + 8, :].rearrange("p t e -> p (t e)"), ident[0:TOK, 0:TOK])
            mm.then_inc(pT_mm, 1)

            l1(1)
            pe.wait_ge(ld["sw2"], 16)
            pe.wait_ge(prep_p, 9)
            pe.wait_ge(pT_sb, 1)
            for m in range(DIGITS):
                pe.wait_ge(cmp_ok, m + 1)
                pe.matmul(ps[:, 7, 0:3], same16[:, :], cnt[:, :], start=True, stop=True).then_inc(cnt_mm, 1)
                if m % 2:
                    l1(m // 2 + 2)
                else:
                    l2(m // 2)
            l1(9)

            pe.wait_ge(tot_ok, 1)
            pe.matmul(ps[:, 7, 0:6], same_e, pre[:, :], start=True, stop=False)
            pe.matmul(ps[:, 7, 0:6], below, tot[:, :], start=False, stop=True).then_inc(off_mm, 1)
            l2(8)
            pe.wait_ge(pos_ok, 1)
            for g in range(GROUPS):
                mm = pe.transpose(ps[0:TOK, 6, g * 128:(g + 1) * 128], pos[:, g, :], ident[:, :])
            mm.then_inc(posT_mm, 1)
            l1(10)
            for k in range(4):
                pe.wait_ge(hot_ok, k + 1)
                es = slice(QUARTER * k, QUARTER * (k + 1))
                for t in range(T):
                    mm = pe.matmul(ps[0:QUARTER * SLOTA, 6, k * QUARTER * SLOTB:(k + 1) * QUARTER * SLOTB],
                                   hotV[:, es, :, t].rearrange("p e n -> p (e n)"),
                                   hotB[:, es, :, t].rearrange("p e n -> p (e n)"), start=(t == 0), stop=(t == T - 1))
                mm.then_inc(lst_mm, 1)
                if k == 0:
                    l2(9)
            pe.wait_ge(dg_ok, 1)
            pe.matmul(ps[0:NL, 7, 32:32 + NL], sel16[0:QUARTER * SLOTA, :], dgl[:, :], start=True, stop=True)
            pe.matmul(ps[0:NL, 7, 16:17], dgl[:, :], sel16[0:QUARTER * SLOTA, 0:1], start=True, stop=True).then_inc(idx_mm, 1)
            for b in range(SLOTB):
                mm = pe.matmul(ps[:, 6, 256:256 + E], slide16[0:QUARTER * SLOTA, SLOTB - b:SLOTB - b + MAIN],
                               dg[:, :, :, b].rearrange("p k e -> p (k e)"), start=(b == 0), stop=(b == SLOTB - 1))
            mm.then_inc(idx_mm, 1)
            l2(10)

            pe.wait_ge(ld["w1"], 16)
            pe.wait_ge(ld["w2"], 16)
            pe.wait_ge(got_ld[E], 16)
            pe.wait_ge(dup_ok, 1)
            pe.transpose(ps[:, 7, 0:NL], got[0:NL, E, 0:D], ident[0:NL, 0:NL]).then_inc(xe_mm, 1)

            def first(e):
                pe.wait_ge(got_ld[e], 16)
                if e:
                    pe.wait_ge(xe_sb, e)
                pe.transpose(ps[:, 6 + e % 2, 128 + 0:256], got[:, e, 0:D], ident[:, :]).then_inc(xe_mm, 1)

            def layer1(e):
                pe.wait_ge(xe_sb, e + 2)
                if e >= 2:
                    pe.wait_ge(e1_ok, e - 1)
                b = 2 * (e % 2)
                for c in range(HC):
                    mm = pe.matmul(ps[:, b + c // 2, (c % 2) * CAP:(c % 2 + 1) * CAP], w1[:, e, c * 128:(c + 1) * 128],
                                   xe[:, e, :], start=True, stop=True)
                mm.then_inc(e1_mm, 1)

            def layer2(e):
                pe.wait_ge(e1_ok, e + 1)
                if e >= 2:
                    pe.wait_ge(ys_ok, e - 1)
                for c in range(HC):
                    mm = pe.matmul(ps[:, 4 + e % 2, 0:CAP], w2[:, e, c * D:(c + 1) * D], hid[:, e % 2, c, 0:CAP],
                                   start=(c == 0), stop=(c == HC - 1))
                mm.then_inc(e2_mm, 1)

            def turn(e):
                pe.wait_ge(ye_ok, e + 1)
                if e >= 2:
                    pe.wait_ge(ys_ok, e - 1)
                pe.transpose(ps[:, 4 + e % 2, 256:384], ye[:, e, 0:MAIN], ident[:, :]).then_inc(yt_mm, 1)

            first(0)
            for e in range(E):
                if e + 1 < E:
                    first(e + 1)
                layer1(e)
                if e:
                    layer2(e - 1)
                if e >= 2:
                    turn(e - 2)
            layer2(E - 1)
            turn(E - 2)
            turn(E - 1)
            pe.wait_ge(yel_ok, 1)
            pe.transpose(ps[0:NL, 6, 0:D], yel[:, :], ident[:, :]).then_inc(yt_mm, 1)
            pe.wait_ge(left_ok, 1)
            pe.matmul(ps[0:NL, 6, 256:256 + D], eqm[:, :], yl[:, 0, :], start=True, stop=True).then_inc(left_mm, 1)

        @block.scalar
        def _(act):
            def last_taps(p):
                if pair(p):
                    for mm_, cc in ((bc_mm, (2,)), (x_mm, (0, 1))):
                        act.wait_ge(mm_, p + 1)
                        if pair(p - 1):
                            act.wait_ge(conv_ok, 2 * p - (cc == (2,)))
                        for c in cc:
                            raw = (XA, XB, BC)[c]
                            act.activation(taps3[:, c, :], raw, ACT.Identity,
                                           scale=conv_w[:, 4 * c + 3:4 * c + 4], bias=conv_b[:, c:c + 1])
                            tp = act.activation(by_seq(tap1[:, c, :])[:, :, 1:S], by_seq(raw)[:, :, 0:S - 1], ACT.Copy,
                                                scale=conv_w[:, 4 * c + 2:4 * c + 3])
                        tp.then_inc(tap0_ok, 1)

            def half_tanh(p):
                if pair(p):
                    act.wait_ge(conv_ok, 2 * p + 1)
                    act.activation(tanhb[:, :], conv[:, 2, :], ACT.Tanh, scale=0.5).then_inc(tanh_b, 1)
                    act.wait_ge(conv_ok, 2 * p + 2)
                    act.activation(tanh3[:, 0:2, :], conv[:, 0:2, :], ACT.Tanh, scale=0.5).then_inc(tanh_x, 1)

            def block_act(i):
                if not first_pair(i):
                    last_taps(i + 1)
                if pair(i):
                    act.wait_ge(g_mm, i + 1)
                    for j in range(2):
                        for hh in range(NH):
                            ex_ = act.activation(lmask[:, j, hh, :], SEG[j][:, hh * TOK:(hh + 1) * TOK], ACT.Exp,
                                                 bias=bias_s[:, bass.ds((2 * i + j) * NH + hh, 1)])
                    ex_.then_inc(exp_ok, 1)
                if pair(i - 2):
                    act.wait_ge(o_mm, i - 1)
                    act.activation(o[:, bass.ds(2 * (i - 2), 2), :], O, ACT.Copy).then_inc(o_sb, 1)
                if pair(i):
                    act.wait_ge(xtr_mm, i + 1)
                    if pair(i - 1):
                        act.wait_ge(y_mm, i)
                    act.activation(xrow[:, :, :], XR, ACT.Copy).then_inc(xrow_ok, 1)
                half_tanh(i + 1)
                if pair(i):
                    act.wait_ge(z_mm, i + 1)
                    act.activation(tanhz[:, :, :].rearrange("p c n -> p (c n)"), Z, ACT.Tanh, scale=0.5).then_inc(tanh_z, 1)

            act.wait_ge(p_step, 1)
            act.activation(tanhz[0:TOK, 0, 0:T], half_neg[:, :], ACT.Exp).then_inc(a_step, 1)

            def keep_h(g):
                n = min(4, T - 4 * g)
                act.wait_ge(h_mm, 4 * g + n)
                act.activation(h[:, 4 * g:4 * g + n, :].rearrange("p t c -> p (t c)"), ps_h(4 * g, n), ACT.Copy)\
                   .then_inc(h_sb, 1)

            def normalise(t0, t1, src, dst, ok):
                for t in range(t0 + 1, t1, 2):
                    act.activation(dst[:, t, 0:D], src[:, t, :], ACT.Identity, scale=rstd[:, t:t + 1],
                                   bias=shift[:, t:t + 1]).then_inc(ok, 1)

            def keep_turned(g, turned, kept):
                n = min(4, T - 4 * g)
                act.wait_ge(turned, 4 * g + n)
                act.activation(tile_of(uT, 4 * g, n).rearrange("p (t c) -> p t c", t=n),
                               psf[:, g * 512:g * 512 + n * 128].rearrange("p (t c) -> p t c", t=n)[:, :, 0:TOK],
                               ACT.Copy).then_inc(kept, 1)

            for g in range(4):
                keep_h(g)
            act.wait_ge(shift_ok, 1)
            normalise(*NORM1[0], h, u, ua_ok)
            for g in range(4, BANKS):
                keep_h(g)
            for g in range(2):
                keep_turned(g, uT_mm, uT_sb)
            act.wait_ge(shift_ok, 2)
            normalise(*NORM1[1], h, u, ua_ok)
            act.wait_ge(ld["cols"], 16)
            last_taps(0)
            for g in range(2, 4):
                keep_turned(g, uT_mm, uT_sb)
            act.wait_ge(shift_ok, 3)
            normalise(*NORM1[2], h, u, ua_ok)
            for g in range(4, BANKS):
                keep_turned(g, uT_mm, uT_sb)
            half_tanh(0)
            act.wait_ge(ld["rows"], 16)
            act.activation(exp_a[:, :], a_log, ACT.Exp).then_inc(exp_a_ok, 1)
            act.wait_ge(dtx_ok, 1)
            act.activation(dt_abs, dt_x, ACT.Abs).then_inc(a_step, 1)
            act.wait_ge(a_step, 2)
            act.activation(dt_exp, dt_abs, ACT.Exp, scale=-1.0).then_inc(a_step, 1)
            act.wait_ge(a_step, 3)
            act.activation(dt_log, dt_exp, ACT.Ln, bias=1.0).then_inc(log_ok, 1)
            last_taps(1)
            act.wait_ge(dtc_ok, 1)
            act.activation(ln_dt, dt_c, ACT.Ln).then_inc(ln_ok, 1)
            act.activation(tanhz[:, 0, 0:1], ident[:, 0:1], ACT.Tanh).then_inc(a_step, 1)
            act.wait_ge(a_step, 4)
            act.wait_ge(cum_ok, 1)
            block_act(0)
            for i in range(1, 3):
                block_act(i)
            with act.Fori(3, PAIRS - 1) as i:
                block_act(i)
            block_act(PAIRS - 1)
            block_act(PAIRS)
            block_act(PAIRS + 1)
            for k, (t0, t1) in enumerate(NORM2):
                if k:
                    act.wait_ge(shift_ok, 3 + k)
                    normalise(t0, t1, h, table, u2a_ok)
                for g in range(t0 // 4, BANKS if t1 == T else t1 // 4):
                    keep_turned(g, u2T_mm, u2T_sb)
            act.wait_ge(sm_v, 1)
            act.activation(ex[:, :, :], prob[:, 0:T, :], ACT.Exp).then_inc(sm_a, 1)

            act.wait_ge(ld["biases"], 16)

            def gelu(p, q):
                act.wait_ge(l1_mm, p + 1)
                for c in range(HC):
                    g_ = act.activation(hid[:, q, c, :], ps[:, 2 * q + c // 2, (c % 2) * PAIR:(c % 2 + 1) * PAIR],
                                        ACT.Gelu_apprx_tanh, bias=sb1[:, c:c + 1])
                g_.then_inc(hid_ok, 1)
            act.activation(hid[:, 0, 0, 0:1], ident[:, 0:1], ACT.Gelu_apprx_tanh).then_inc(a_step, 1)
            act.wait_ge(a_step, 5)
            with act.Fori(0, PAIRS // 2) as i:
                for q in range(2):
                    gelu(2 * i + q, q)
            gelu(PAIRS - 1, 0)

            act.wait_ge(l2_mm, PAIRS)
            for e in range(E):
                act.wait_ge(e1_mm, e + 1)
                if e >= 2:
                    act.wait_ge(e2_mm, e - 1)
                b = 2 * (e % 2)
                for c in range(HC):
                    g_ = act.activation(hid[:, e % 2, c, 0:CAP], ps[:, b + c // 2, (c % 2) * CAP:(c % 2 + 1) * CAP],
                                        ACT.Gelu_apprx_tanh, bias=b1[:, e * HC + c:e * HC + c + 1])
                g_.then_inc(e1_ok, 1)

        @block.gpsimd
        def _(pool):
            pool.memset(half_neg[:, :], -0.5).then_inc(p_step, 1)
            pool.memset(zero[:, :], 0.0).then_inc(zero_ok, 1)
            pool.memset(ones[:, :], 1.0).then_inc(prep_p, 1)
            pool.memset(ones3[:, :], 1.0).then_inc(ones3_ok, 1)
            pool.memset(share[:, :], 1.0 / DIN).then_inc(prep_p, 1)
            pool.memset(eps16[:, :], 16 * EPS).then_inc(prep_p, 1)
            pool.memset(prob[:, :, :], -1.0).then_inc(prep_p, 1)
            pool.memset(by_seq(tap1[:, :, :].rearrange("p c n -> p (c n)"))[:, :, 0:1], 0.0).then_inc(tap1_zero, 1)
            pool.wait_ge(p_step, 1)

            def root(k, t0, t1):
                pool.wait_ge(var_ok, k)
                pool.tensor_tensor(rstd[:, t0:t1], s_var[:, t0:t1], half_neg[:, t0:t1], ALU.pow).then_inc(pow_ok, 1)

            pool.wait_ge(ld["ident"], 16)
            pool.tensor_copy(ident16[:, :], ident[:, :]).then_inc(prep_v, 1)
            root(1, *NORM1[0])
            pool.wait_ge(ld["mask"], 16)
            pool.tensor_copy(mask[:, :], mask32[:, :]).then_inc(prep_v, 1)
            root(2, *NORM1[1])
            root(3, *NORM1[2])
            pool.wait_ge(ld["cols"], 16)
            pool.wait_ge(ld["w_out"], 16)
            for c in range(2):
                wo = pool.tensor_scalar(w_out[:, c, :], w_out_raw[:, c, :], norm_w[:, c:c + 1], None, ALU.mult)
            wo.then_inc(prep_v, 1)
            pool.wait_ge(ld["rows"], 16)
            pool.tensor_tensor(d_eye[:, :, :], ident[0:TOK, 0:TOK].unsqueeze(1).broadcast_to([TOK, NH, TOK]),
                               d_row.unsqueeze(2).broadcast_to([TOK, NH, TOK]), ALU.mult).then_inc(p_step, 1)
            pool.wait_ge(p_step, 2)
            def second_last_tap(p):
                if pair(p):
                    for k, cc in enumerate((slice(2, 3), slice(0, 2))):
                        pool.wait_ge(taps, 3 * p + (1, 3)[k])
                        if pair(p - 1):
                            pool.wait_ge((bc_ok, xs_ok)[k], p)
                        pool.tensor_tensor(conv[:, cc, :], taps3[:, cc, :], tap1[:, cc, :], ALU.add).then_inc(conv_ok, 1)

            pool.wait_ge(tap1_zero, 1)
            second_last_tap(0)
            def block_pool(i):
                second_last_tap(i + 1)
                if pair(i - 1) and not last(i - 1):
                    pool.wait_ge(yg_ok, i)
                    pool.tensor_tensor(ysq[:, :, :], yg[:, :, :], yg[:, :, :], ALU.mult).then_inc(ysq_ok, 1)
                if pair(i):
                    pool.wait_ge(gm_ok, i + 1)
                    for j in range(2):
                        sk = pool.tensor_tensor(gm[:, j, :, :], gm[:, j, :, :], d_eye[:, :, :], ALU.add)
                    sk.then_inc(skip_ok, 1)
                if pair(i - 2):
                    if isinstance(i, int) and i == 2:
                        pool.wait_ge(prep_p, 3)
                    pool.wait_ge(o_sb, i - 1)
                    ms, rs = (rms[:, k, bass.ds(2 * (i - 2), 2)] for k in range(2))
                    pool.tensor_tensor(ms, o[:, bass.ds(2 * (i - 2), 2), D], eps16[:, :], ALU.add)\
                        .then_inc(ms_ok, 1)
                    pool.wait_ge(ms_ok, i - 1)
                    pool.tensor_tensor(rs, ms, half_neg[:, 0:2], ALU.pow).then_inc(rms_ok, 1)

            for i in range(3):
                block_pool(i)
            with pool.Fori(3, PAIRS - 1) as i:
                block_pool(i)
            block_pool(PAIRS - 1)
            root(4, *NORM2[0])
            block_pool(PAIRS)
            block_pool(PAIRS + 1)
            root(5, *NORM2[1])
            root(6, *NORM2[2])
            pool.wait_ge(ld["consts"], 16)
            pool.tensor_copy(same16[:, :], same_e).then_inc(prep_p, 1)
            pool.tensor_copy(value16[:, :], value[0:TOK, :]).then_inc(prep_p, 1)
            pool.tensor_copy(iota_t[:, :, :], iota16[0:TOK, :].unsqueeze(2).broadcast_to([TOK, SLOTB, T])).then_inc(prep_p, 1)
            pool.tensor_copy(slide16[:, :], slide).then_inc(prep_p, 1)
            pool.tensor_copy(sel16[:, :], last_a.broadcast_to([128, NL])).then_inc(prep_p, 1)
            pool.wait_ge(u2_ok, (NORM2[0][1] + T) // 2)
            pool.wait_ge(u2a_ok, (T - NORM2[0][1]) // 2)
            pool.wait_ge(ld["sb2"], 16)
            pool.tensor_tensor(h[:, :, :], h[:, :, :], sb2[:, :].unsqueeze(1).broadcast_to([TOK, T, D]), ALU.add)\
                .then_inc(hb_ok, 1)
            pool.wait_ge(tab_st, 16)
            pool.wait_ge(idx_ok, 1)
            pool.indirect_dma_start(got[0:NL, E, :], None, table_dram, bass.IndirectOffsetOnAxis(idx_l[:, 0:1], 0))\
                .then_inc(got_ld[E], 16)
            pool.wait_ge(idx_ok, 2)

            def fetch(e):
                pool.indirect_dma_start(got[:, e, :], None, table_dram, bass.IndirectOffsetOnAxis(idx[:, e:e + 1], 0))\
                    .then_inc(got_ld[e], 16)
            for e in range(AHEAD):
                fetch(e)
            pool.wait_ge(out_st[0], 16 * (PAIRS // 2 + 2))
            pool.wait_ge(out_st[1], 16 * (PAIRS // 2))
            pool.wait_ge(odd_st, 16)
            for e in range(E):
                pool.wait_ge(ys_ok, e + 1)
                if e >= 2:
                    pool.wait_ge(added[e % 2], 16 * (e // 2))
                pool.indirect_dma_start(odd_dram if e % 2 else out, bass.IndirectOffsetOnAxis(idx[:, e:e + 1], 0),
                                        ys[:, e % 4, :], None, compute_op=ALU.add).then_inc(added[e % 2], 16)
                if e + AHEAD < E:
                    fetch(e + AHEAD)
            pool.wait_ge(left_ok, 2)
            pool.wait_ge(added[0], 16 * (E // 2))
            pool.indirect_dma_start(out, bass.IndirectOffsetOnAxis(idx_s[:, 0:1], 0), yl[:, 1, :], None,
                                    compute_op=ALU.add).then_inc(added[0], 16)
            pool.wait_ge(added[0], 16 * (E // 2 + 1))
            pool.wait_ge(added[1], 16 * (E // 2))
            eight = lambda ap: ap.rearrange("(p r) c -> p (r c)", r=8)
            pool.dma_start(eight(out[0:NTOK, :]), eight(odd_dram), accum_op=ALU.add, max_dma_last_dim=8 * D * 4).then_inc(joined, 16)
            pool.wait_ge(joined, 16)

        @block.vector
        def _(dve):
            done = [0]

            def chain(ins):
                done[0] += 1
                ins.then_inc(v_step, 1)
                dve.wait_ge(v_step, done[0])

            def earlier_taps(p):
                if pair(p):
                    for n in range(2, 4):
                        for k, c in enumerate((2, 0, 1)):
                            if n == 2:
                                dve.wait_ge(tap0_ok, 2 * p + 1 + (k > 0))
                            else:
                                dve.wait_ge(tap_v, 3 * p + k + 1)
                            dst, src = by_seq(taps3[:, c, :]), by_seq((XA, XB, BC)[c])
                            dve.scalar_tensor_tensor(dst[:, :, n:S], src[:, :, 0:S - n],
                                                     conv_w[:, 4 * c + 3 - n:4 * c + 4 - n], dst[:, :, n:S],
                                                     ALU.mult, ALU.add).then_inc(tap_v if n < 3 else taps, 1)

            def gate_x(p):
                if pair(p):
                    dve.wait_ge(tanh_b, p + 1)
                    dve.scalar_tensor_tensor(bs[:, :], tanhb[0:NST, :], 1.0, conv[0:NST, 2, :], ALU.add, ALU.mult)
                    dve.scalar_tensor_tensor(cs[:, :], tanhb[NST:2 * NST, :], 1.0, conv[NST:2 * NST, 2, :], ALU.add, ALU.mult)\
                        .then_inc(bc_ok, 1)
                    dve.wait_ge(tanh_x, p + 1)
                    if pair(p - 1):
                        dve.wait_ge(xtr_mm, p)
                    dve.scalar_tensor_tensor(xs[:, :, :], tanh3[:, 0:2, :], 1.0, conv[:, 0:2, :], ALU.add, ALU.mult)\
                        .then_inc(xs_ok, 1)

            def block_dve(i):
                if not first_pair(i):
                    earlier_taps(i + 1)
                if pair(i - 1):
                    dve.wait_ge(y_mm, i)
                    dve.wait_ge(zs_ok, i)
                    if last(i - 1):
                        dve.tensor_tensor(yg_last[:, :, :], Y, zs[:, :, :], ALU.mult).then_inc(yg_ok, 1)
                        dve.wait_ge(yg_ok, PAIRS)
                        dve.wait_ge(ysq_ok, PAIRS - 1)
                        dve.tensor_tensor(ysq_last[:, :, :], yg_last[:, :, :], yg_last[:, :, :], ALU.mult)\
                           .then_inc(ysq_ok, 1)
                    else:
                        if pair(i - 2):
                            dve.wait_ge(o_mm, i - 1)
                        dve.tensor_tensor(yg[:, :, :], Y, zs[:, :, :], ALU.mult).then_inc(yg_ok, 1)
                if pair(i):
                    dve.wait_ge(exp_ok, i + 1)
                    if pair(i - 1):
                        dve.wait_ge(y_mm, i)
                    for j in range(2):
                        g_ = dve.tensor_tensor(gm[:, j, :, :], lmask[:, j, :, :],
                                               G[j].unsqueeze(1).broadcast_to([TOK, NH, TOK]), ALU.mult)
                    g_.then_inc(gm_ok, 1)
                gate_x(i + 1)
                if pair(i - 3):
                    dve.wait_ge(rms_ok, i - 2)
                    for j in range(2):
                        dve.scalar_tensor_tensor(h[:, 2 * (i - 3) + j, :], o[:, 2 * (i - 3) + j, 0:D],
                                                 rms[:, 1, bass.ds(2 * (i - 3) + j, 1)], h[:, 2 * (i - 3) + j, :],
                                                 ALU.mult, ALU.add).then_inc(h2_ok, 1)
                    for j in range(2):
                        dve.wait_ge(h2_ok, 2 * (i - 3) + j + 1)
                        dve.bn_stats(stats[:, 2 * (i - 3) + j, :], h[:, 2 * (i - 3) + j, :]).then_inc(st2_ok, 1)
                if pair(i):
                    dve.wait_ge(tanh_z, i + 1)
                    if pair(i - 1):
                        dve.wait_ge(yg_ok, i)
                    dve.scalar_tensor_tensor(zs[:, :, :].rearrange("p c n -> p (c n)"),
                                             tanhz[:, :, :].rearrange("p c n -> p (c n)"), 1.0, Z, ALU.add, ALU.mult)\
                        .then_inc(zs_ok, 1)

            def variance(t0, t1):
                me, qe, mo, qo = (stats[:, t0:t1, k] for k in (1, 2, 4, 5))
                m_, s_, d_, q_, v_ = (ap[:, t0:t1] for ap in (mean, s_sum, s_dif, s_sq, s_var))
                dve.tensor_tensor(d_, me, mo, ALU.subtract)
                dve.tensor_tensor(s_, me, mo, ALU.add)
                chain(dve.tensor_tensor(q_, qe, qo, ALU.add))
                dve.tensor_scalar(m_, s_, 0.5, None, ALU.mult)
                dve.tensor_scalar(q_, q_, 1.0 / D, EPS, ALU.mult, ALU.add)
                chain(dve.scalar_tensor_tensor(d_, d_, 0.25, d_, ALU.mult, ALU.mult))
                dve.tensor_tensor(v_, q_, d_, ALU.add).then_inc(var_ok, 1)

            def normalise(k, t0, t1, src, dst, ok, shared=True):
                dve.wait_ge(pow_ok, k)
                if shared:
                    dve.scalar_tensor_tensor(shift[:, t0:t1], mean[:, t0:t1], -1.0, rstd[:, t0:t1], ALU.mult, ALU.mult)\
                        .then_inc(shift_ok, 1)
                for t in range(t0, t1, 2 if shared else 1):
                    dve.tensor_scalar(dst[:, t, 0:D], src[:, t, :], mean[:, t:t + 1], rstd[:, t:t + 1],
                                      ALU.subtract, ALU.mult).then_inc(ok, 1)

            for k, (t0, t1) in enumerate(NORM1):
                for t in range(t0, t1):
                    dve.wait_ge(h_sb, t // 4 + 1)
                    dve.bn_stats(stats[:, t, :], h[:, t, :]).then_inc(st_a, 1)
                if k:
                    normalise(k, *NORM1[k - 1], h, u, u_ok)
                dve.wait_ge(st_a, t1)
                variance(t0, t1)
            normalise(3, *NORM1[2], h, u, u_ok)
            dve.wait_ge(ld["cols"], 16)
            earlier_taps(0)
            dve.wait_ge(dt_mm, 1)
            dve.wait_ge(ld["rows"], 16)
            per_tile = lambda ap: ap.unsqueeze(1).broadcast_to([TOK, T, NH])
            tiles = lambda ap: ap.rearrange("p (t h) -> p t h", h=NH)
            dve.tensor_tensor(tiles(dt_x), tiles(ps[0:TOK, 6, 0:T * NH]), per_tile(dt_bias), ALU.add).then_inc(dtx_ok, 1)
            gate_x(0)
            dve.wait_ge(ld["consts"], 16)
            dve.tensor_copy(digit_i[:, :, :].rearrange("p m k -> p (m k)"), digits)
            dve.wait_ge(dtx_ok, 1)
            dve.wait_ge(log_ok, 1)
            chain(dve.scalar_tensor_tensor(dt, dt_x, 0.0, dt_log, ALU.max, ALU.add))
            dve.wait_ge(exp_a_ok, 1)
            dve.scalar_tensor_tensor(tiles(decay), tiles(dt), -1.0, per_tile(exp_a[:, :]), ALU.mult, ALU.mult)\
                .then_inc(dec_ok, 1)
            dve.tensor_scalar(dt_c, dt, 1e-19, 0.25, ALU.max, ALU.mult).then_inc(dtc_ok, 1)

            earlier_taps(1)
            dve.wait_ge(cum_mm, 1)
            dve.wait_ge(ln_ok, 1)
            dve.tensor_tensor(bias_s, ln_dt, ps[0:TOK, 7, 0:T * NH], ALU.subtract).then_inc(cum_ok, 1)
            cum_t = ps[0:T * NH, 7, 128:128 + TOK]
            chain(dve.tensor_copy(cum_parts[:, 0, :], cum_t))
            chain(dve.tensor_tensor(cum_r[:, 0, :], cum_t, cum_parts[:, 0, :], ALU.subtract))
            chain(dve.tensor_copy(cum_parts[:, 1, :], cum_r[:, 0, :]))
            chain(dve.tensor_tensor(cum_r[:, 1, :], cum_r[:, 0, :], cum_parts[:, 1, :], ALU.subtract))
            dve.tensor_copy(cum_parts[:, 2, :], cum_r[:, 1, :]).then_inc(parts_ok, 1)
            block_dve(0)
            for i in range(1, 3):
                block_dve(i)
            with dve.Fori(3, PAIRS - 1) as i:
                block_dve(i)
            block_dve(PAIRS - 1)
            dve.wait_ge(st2_ok, NORM2[0][1])
            variance(*NORM2[0])
            block_dve(PAIRS)
            t0, t1 = NORM2[0]
            normalise(4, t0, t1 - 4, h, table, u2_ok, shared=False)
            block_dve(PAIRS + 1)
            dve.wait_ge(st2_ok, NORM2[1][1])
            variance(*NORM2[1])
            normalise(4, t1 - 4, t1, h, table, u2_ok, shared=False)
            block_dve(PAIRS + 2)
            normalise(5, *NORM2[1], h, table, u2_ok)
            dve.wait_ge(st2_ok, NORM2[2][1])
            variance(*NORM2[2])
            normalise(6, *NORM2[2], h, table, u2_ok)
            dve.wait_ge(lg_mm, 1)
            dve.wait_ge(prep_p, 4)
            lg = ps[0:TOK, 6, 0:T * E].rearrange("p (t e) -> p t e", e=E)
            over_e = lambda ap: ap.unsqueeze(2).broadcast_to([TOK, T, E])
            chain(dve.tensor_reduce(mx[:, :], lg, AX.X, ALU.max))
            dve.tensor_tensor(prob[:, 0:T, :], lg, over_e(mx[:, :]), ALU.subtract).then_inc(sm_v, 1)
            dve.wait_ge(sm_a, 1)
            chain(dve.tensor_reduce(den[:, :], ex[:, :, :], AX.X, ALU.add))
            chain(dve.reciprocal(rden[:, :], den[:, :]))
            dve.wait_ge(sm_v, 1)
            chain(dve.tensor_tensor(prob[:, 0:T, :], ex[:, :, :], over_e(rden[:, :]), ALU.mult))
            dve.tensor_scalar(prob[:, T - 1, :], prob[:, T - 1, :], valid[0:TOK, :], invalid[0:TOK, :],
                              ALU.mult, ALU.add).then_inc(prob_ok, 1)
            chain(dve.tensor_copy(cand[:, :], digit_i[:, 0, :]))
            dve.tensor_tensor(table[:, :, D:ROW], ex[:, :, :], over_e(rden[:, :]), ALU.mult).then_inc(prob_ok, 1)

            def add_rows(p):
                dve.wait_ge(l2_mm, p + 1)
                if p >= 2:
                    dve.wait_ge(out_st[p % 2], 16 * (p // 2))
                dve.tensor_tensor(stage[:, p % 2, :, :].rearrange("p j c -> p (j c)"), ps[0:TOK, 4 + p % 2, 0:2 * D],
                                  h[:, 2 * p:2 * p + 2, :].rearrange("p j c -> p (j c)"), ALU.add).then_inc(stg_ok, 1)

            dve.wait_ge(pT_mm, 1)
            dve.tensor_copy(pse[:, :, :].rearrange("p g n -> p (g n)"), ps[:, 7, 0:GROUPS * TOK]).then_inc(pT_sb, 1)
            dve.wait_ge(pT_sb, 1)
            thr = cand[:, :].bitcast(F32)
            for m in range(DIGITS):
                for k in range(1, 4):
                    cm = dve.tensor_scalar(hits[:, k - 1, :, :], pse[:, :, :], thr[:, k:k + 1], 0.0, ALU.is_ge, ALU.add,
                                           accum_out=cnt[:, k - 1:k])
                cm.then_inc(cmp_ok, 1)
                dve.tensor_tensor(settled[:, :], cand[:, 0:1].broadcast_to([128, 4]), digit_i[:, m + 1, :],
                                  ALU.bitwise_xor).then_inc(srch_v, 1)
                if m % 2:
                    if m == 1:
                        dve.wait_ge(hb_ok, 1)
                    add_rows(m // 2)
                dve.wait_ge(cnt_mm, m + 1)
                dve.scalar_tensor_tensor(met[:, :], ps[:, 7, 0:3], CAP - 0.5,
                                         digits[:, 4 * m + 1:4 * m + 2].broadcast_to([128, 3]), ALU.is_ge, ALU.mult,
                                         accum_out=digit[:, :]).then_inc(srch_v, 1)
                dve.wait_ge(srch_v, 4 * m + 2)
                dve.tensor_copy(digit_bits[:, :], digit[:, :]).then_inc(srch_v, 1)
                dve.wait_ge(srch_v, 4 * m + 3)
                dve.tensor_tensor(cand[:, :], settled[:, :], digit_bits[:, 0:1].broadcast_to([128, 4]), ALU.bitwise_xor)\
                    .then_inc(srch_v, 1)
                dve.wait_ge(srch_v, 4 * m + 4)

            tau = thr
            dve.tensor_scalar(ge[:, :, :], pse[:, :, :], tau[:, 0:1], None, ALU.is_ge)
            chain(dve.tensor_scalar(m6[:, 1, :, :], pse[:, :, :], tau[:, 0:1], None, ALU.is_equal))
            chain(dve.tensor_tensor(m6[:, 0, :, :], ge[:, :, :], m6[:, 1, :, :], ALU.subtract))
            for k in range(2):
                for g in range(GROUPS):
                    sc_ = dve.tensor_tensor_scan(rank[:, k, g, :], ones[:, :], m6[:, k, g, :], 0.0, ALU.mult, ALU.add)
            chain(sc_)
            chain(dve.tensor_copy(tot[:, :], rank[:, :, :, TOK - 1].rearrange("p k g -> p (k g)")))
            chain(dve.tensor_tensor_scan(pre[:, :], ones[:, 0:6], tot[:, :], 0.0, ALU.mult, ALU.add))
            dve.tensor_tensor(pre[:, :], pre[:, :], tot[:, :], ALU.subtract).then_inc(tot_ok, 1)
            add_rows(7)
            dve.wait_ge(off_mm, 1)
            chain(dve.tensor_copy(off[:, :], ps[:, 7, 0:6]))
            for k in range(2):
                for g in range(GROUPS):
                    st_ = dve.scalar_tensor_tensor(rank[:, k, g, :], rank[:, k, g, :], off[:, 3 * k + g:3 * k + g + 1],
                                                   m6[:, k, g, :], ALU.add, ALU.mult)
            dve.tensor_scalar(ge[:, :, :], ge[:, :, :], -BIG, BIG - 1, ALU.mult, ALU.add)
            chain(st_)
            chain(dve.tensor_tensor(pos[:, :, :], rank[:, 0, :, :], rank[:, 1, :, :], ALU.add))
            dve.tensor_tensor(pos[:, :, :], pos[:, :, :], ge[:, :, :], ALU.add).then_inc(pos_ok, 1)
            add_rows(8)
            dve.wait_ge(posT_mm, 1)
            by_e = lambda ap: ap.rearrange("p (t e) -> p e t", e=E)
            chain(dve.tensor_copy(pos_i[:, :, :], by_e(ps[0:TOK, 6, 0:T * E])))
            dve.tensor_scalar(pa_i[:, :, :], pos_i[:, :, :], 4, None, ALU.logical_shift_right)
            chain(dve.tensor_scalar(pb_i[:, :, :], pos_i[:, :, :], SLOTB - 1, None, ALU.bitwise_and))
            dve.tensor_copy(pa_h[:, :, :], pa_i[:, :, :])
            chain(dve.tensor_copy(pb_h[:, :, :], pb_i[:, :, :]))
            dve.wait_ge(prep_p, 9)
            for k in range(4):
                es = slice(QUARTER * k, QUARTER * (k + 1))
                hot = lambda ap, n: ap[:, es, :].unsqueeze(2).broadcast_to([TOK, QUARTER, n, T])
                number = lambda n: iota_t[:, 0:n, :].unsqueeze(1).broadcast_to([TOK, QUARTER, n, T])
                dve.tensor_tensor(hotA[:, es, :, :], hot(pa_h, SLOTA), number(SLOTA), ALU.is_equal).then_inc(hot_a, 1)
                dve.tensor_tensor(hotB[:, es, :, :], hot(pb_h, SLOTB), number(SLOTB), ALU.is_equal)
                dve.wait_ge(hot_a, k + 1)
                dve.tensor_tensor(hotV[:, es, :, :].rearrange("p e n t -> p (e n) t"),
                                  hotA[:, es, :, :].rearrange("p e n t -> p (e n) t"),
                                  value16[:, :].unsqueeze(1).broadcast_to([TOK, QUARTER * SLOTA, T]), ALU.mult)\
                    .then_inc(hot_ok, 1)
                if k == 2:
                    add_rows(9)
            dve.wait_ge(lst_mm, 4)
            chain(dve.tensor_tensor(dg[:, :, :, :],
                                    ps[0:QUARTER * SLOTA, 6, 0:E * SLOTB].rearrange("p (k e b) -> p k e b", k=4, e=QUARTER),
                                    diag[0:QUARTER * SLOTA, :].unsqueeze(1).unsqueeze(3)
                                    .broadcast_to([QUARTER * SLOTA, 4, QUARTER, SLOTB]), ALU.mult))
            dve.tensor_copy(dgl[:, :].rearrange("p (k e r) -> p k e r", k=4, e=QUARTER), dg[:, :, :, 0:LEFT])\
                .then_inc(dg_ok, 1)
            dve.wait_ge(idx_mm, 1)
            dve.tensor_scalar(idx_l[:, :], ps[0:NL, 7, 16:17], float(VALUE0), None, ALU.add).then_inc(idx_ok, 1)
            dve.wait_ge(idx_mm, 2)
            dve.tensor_scalar(idx[:, :], ps[:, 6, 256:256 + E], float(VALUE0), None, ALU.add).then_inc(idx_ok, 1)
            dve.tensor_scalar(idx_lf[:, :], ps[0:NL, 7, 16:17], float(VALUE0), None, ALU.add)
            chain(dve.tensor_scalar(idx_rowf[:, :], ps[0:NL, 7, 32:32 + NL], float(VALUE0), None, ALU.add))
            chain(dve.tensor_scalar(eqm[:, :], idx_rowf[:, :], idx_lf[:, 0:1], None, ALU.is_equal))
            chain(dve.tensor_tensor(eqe[:, :], eqm[:, :], earlier[0:NL, :], ALU.mult))
            chain(dve.tensor_reduce(dup[:, 0:1], eqe[:, :], AX.X, ALU.max))
            chain(dve.tensor_scalar(dup[:, 1:2], dummy[0:NL, :], idx_lf[:, 0:1], None, ALU.subtract))
            dve.scalar_tensor_tensor(idx_s[:, :], dup[:, 1:2], dup[:, 0:1], idx_lf[:, :], ALU.mult, ALU.add)\
                .then_inc(dup_ok, 1)
            add_rows(10)
            dve.wait_ge(xe_mm, 1)
            dve.tensor_copy(xe[:, :, MAIN:CAP], ps[:, 7, 0:NL].rearrange("p (e r) -> p e r", e=E)).then_inc(xe_sb, 1)

            def take(e):
                dve.wait_ge(xe_mm, e + 2)
                dve.tensor_copy(xe[:, e, 0:MAIN], ps[:, 6 + e % 2, 128:256]).then_inc(xe_sb, 1)

            def bias2(e):
                dve.wait_ge(e2_mm, e + 1)
                dve.tensor_scalar(ye[:, e, :], ps[:, 4 + e % 2, 0:CAP], b2[:, e:e + 1], None, ALU.add).then_inc(ye_ok, 1)

            def scale(e):
                dve.wait_ge(yt_mm, e + 1)
                if e >= 4:
                    dve.wait_ge(added[e % 2], 16 * (e // 2 - 1))
                dve.tensor_scalar(ys[:, e % 4, :], ps[:, 4 + e % 2, 256:384], got[:, e, D + e:D + e + 1], None,
                                  ALU.mult).then_inc(ys_ok, 1)
            take(0)
            for e in range(E):
                if e + 1 < E:
                    take(e + 1)
                if e:
                    bias2(e - 1)
                if e >= 2:
                    scale(e - 2)
            bias2(E - 1)
            dve.wait_ge(ye_ok, E)
            dve.tensor_copy(yel[:, :].rearrange("p (e r) -> p e r", e=E), ye[:, :, MAIN:CAP]).then_inc(yel_ok, 1)
            scale(E - 2)
            scale(E - 1)
            chain(dve.tensor_tensor(sc_l[:, 0:E], got[0:NL, E, D:ROW], own_e[0:NL, :], ALU.mult))
            chain(dve.tensor_reduce(sc_l[:, E:E + 1], sc_l[:, 0:E], AX.X, ALU.add))
            dve.wait_ge(yt_mm, E + 1)
            dve.tensor_scalar(yl[:, 0, :], ps[0:NL, 6, 0:D], sc_l[:, E:E + 1], None, ALU.mult).then_inc(left_ok, 1)
            dve.wait_ge(left_mm, 1)
            dve.tensor_copy(yl[:, 1, :], ps[0:NL, 6, 256:256 + D]).then_inc(left_ok, 1)
    return nc


def constants():
    n = np.arange(2 * HOP, dtype=np.float64) + 0.5
    mdct = np.sqrt(4.0 / HOP) * np.cos(np.outer(n + HOP / 2, np.pi / HOP * n[:HOP]))
    wtok = np.sin(np.pi * n / (2 * HOP))[:, None].astype(np.float32) * mdct.astype(np.float32)
    r = np.arange(TOK)
    seq = r[:, None] // S == r[None, :] // S
    tri = (seq & (r[:, None] <= r[None, :])).astype(np.float32)
    q = np.arange(128)
    same = (q[:, None] % E == q[None, :] % E)
    below = same & (q[:, None] // E < q[None, :] // E)
    ea, el = q // SLOTA, q // LEFT
    parts = [
        same, below,
        np.tile([k * 4.0 ** (DIGITS - 1 - m) if m < DIGITS else 0.0 for m in range(DIGITS + 1) for k in range(4)], (128, 1)),
        np.tile(np.arange(16.0), (128, 1)),
        q[:, None] + TOK * np.arange(T)[None, :] - float(VALUE0),
        ea[:, None] == np.arange(QUARTER)[None, :],
        np.arange(NL)[None, :] < q[:, None],
        el[:, None] == np.arange(E)[None, :],
        (q < S)[:, None], (q < S)[:, None] - 1.0, (NTOK + q)[:, None],
        ((q % SLOTA == SLOTA - 1) & (ea < QUARTER))[:, None],
        np.arange(SLOTB + MAIN)[None, :] == SLOTB + SLOTB * (q % SLOTA)[:, None]]
    return {
        "wtok": wtok.reshape(2, HOP, HOP).transpose(1, 0, 2).reshape(128, 2 * D),
        "tri": tri,
        "mask": np.where(tri > 0, 0.0, -1e30).astype(np.float32),
        "ident": np.eye(128, dtype=np.float32),
        "consts": np.concatenate([np.asarray(p, np.float32) for p in parts], axis=1),
    }


def layout(i):
    x = np.zeros((3 * T, NBLK * HOP), np.float32)
    x[:B, HOP:HOP + 4000] = i["x"]
    blocks = x.reshape(3 * T, NBLK, HOP)
    conv_w = i["L0_attn_conv_w"][:, 0, :].reshape(3, 128, 4).transpose(1, 0, 2).reshape(128, 12)
    cols = np.concatenate([
        i["L0_attn_norm_w"].reshape(2, 128).T, conv_w, i["L0_attn_conv_b"].reshape(3, 128).T], axis=1)
    return {
        "xT": np.stack([blocks[:, k:k + S].transpose(2, 0, 1).reshape(HOP, T * TOK) for k in range(2)], axis=1),
        "w_in": i["L0_attn_W_in"].T,
        "cols": cols,
        "rows": np.tile(np.concatenate([i["L0_attn_dt_bias"], i["L0_attn_A_log"], i["L0_attn_D"]]), (TOK, 1)),
        "w_out": i["L0_attn_W_out"].T.reshape(2, 128, D).transpose(1, 0, 2),
        "gate_w": i["L0_ffn_gate_w"],
        "sw1": i["L0_ffn_sw1"],
        "sw2": i["L0_ffn_sw2"].reshape(HC, 128, D).transpose(1, 0, 2),
        "sb2": np.tile(i["L0_ffn_sb2"], (TOK, 1)),
        "biases": np.concatenate([
            i["L0_ffn_sb1"].reshape(HC, 128).T, i["L0_ffn_b1"].reshape(E * HC, 128).T, i["L0_ffn_b2"].T], axis=1),
        "w1": i["L0_ffn_w1"].transpose(1, 0, 2),
        "w2": i["L0_ffn_w2"].reshape(E, HC, 128, D).transpose(2, 0, 1, 3).reshape(128, E, HC * D),
    }


def kernel(**inputs):
    import concourse.bacc as bacc
    from concourse.bass_utils import run_bass_kernel_spmd

    nc = bacc.Bacc("TRN2", target_bir_lowering=False, num_devices=1)
    arrays = layout({k: np.asarray(v) for k, v in inputs.items()}) | constants()
    arrays = {k: np.ascontiguousarray(v) for k, v in arrays.items()}
    aps = {k: nc.dram_tensor("in_" + k, v.shape, F32, kind="ExternalInput").ap() for k, v in arrays.items()}
    aps["out"] = nc.dram_tensor("out_rows", (NTOK + NL, D), F32, kind="ExternalOutput").ap()
    program(nc, aps)
    r = run_bass_kernel_spmd(nc, [{"in_" + k: v for k, v in arrays.items()}], core_ids=[0])
    return r.results[0]["out_rows"][:NTOK].reshape(B, S, D)
```
